# Optimizing a Trainium2 kernel written in Bass

```python
import numpy as np
import jax
import jax.numpy as jnp

def _softmax(x, axis=-1):
    return jax.nn.softmax(x, axis=axis)

def _gelu(x):
    return jax.nn.gelu(x, approximate=True)

def _silu(x):
    return jax.nn.silu(x)

def _sigmoid(x):
    return jax.nn.sigmoid(x)

def _layernorm(x, axis=-1, eps=1e-05):
    m = jnp.mean(x, axis=axis, keepdims=True)
    v = jnp.var(x, axis=axis, keepdims=True)
    return (x - m) / jnp.sqrt(v + eps)

def _scatter_add(tgt, idx, src, axis=0):
    return tgt.at[idx].add(src)

def _segment_sum(src, seg, n):
    return jax.ops.segment_sum(src, seg, n)
kernel_name = 'mk_xattn_ffn_d1_seqx_r4_aa1a49'

def setup_inputs(seed: int=0):
    np.random.seed(seed)
    _w = jnp.asarray

    def _rec_inputs():
        import jax
        import jax.numpy as jnp
        _rk = jax.random.key(seed)
        x = -0.0005146 + 1 * jax.random.normal(jax.random.fold_in(_rk, 1), (8, 512, 256), jnp.float32)
        _lenS = 512 - jax.random.randint(jax.random.fold_in(_rk, 7), (8,), 0, max(1, 512 // 4) + 1, jnp.int32)
        _lenS2 = 1024 - jax.random.randint(jax.random.fold_in(_rk, 8), (8,), 0, max(1, 1024 // 4) + 1, jnp.int32)
        _ctx_768P = jax.random.normal(jax.random.fold_in(_rk, 11), (8, 16, 192), jnp.float32)
        _ctx_768c = jax.random.dirichlet(jax.random.fold_in(_rk, 511), 0.3 * jnp.ones((16,), jnp.float32), (8, 1024))
        _ctx_768t = jnp.einsum('bsk,bkd->bsd', _ctx_768c, _ctx_768P)
        _ctx_768t = _ctx_768t * jax.lax.rsqrt(jnp.mean(jnp.square(_ctx_768t)) + 1e-12) * 0.953939
        ctx_768 = -0.00040386 + 0.999972 * (_ctx_768t + 0.3 * jax.random.normal(jax.random.fold_in(_rk, 611), (8, 1024, 192), jnp.float32))
        _validS = jnp.arange(512)[None, :] < _lenS[:, None]
        _validS2 = jnp.arange(1024)[None, :] < _lenS2[:, None]
        _causal = jnp.tril(jnp.ones((512, 512), dtype=bool))
        mask_BxS2_bk0 = jnp.logical_not(jnp.broadcast_to(_validS2[:, :], (8, 1024)))
        return (x, ctx_768, mask_BxS2_bk0)
    x, ctx_768, mask_BxS2_bk0 = _rec_inputs()

    def _L0_xattn_setup():
        import jax, jax.numpy as jnp
        import numpy as np
        DIM_IN, DIM_LAT, DIM_HEAD = (192, 256, 64)
        INNER = max(DIM_LAT, DIM_IN)
        HEADS = INNER // DIM_HEAD
        SCALE = DIM_HEAD ** (-0.5)
        RMS_EPS = 1e-08
        LN_EPS = 1e-05

        def layernorm(x, g, b):
            mu = jnp.mean(x, axis=-1, keepdims=True)
            var = jnp.mean((x - mu) ** 2, axis=-1, keepdims=True)
            return (x - mu) * jax.lax.rsqrt(var + LN_EPS) * g + b

        def rmsnorm(x, gamma):
            norm = jnp.sqrt(jnp.sum(x * x, axis=-1, keepdims=True)) * x.shape[-1] ** (-0.5)
            return x / jnp.maximum(norm, RMS_EPS) * gamma
        key = jax.random.key(seed)
        ks = jax.random.split(key, 12)
        b, n, m = (4, 1024, 128)
        x = jax.random.normal(ks[0], (b, n, DIM_IN), jnp.float32)
        latents = jax.random.normal(ks[1], (b, m, DIM_LAT), jnp.float32)
        mask = jax.random.randint(ks[2], (b, n), 0, 2).astype(bool)
        s = lambda k, sh, fan: jax.random.normal(k, sh, jnp.float32) * fan ** (-0.5)
        return {'x': x, 'latents': latents, 'mask': mask, 'ln_x_g': jnp.ones((DIM_IN,), jnp.float32), 'ln_x_b': jnp.zeros((DIM_IN,), jnp.float32), 'ln_l_g': jnp.ones((DIM_LAT,), jnp.float32), 'ln_l_b': jnp.zeros((DIM_LAT,), jnp.float32), 'qn_g': jnp.ones((DIM_HEAD,), jnp.float32), 'kn_g': jnp.ones((DIM_HEAD,), jnp.float32), 'Wq': s(ks[3], (INNER, DIM_LAT), DIM_LAT), 'Wkv': s(ks[4], (2 * INNER, DIM_IN), DIM_IN), 'Wlkv': s(ks[5], (2 * INNER, DIM_LAT), DIM_LAT), 'Wo': s(ks[6], (DIM_LAT, INNER), INNER), 'bo': jnp.zeros((DIM_LAT,), jnp.float32)}
    _L0_xattn_all = _L0_xattn_setup()
    _L0_xattn_in = {k: v for k, v in _L0_xattn_all.items() if k in ('ln_x_g', 'ln_x_b', 'ln_l_g', 'ln_l_b', 'qn_g', 'kn_g', 'Wq', 'Wkv', 'Wlkv', 'Wo', 'bo')}
    del _L0_xattn_all

    def _L0_ffn_setup():
        import jax, jax.numpy as jnp
        import numpy as np
        import math
        B, L, D = (4, 1024, 256)
        F = 1024
        E = 16
        CAP_FACTOR = 1.0
        EPS = 1e-05
        key = jax.random.key(seed)
        ks = jax.random.split(key, 8)
        std = 0.02
        return {'x': jax.random.normal(ks[0], (B, L, D), dtype=jnp.float32), 'norm_weight': jnp.ones((D,), dtype=jnp.float32), 'router_weight': jax.random.normal(ks[1], (E, D), dtype=jnp.float32) * std, 'router_bias': jnp.zeros((E,), dtype=jnp.float32), 'fc1_weight': jax.random.normal(ks[2], (E, F, D), dtype=jnp.float32) * std, 'fc1_bias': jnp.zeros((E, F), dtype=jnp.float32), 'fc2_weight': jax.random.normal(ks[3], (E, D, F), dtype=jnp.float32) * std, 'fc2_bias': jnp.zeros((E, D), dtype=jnp.float32)}
    _L0_ffn_all = _L0_ffn_setup()
    _L0_ffn_in = {k: v for k, v in _L0_ffn_all.items() if k in ('norm_weight', 'router_weight', 'router_bias', 'fc1_weight', 'fc1_bias', 'fc2_weight', 'fc2_bias')}
    del _L0_ffn_all
    return {'x': x, 'ctx_768': ctx_768, 'mask_BxS2_bk0': mask_BxS2_bk0, 'L0_xattn_ln_x_g': _L0_xattn_in['ln_x_g'], 'L0_xattn_ln_x_b': _L0_xattn_in['ln_x_b'], 'L0_xattn_ln_l_g': _L0_xattn_in['ln_l_g'], 'L0_xattn_ln_l_b': _L0_xattn_in['ln_l_b'], 'L0_xattn_qn_g': _L0_xattn_in['qn_g'], 'L0_xattn_kn_g': _L0_xattn_in['kn_g'], 'L0_xattn_Wq': _L0_xattn_in['Wq'], 'L0_xattn_Wkv': _L0_xattn_in['Wkv'], 'L0_xattn_Wlkv': _L0_xattn_in['Wlkv'], 'L0_xattn_Wo': _L0_xattn_in['Wo'], 'L0_xattn_bo': _L0_xattn_in['bo'], 'L0_ffn_norm_weight': _L0_ffn_in['norm_weight'], 'L0_ffn_router_weight': _L0_ffn_in['router_weight'], 'L0_ffn_router_bias': _L0_ffn_in['router_bias'], 'L0_ffn_fc1_weight': _L0_ffn_in['fc1_weight'], 'L0_ffn_fc1_bias': _L0_ffn_in['fc1_bias'], 'L0_ffn_fc2_weight': _L0_ffn_in['fc2_weight'], 'L0_ffn_fc2_bias': _L0_ffn_in['fc2_bias']}

def reference(x, ctx_768, mask_BxS2_bk0, L0_xattn_ln_x_g, L0_xattn_ln_x_b, L0_xattn_ln_l_g, L0_xattn_ln_l_b, L0_xattn_qn_g, L0_xattn_kn_g, L0_xattn_Wq, L0_xattn_Wkv, L0_xattn_Wlkv, L0_xattn_Wo, L0_xattn_bo, L0_ffn_norm_weight, L0_ffn_router_weight, L0_ffn_router_bias, L0_ffn_fc1_weight, L0_ffn_fc1_bias, L0_ffn_fc2_weight, L0_ffn_fc2_bias):
    import jax
    import jax.numpy as jnp

    def _L0_xattn_ref(x, latents, mask, ln_x_g, ln_x_b, ln_l_g, ln_l_b, qn_g, kn_g, Wq, Wkv, Wlkv, Wo, bo):
        import jax, jax.numpy as jnp
        import numpy as np
        DIM_IN, DIM_LAT, DIM_HEAD = (192, 256, 64)
        INNER = max(DIM_LAT, DIM_IN)
        HEADS = INNER // DIM_HEAD
        SCALE = DIM_HEAD ** (-0.5)
        RMS_EPS = 1e-08
        LN_EPS = 1e-05

        def layernorm(x, g, b):
            mu = jnp.mean(x, axis=-1, keepdims=True)
            var = jnp.mean((x - mu) ** 2, axis=-1, keepdims=True)
            return (x - mu) * jax.lax.rsqrt(var + LN_EPS) * g + b

        def rmsnorm(x, gamma):
            norm = jnp.sqrt(jnp.sum(x * x, axis=-1, keepdims=True)) * x.shape[-1] ** (-0.5)
            return x / jnp.maximum(norm, RMS_EPS) * gamma
        b, n, _ = x.shape
        m = latents.shape[1]
        xn = layernorm(x, ln_x_g, ln_x_b)
        ln = layernorm(latents, ln_l_g, ln_l_b)
        q = ln @ Wq.T
        kv = jnp.concatenate([xn @ Wkv.T, ln @ Wlkv.T], axis=1)
        k, v = (kv[..., :INNER], kv[..., INNER:])
        split_heads = lambda t: t.reshape(t.shape[0], t.shape[1], HEADS, DIM_HEAD).transpose(0, 2, 1, 3)
        q, k, v = (split_heads(q), split_heads(k), split_heads(v))
        qn = rmsnorm(q, qn_g) * SCALE
        kn = rmsnorm(k, kn_g)
        attn = jnp.einsum('bhid,bhjd->bhij', qn, kn)
        full_mask = jnp.pad(mask, ((0, 0), (0, m)), constant_values=True)
        attn = jnp.where(full_mask[:, None, None, :], attn, -jnp.finfo(attn.dtype).max)
        attn = jax.nn.softmax(attn, axis=-1)
        out = jnp.einsum('bhij,bhjd->bhid', attn, v)
        out = out.transpose(0, 2, 1, 3).reshape(b, m, INNER)
        return out @ Wo.T + bo

    def _L0_ffn_ref(x, norm_weight, router_weight, router_bias, fc1_weight, fc1_bias, fc2_weight, fc2_bias):
        import jax, jax.numpy as jnp
        import numpy as np
        import math
        B, L, D = (4, 1024, 256)
        F = 1024
        E = 16
        CAP_FACTOR = 1.0
        EPS = 1e-05
        b, l, d = x.shape
        n_tokens = b * l
        n_experts = router_weight.shape[0]
        capacity = max(1, math.ceil(CAP_FACTOR * n_tokens / n_experts))
        top_k = min(capacity, n_tokens)
        xf = x.reshape(n_tokens, d)
        rms = jnp.sqrt(jnp.mean(xf * xf, axis=-1, keepdims=True) + EPS)
        xn = xf / rms * norm_weight
        logits = xn @ router_weight.T + router_bias
        probs = jax.nn.softmax(logits, axis=-1)
        _, idx = jax.lax.top_k(logits.T, top_k)
        xe = xn[idx]
        h = jnp.einsum('ecd,efd->ecf', xe, fc1_weight) + fc1_bias[:, None, :]
        h = jax.nn.gelu(h, approximate=False)
        y = jnp.einsum('ecf,edf->ecd', h, fc2_weight) + fc2_bias[:, None, :]
        gates = jnp.take_along_axis(probs.T, idx, axis=1)
        flat_idx = idx.reshape(-1)
        contrib = (y * gates[:, :, None]).reshape(-1, d)
        output = jnp.zeros((n_tokens, d), dtype=x.dtype).at[flat_idx].add(contrib)
        gate_sums = jnp.zeros((n_tokens, 1), dtype=x.dtype).at[flat_idx].add(gates.reshape(-1, 1))
        assigned = gate_sums > 0
        output = jnp.where(assigned, output / jnp.where(assigned, gate_sums, 1.0), output)
        return output.reshape(b, l, d)
    x = x + _L0_xattn_ref(ctx_768, _layernorm(x, axis=-1), mask_BxS2_bk0, L0_xattn_ln_x_g, L0_xattn_ln_x_b, L0_xattn_ln_l_g, L0_xattn_ln_l_b, L0_xattn_qn_g, L0_xattn_kn_g, L0_xattn_Wq, L0_xattn_Wkv, L0_xattn_Wlkv, L0_xattn_Wo, L0_xattn_bo)
    x = x + _L0_ffn_ref(_layernorm(x, axis=-1), L0_ffn_norm_weight, L0_ffn_router_weight, L0_ffn_router_bias, L0_ffn_fc1_weight, L0_ffn_fc1_bias, L0_ffn_fc2_weight, L0_ffn_fc2_bias)
    return x

_drawn_inputs = setup_inputs


def setup_inputs(seed=0):
    import zlib

    import numpy as np

    out = dict(_drawn_inputs(seed))
    spreads = {'L0_xattn_ln_x_g': (1.0, 0.2),
     'L0_xattn_ln_x_b': (0.0, 0.1),
     'L0_xattn_ln_l_g': (1.0, 0.2),
     'L0_xattn_ln_l_b': (0.0, 0.1),
     'L0_xattn_qn_g': (1.0, 0.558),
     'L0_xattn_kn_g': (1.0, 0.538),
     'L0_xattn_bo': (0.0, 0.1),
     'L0_ffn_norm_weight': (1.0, 0.2),
     'L0_ffn_router_bias': (0.0, 2.0),
     'L0_ffn_fc1_bias': (0.0, 0.324),
     'L0_ffn_fc2_bias': (0.0, 0.1)}
    factors = {}
    for name, (base, spread) in spreads.items():
        noise = np.random.default_rng([zlib.crc32(name.encode()), seed]).standard_normal(out[name].shape)
        drawn = base * np.exp(spread * noise) if base else spread * noise
        out[name] = jnp.asarray(drawn.astype(out[name].dtype))
    for name, factor in factors.items():
        out[name] = (out[name] * factor).astype(out[name].dtype)
    return out
```

```python
from contextlib import ExitStack

import numpy as np

import concourse.bass as bass
from concourse import mybir

F32, F32R, BF16 = mybir.dt.float32, mybir.dt.float32r, mybir.dt.bfloat16
I32, U32, U8 = mybir.dt.int32, mybir.dt.uint32, mybir.dt.uint8
ALU, ACT, AX = mybir.AluOpType, mybir.ActivationFunctionType, mybir.AxisListType.X

P = 128
B, M, D = 8, 512, 256
NC_, DC = 1024, 192
H, DH = 4, 64
INNER = H * DH
E, F = 16, 1024
T = B * M
CAP = T // E
MT, CT = M // P, NC_ // P
KT = CT + MT
NT = T // P
KEYS = KT * P
DHF, CHF = D // 2, DC // 2
FT = F // P
ROW = D + E
ACC = D + 1
LN_EPS = 1e-5
RMS_EPS = 1e-8
SCALE = DH ** -0.5
MASKED = -1e30
RSQRT_MAGIC = 0x5F3759DF
NO_SLOT = 2 * CAP


class Signal:

    def __init__(self, sem):
        self.sem, self.value = sem, 0

    def post(self, by):
        self.value += by
        return (self, self.value)


class Lane:

    def __init__(self, done):
        self.done, self.steps, self.waited = done, [], {}

    def wait(self, *posts):
        for post in posts:
            if post is None:
                continue
            signal, value = post
            if self.waited.get(signal, 0) < value:
                self.waited[signal] = value
                self.steps.append((lambda e, s=signal.sem, v=value: e.wait_ge(s, v), None, 0))

    def do(self, instruction, signal=None, by=1):
        signal = signal or self.done
        self.steps.append((instruction, signal.sem, by))
        return signal.post(by)

    def latest(self):
        return (self.done, self.done.value)

    def quiet(self, instruction):
        self.steps.append((instruction, None, 0))

    def write(self, engine):
        for instruction, sem, by in self.steps:
            made = instruction(engine)
            if sem is not None:
                made.then_inc(sem, by)


class Ring:

    def __init__(self, buffers):
        self.buffers, self.freed, self.at = buffers, [()] * len(buffers), -1
        self.held = [False] * len(buffers)

    def take(self, *lanes):
        self.at = (self.at + 1) % len(self.buffers)
        assert not self.held[self.at], "the next buffer is still in use"
        self.held[self.at] = True
        for lane in lanes:
            lane.wait(*self.freed[self.at])
        return self.at, self.buffers[self.at]

    def give(self, at, *posts):
        self.freed[at], self.held[at] = posts, False


def build(nc, io):
    with ExitStack() as everything:
        _build(nc, io, everything)


def _build(nc, io, everything):
    def semaphore(name):
        return Signal(everything.enter_context(nc.semaphore(name)))

    def sb(name, shape, dt, where=None):
        return (where or everything).enter_context(nc.sbuf_tensor(name, shape, dt))

    pe, act, dve, pool = (Lane(semaphore(n)) for n in ("pe_done", "act_done", "dve_done", "pool_done"))
    sync = Lane(None)

    bank = [everything.enter_context(nc.psum_tensor(f"bank{i}", [P, 512], F32)) for i in range(8)]

    def mm(out, lhsT, rhs, start, stop, post=False):
        f = lambda e: e.matmul(out, lhsT, rhs, start=start, stop=stop, skip_group_check=True)
        return pe.do(f) if post else pe.quiet(f)

    def flip(out, in_, ident, post=False):
        f = lambda e: e.transpose(out, in_, ident)
        return pe.do(f) if post else pe.quiet(f)

    def tt(lane, out, a, b, op):
        return lane.do(lambda e: e.tensor_tensor(out, a, b, op))

    def ts(lane, out, a, s1, s2, op0, op1=ALU.bypass):
        return lane.do(lambda e: e.tensor_scalar(out, a, s1, s2, op0, op1))

    def stt(out, a, s, b, op0, op1):
        return dve.do(lambda e: e.scalar_tensor_tensor(out, a, s, b, op0, op1))

    def copy(lane, out, a):
        return lane.do(lambda e: e.tensor_copy(out, a))

    def func(out, a, f, bias=0.0, scale=1.0):
        return act.do(lambda e: e.activation(out, a, f, bias=bias, scale=scale))

    def reduce(out, a, op):
        return dve.do(lambda e: e.tensor_reduce(out, a, AX, op))

    def recip(out, a):
        return dve.do(lambda e: e.reciprocal(out, a))

    def load(out, in_, signal, lane=sync):
        return lane.do(lambda e: e.dma_start(out, in_), signal, 16)

    def as32(ap):
        return ap.bitcast(F32)

    rows_dram = nc.dram_tensor("rows_scratch", [T, ROW], F32, kind="Internal").ap()
    x2_dram = nc.dram_tensor("x2_scratch", [T, D], F32, kind="Internal").ap()
    acc_dram = nc.dram_tensor("acc_scratch", [T, ACC], F32, kind="Internal").ap()

    small = semaphore("small_loaded")
    ident = sb("ident", [P, P], F32)
    neg_ident = sb("neg_ident", [P, P], F32)
    ones_col = sb("ones_col", [P, 1], F32)
    lnl_g, lnl_b = sb("lnl_g", [P, 2], F32), sb("lnl_b", [P, 2], F32)
    lnx_g, lnx_b = sb("lnx_g", [CHF, 2], F32), sb("lnx_b", [CHF, 2], F32)
    qn_col, kn_col, gqk = sb("qn_col", [P, 1], F32), sb("kn_col", [P, 1], F32), sb("gqk", [P, 1], F32)
    router_w, router_b = sb("router_w", [P, 2, E], F32), sb("router_b", [E, 1], F32)
    mask_rows = sb("mask_rows", [B * CT, P], U8)
    mask_rows_f = sb("mask_rows_f", [B * CT, P], F32)
    mask_col = sb("mask_col", [P, B * CT], F32)
    logits = sb("logits", [P, NT, E], F32)
    logits_by_chunk = sb("logits_by_chunk", [P, M], F32)

    attention = ExitStack()
    ab = lambda name, shape, dt: sb(name, shape, dt, attention)
    zeros = ab("zeros", [P, ACC], F32)
    bo_rows, nw_rows = ab("bo_rows", [P, D], F32), ab("nw_rows", [P, D], F32)
    WL = 3 * INNER
    w_lat_hi, w_lat_lo = ab("w_lat_hi", [P, 2, WL], F32R), ab("w_lat_lo", [P, 2, WL], F32R)
    w_ctx_hi, w_ctx_lo = ab("w_ctx_hi", [CHF, 2, 2 * INNER], F32R), ab("w_ctx_lo", [CHF, 2, 2 * INNER], F32R)
    wo_hi, wo_lo = ab("wo_hi", [P, H, D], F32R), ab("wo_lo", [P, H, D], F32R)
    x_in = [ab(f"x_in{i}", [P, MT, D], F32) for i in range(2)]
    c_in = [ab(f"c_in{i}", [P, 4, DC], F32) for i in range(2)]
    z_nat = ab("z_nat", [P, 4, D], F32)
    z_full = ab("z_full", [P, 2, 512], F32)
    z_hi, z_lo = ab("z_hi", [P, 2, 512], F32R), ab("z_lo", [P, 2, 512], F32R)
    squares = [ab(f"squares{i}", [P, 512], F32) for i in range(2)]
    qk_nat = ab("qk_nat", [P, MT, 2 * INNER], F32)
    kc_nat = ab("kc_nat", [P, CT, INNER], F32)
    v_nat = [ab(f"v_nat{i}", [P, KT, INNER], F32) for i in range(2)]
    qa = [ab(f"qa{i}", [P, 2, M], F32R) for i in range(2)]
    qb = [ab(f"qb{i}", [P, 2, M], F32R) for i in range(2)]
    ka = [ab(f"ka{i}", [P, 2, KEYS], F32R) for i in range(2)]
    kb = [ab(f"kb{i}", [P, 2, KEYS], F32R) for i in range(2)]
    maxima = ab("maxima", [P, 2, MT, 3], F32)
    row_max = ab("row_max", [P, 2, MT], F32)
    masked_scores = [ab(f"masked_scores{i}", [P, 512], BF16) for i in range(2)]
    mask_bias8 = ab("mask_bias8", [P, NC_], U8)
    mask_bias = ab("mask_bias", [P, NC_], BF16)
    probs = [ab(f"probs{i}", [P, M], F32) for i in range(6)]
    prob_sum = [ab("prob_sum", [P, 2, M], F32)]
    inv_den = ab("inv_den", [P, H, MT], F32)
    o_stack = ab("o_stack", [P, H, M], F32R)
    router_probs = ab("router_probs", [P, MT, E], F32)
    xn_T = z_full
    logits_T = ab("logits_T", [E, M], F32)
    stats = ab("stats", [P, 4, 6], F32)
    mean_var = ab("mean_var", [P, 4, 2], F32)
    norm_w, norm_y, norm_t = (ab(n, [P, 32], F32) for n in ("norm_w", "norm_y", "norm_t"))
    sq_sum = ab("sq_sum", [P, 32], F32)
    soft = ab("soft", [P, MT, E], F32)
    soft_s = ab("soft_s", [P, 2, MT], F32)

    def column(name, tile):
        return load(tile[:], io[name], small)

    x_sem = [semaphore(f"x_loaded{i}") for i in range(2)]
    c_sem = [semaphore(f"c_loaded{i}") for i in range(2)]
    mask_sem = semaphore("mask_loaded")
    weight_sem = semaphore("weights_loaded")
    x_ring, c_ring = Ring(x_in), Ring(c_in)
    x_loaded, c_loaded = {}, {}

    def load_x(b):
        at, buf = x_ring.take(sync)
        x_loaded[b] = load(buf[:], io["x"][b].rearrange("(j p) d -> p j d", p=P), x_sem[at])

    def load_ctx(b, half):
        at, buf = c_ring.take(sync)
        src = io["ctx"][b].rearrange("(j p) d -> p j d", p=P)[:, 4 * half:4 * half + 4, :]
        c_loaded[b, half] = (at, load(buf[:], src, c_sem[at]))

    load_x(0)
    column("ident", ident)
    column("neg_ident", neg_ident)
    for name, tile in (("lnl_g", lnl_g), ("lnl_b", lnl_b), ("lnx_g", lnx_g), ("lnx_b", lnx_b),
                       ("router_w", router_w), ("router_b", router_b)):
        column(name, tile)
    for half in (slice(0, DH), slice(DH, P)):
        load(qn_col[half, :], io["qn_g"], small)
        load(kn_col[half, :], io["kn_g"], small)
    load(mask_rows[:], io["mask"].rearrange("b (j p) -> (b j) p", p=P), small)
    load(bo_rows[:], io["bo"].partition_broadcast(P), small)
    small_loaded = load(nw_rows[:], io["norm_weight"].partition_broadcast(P), small)
    raw = v_nat[1][:].rearrange("p j d -> p (j d)")
    raw_lat = raw[:, 0:2 * WL].rearrange("p (a b) -> p a b", a=2)
    raw_ctx = raw[0:CHF, 2 * WL:2 * WL + 4 * INNER].rearrange("p (a b) -> p a b", a=2)
    raw_wo = [probs[i][:].rearrange("p (a b) -> p a b", a=2) for i in range(2)]
    load(raw_lat, io["w_lat"].rearrange("(a p) n -> p a n", p=P), weight_sem)
    load_ctx(0, 0)
    load(raw_ctx, io["w_ctx"].rearrange("(a p) n -> p a n", p=CHF), weight_sem)
    load_ctx(0, 1)
    for half in (slice(0, DH), slice(DH, P)):
        for i in range(2):
            weights_loaded = load(raw_wo[i][half], io["wo"].rearrange("(h d) n -> d h n", d=DH)[:, 2 * i:2 * i + 2, :],
                                  weight_sem)

    pool.do(lambda e: e.memset(ones_col[:], 1.0))
    zeros_set = pool.do(lambda e: e.memset(zeros[:], 0.0))
    for h in range(H):
        other = slice(DH, P) if h % 2 == 0 else slice(0, DH)
        wo_lo_cleared = dve.do(lambda e, o=wo_lo[other, h, :]: e.memset(as32(o), 0.0))
    act.wait(weights_loaded)
    lat_hi_made = func(w_lat_hi[:], raw_lat, ACT.Copy)
    ctx_hi_made = func(w_ctx_hi[:], raw_ctx, ACT.Copy)
    for i in range(2):
        wo_hi_made = func(wo_hi[:, 2 * i:2 * i + 2, :], raw_wo[i], ACT.Copy)
    pool.wait(weights_loaded, lat_hi_made)
    lat_lo_made = tt(pool, w_lat_lo[:], raw_lat, as32(w_lat_hi[:]), ALU.subtract)
    pool.wait(ctx_hi_made)
    ctx_lo_made = tt(pool, w_ctx_lo[:], raw_ctx, as32(w_ctx_hi[:]), ALU.subtract)
    dve.wait(wo_hi_made, wo_lo_cleared)
    for h in range(H):
        own = slice(0, DH) if h % 2 == 0 else slice(DH, P)
        wo_lo_made = tt(dve, wo_lo[own, h, :], raw_wo[h // 2][own, h % 2, :], as32(wo_hi[own, h, :]), ALU.subtract)
    dve.wait(wo_lo_made)
    for i in range(2):
        for hh, half in enumerate((slice(DH, P), slice(0, DH))):
            kb_ones_set = dve.do(lambda e, o=kb[i][half, hh, :]: e.memset(as32(o), 1.0))
    dve.wait(small_loaded)
    mask_f_made = ts(dve, mask_rows_f[:], mask_rows[:], -1.0, -MASKED, ALU.add, ALU.mult)
    gqk_made = ts(dve, gqk[:], qn_col[:], kn_col[:, 0:1], SCALE, ALU.mult, ALU.mult)
    zero_sem = semaphore("acc_cleared")
    sync.wait(zeros_set)
    acc_view = acc_dram.rearrange("(j p) d -> p j d", p=P)
    for j in range(0, NT, 8):
        acc_cleared = load(acc_view[:, j:j + 8, :], zeros[:].unsqueeze(1).broadcast_to([P, 8, ACC]), zero_sem)

    score_banks = Ring(bank[0:3])
    o_bank, o_bank_freed = bank[3], [()]
    max_banks = Ring(bank[4:6])
    misc = Ring(bank[6:8])

    at, out = misc.take(pe)
    pe.wait(small_loaded, mask_f_made)
    mask_flipped = flip(out[:, 0:B * CT], mask_rows_f[:], ident[0:B * CT, 0:B * CT], post=True)
    act.wait(mask_flipped)
    mask_col_made = func(mask_col[:], out[:, 0:B * CT], ACT.Copy)
    misc.give(at, mask_col_made)

    def rsqrt(y, w, t):
        yi, wi = y.bitcast(I32), w.bitcast(I32)
        dve.wait(dve.latest())
        dve.wait(ts(dve, yi, wi, 1, None, ALU.logical_shift_right))
        dve.wait(ts(dve, yi, yi, -1.0, float(RSQRT_MAGIC), ALU.mult, ALU.add))
        for _ in range(3):
            dve.wait(tt(dve, t, y, y, ALU.mult))
            dve.wait(stt(t, t, -0.5, w, ALU.mult, ALU.mult))
            last = stt(y, t, 1.5, y, ALU.add, ALU.mult)
            dve.wait(last)
        return last

    z_free = [(), ()]
    sq_ring = Ring(squares)
    nat_free = {"qk": (), "kc": ()}
    qk_normed, v_written = {}, {}
    v_free = [(), (lat_lo_made, ctx_lo_made)]

    def normalise(src, width, eps_w, eps_b, dst):
        for i in range(4):
            last = dve.do(lambda e, o=stats[:, i, :], a=src[:, i, :]: e.bn_stats(o, a))
        dve.wait(last)
        for i in range(4):
            last = dve.do(lambda e, o=mean_var[:, i, :], a=stats[:, i, :]: e.bn_aggr(o, a))
        dve.wait(last)
        dve.wait(ts(dve, norm_w[:, 0:4], mean_var[:, :, 1], eps_w, eps_b, ALU.mult, ALU.add))
        rsqrt(norm_y[:, 0:4], norm_w[:, 0:4], norm_t[:, 0:4])
        for i in range(4):
            last = ts(dve, dst[:, i, :], src[:, i, :], mean_var[:, i, 0:1], norm_y[:, i:i + 1],
                      ALU.subtract, ALU.mult)
        return last

    def transposed_split(z_made, width, g, b):
        z_posts = []
        for half in range(2):
            at, out = misc.take(pe)
            pe.wait(z_made)
            for i in range(4):
                flipped = flip(out[0:width, i * P:(i + 1) * P],
                               z_nat[:, i, half * width:(half + 1) * width], ident[:], post=i == 3)
            dve.wait(flipped, *z_full_free[half])
            full = ts(dve, z_full[0:width, half, :], out[0:width, :], g[:, half:half + 1], b[:, half:half + 1],
                      ALU.mult, ALU.add)
            misc.give(at, full)
            act.wait(full, *z_free[0])
            hi = func(z_hi[0:width, half, :], z_full[0:width, half, :], ACT.Copy)
            pool.wait(full, hi, *z_free[0])
            lo = tt(pool, z_lo[0:width, half, :], z_full[0:width, half, :], as32(z_hi[0:width, half, :]),
                    ALU.subtract)
            z_full_free[half] = (hi, lo)
            z_posts += [hi, lo]
            yield
        z_free[1] = (flipped,)
        z_split[0] = z_posts

    z_full_free = [(), ()]
    z_split = [()]

    def three_passes(out, width, tile, w_hi, w_lo, cols):
        at = slice(tile * P, (tile + 1) * P)
        n = 0
        for half in range(2):
            for z, w in ((z_hi, w_hi), (z_lo, w_hi), (z_hi, w_lo)):
                last = mm(out, z[0:width, half, at], w[0:width, half, cols], n == 0, n == 5, post=n == 5)
                n += 1
        return last

    def head_norms(b, heads, groups):
        n = 4 * heads
        dve.wait(dve.latest())
        dve.wait(ts(dve, norm_w[:, 0:n], sq_sum[:, 0:n], 1.0 / DH, RMS_EPS ** 2, ALU.mult, ALU.max))
        rsqrt(norm_y[:, 0:n], norm_w[:, 0:n], norm_t[:, 0:n])

    def project_latents(b):
        x = x_in[b % 2]
        dve.wait(x_loaded[b], small_loaded, *z_free[1])
        z_made = normalise(x, D, 1.0 + LN_EPS, LN_EPS * LN_EPS, z_nat)
        pool.wait(z_made, small_loaded)
        residual_made[b] = tt(pool, x[:], x[:], bo_rows[:].unsqueeze(1).broadcast_to([P, MT, D]), ALU.add)
        yield
        yield from transposed_split(z_made, DHF, lnl_g, lnl_b)
        for i in range(MT):
            at, out = misc.take(pe)
            pe.wait(lat_lo_made, *z_split[0])
            qk_done = three_passes(out[:], DHF, i, w_lat_hi, w_lat_lo, slice(0, 2 * INNER))
            act.wait(qk_done, *nat_free["qk"])
            qk_out = func(qk_nat[:, i, :], out[:], ACT.Copy)
            sat, sq = sq_ring.take(act)
            sq_out = func(sq[:], out[:], ACT.Square)
            misc.give(at, sq_out)
            dve.wait(sq_out)
            summed = reduce(sq_sum[:, i * 2 * H:(i + 1) * 2 * H],
                            sq[:].rearrange("p (h d) -> p h d", d=DH), ALU.add)
            sq_ring.give(sat, summed)
            yield
            at, out = misc.take(pe)
            v_done = three_passes(out[:, 0:INNER], DHF, i, w_lat_hi, w_lat_lo, slice(2 * INNER, WL))
            act.wait(v_done, *v_free[b % 2])
            v_out = func(v_nat[b % 2][:, CT + i, :], out[:, 0:INNER], ACT.Copy)
            misc.give(at, v_out)
            yield
        z_free[0] = (v_done,)
        v_written[b] = v_out
        head_norms(b, 2 * H, MT)
        for i in range(MT):
            dve.wait(qk_out)
            view = qk_nat[:, i, :].rearrange("p (h d) -> p h d", d=DH)
            normed = tt(dve, view, view,
                        norm_y[:, i * 2 * H:(i + 1) * 2 * H].unsqueeze(2).broadcast_to([P, 2 * H, DH]), ALU.mult)
        qk_normed[b] = normed
        yield

    def project_context(b, chunk):
        at_in, c_here = c_loaded[b, chunk]
        src = c_in[at_in]
        dve.wait(c_here, small_loaded, *z_free[1])
        z_made = normalise(src, DC, 1.0, LN_EPS, z_nat[:, :, 0:DC])
        c_ring.give(at_in, z_made)
        nxt = (b, chunk + 2) if chunk + 2 < 2 else (b + 1, chunk)
        if nxt[0] < B:
            load_ctx(*nxt)
        yield
        yield from transposed_split(z_made, CHF, lnx_g, lnx_b)
        for i in range(4):
            tile = 4 * chunk + i
            at, out = misc.take(pe)
            pe.wait(ctx_lo_made, *z_split[0])
            kv_done = three_passes(out[:], CHF, i, w_ctx_hi, w_ctx_lo, slice(0, 2 * INNER))
            act.wait(kv_done, *nat_free["kc"], *v_free[b % 2])
            k_out = func(kc_nat[:, tile, :], out[:, 0:INNER], ACT.Copy)
            sat, sq = sq_ring.take(act)
            sq_out = func(sq[:, 0:INNER], out[:, 0:INNER], ACT.Square)
            v_out = func(v_nat[b % 2][:, tile, :], out[:, INNER:2 * INNER], ACT.Copy)
            misc.give(at, v_out)
            dve.wait(sq_out)
            summed = reduce(sq_sum[:, i * H:(i + 1) * H],
                            sq[:, 0:INNER].rearrange("p (h d) -> p h d", d=DH), ALU.add)
            sq_ring.give(sat, summed)
            yield
        z_free[0] = (kv_done,)
        v_written[b] = v_out
        head_norms(b, H, 4)
        dve.wait(v_out)
        view = kc_nat[:, 4 * chunk:4 * chunk + 4, :].rearrange("p j (h d) -> p (j h) d", d=DH)
        normed = tt(dve, view, view, norm_y[:, 0:4 * H].unsqueeze(2).broadcast_to([P, 4 * H, DH]), ALU.mult)
        kc_normed[b] = normed
        yield

    residual_made, kc_normed = {}, {}
    unit_free = [(), ()]
    prepared, shift_made = {}, {}
    mask_free = [()]

    def prepare(b, pair):
        u = (2 * b + pair) % 2
        both = slice(2 * pair * DH, 2 * (pair + 1) * DH)
        at, out = misc.take(pe)
        pe.wait(qk_normed[b])
        for j in range(MT):
            flipped = flip(out[:, j * P:(j + 1) * P], qk_nat[:, j, both], ident[:], post=j == MT - 1)
        q_hi, q_lo = [], []
        for hh, (hi, lo) in enumerate(ROWS):
            act.wait(flipped, gqk_made, *unit_free[u])
            q_hi.append(func(qb[u][hi, hh, :], out[hi, :], ACT.Identity, scale=gqk[hi, 0:1]))
            dve.wait(q_hi[hh], *unit_free[u])
            q_lo.append(stt(qa[u][lo, hh, :], out[hi, :], gqk[hi, 0:1], as32(qb[u][hi, hh, :]),
                            ALU.mult, ALU.subtract))
        misc.give(at, *q_lo)
        sync.wait(*q_hi, *unit_free[u])
        for hh, (hi, lo) in enumerate(ROWS):
            load(as32(qa[u][hi, hh, :]), as32(qb[u][hi, hh, :]), copied[u])
        yield
        for g in range(3):
            at, out = misc.take(pe)
            pe.wait(kc_normed[b])
            for j in range(4):
                tile = 4 * g + j
                k = (kc_nat[:, tile, both] if tile < CT else
                     qk_nat[:, tile - CT, INNER + both.start:INNER + both.stop])
                flipped = flip(out[:, j * P:(j + 1) * P], k, ident[:], post=j == 3)
            cols = slice(512 * g, 512 * (g + 1))
            k_hi, k_lo = [], []
            for hh, (hi, lo) in enumerate(ROWS):
                act.wait(flipped, kb_ones_set, *unit_free[u])
                k_hi.append(func(ka[u][hi, hh, cols], out[hi, :], ACT.Copy))
                dve.wait(k_hi[hh], *unit_free[u])
                k_lo.append(tt(dve, kb[u][hi, hh, cols], out[hi, :], as32(ka[u][hi, hh, cols]), ALU.subtract))
            misc.give(at, *k_lo)
            sync.wait(*k_hi)
            for hh, (hi, lo) in enumerate(ROWS):
                k_copied = load(as32(ka[u][lo, hh, cols]), as32(ka[u][hi, hh, cols]), copied[u])
            yield
        prepared[b, pair] = (k_copied, *q_lo, *k_lo)
        if pair == 1:
            nat_free["qk"] = nat_free["kc"] = (flipped,)

    ROWS = ((slice(0, DH), slice(DH, P)), (slice(DH, P), slice(0, DH)))
    copied = [semaphore(f"copied{i}") for i in range(2)]

    def load_mask(b):
        sync.wait(*mask_free[0])
        here = load(mask_bias8[:], io["mask"][b].partition_broadcast(P), mask_sem)
        act.wait(here, *max_free[0])
        made = func(mask_bias[:], mask_bias8[:], ACT.Copy, bias=MASKED, scale=-MASKED)
        mask_free[0] = (made,)
        return made

    max_free = [()]
    mask_made = {}

    def find_maxima(b, pair):
        u = (2 * b + pair) % 2
        if pair == 0:
            mask_made[b] = load_mask(b)
        pe.wait(*prepared[b, pair])
        for hh in range(2):
            for j in range(MT):
                for g in range(3):
                    at, out = max_banks.take(pe)
                    done = mm(out[:], qa[u][:, hh, j * P:(j + 1) * P], ka[u][:, hh, 512 * g:512 * (g + 1)],
                              True, True, post=True)
                    if g < 2:
                        jat, junk = junk_ring.take(dve)
                        dve.wait(done, mask_made[b])
                        mx = dve.do(lambda e, o=junk[:], a=out[:], m=mask_bias[:, 512 * g:512 * (g + 1)],
                                    r=maxima[:, hh, j, g:g + 1]:
                                    e.tensor_tensor_reduce(o, a, m, 1.0, -3e38, ALU.add, ALU.max, r))
                        junk_ring.give(jat, mx)
                    else:
                        dve.wait(done)
                        mx = reduce(maxima[:, hh, j, 2:3], out[:], ALU.max)
                    max_banks.give(at, mx)
                yield
        max_free[0] = (mx,)
        dve.wait(mx)
        dve.wait(reduce(row_max[:], maxima[:], ALU.max))
        for hh, (hi, lo) in enumerate(ROWS):
            cols = qb[u][lo, hh, :].rearrange("p (j q) -> p j q", q=P)
            for low in (0, DH):
                m = row_max[low:low + DH, hh, :].unsqueeze(2).broadcast_to([DH, MT, DH])
                i = neg_ident[low:low + DH, low:low + DH].unsqueeze(1).broadcast_to([DH, MT, DH])
                last = tt(dve, cols[:, :, low:low + DH], i, m, ALU.mult)
        shift_made[b, pair] = last
        yield

    junk_ring = Ring(masked_scores)
    prob_ring = Ring(probs)
    prob_ring.freed[0] = prob_ring.freed[1] = (wo_hi_made, wo_lo_made)
    sum_ring = Ring(prob_sum)
    summed_probs = {}
    o_written = {}
    o_free = [()]
    inv_den_free = [()]
    den_made = {}

    def attend(b, pair, between):
        u = (2 * b + pair) % 2
        pe.wait(*prepared[b, pair], shift_made[b, pair], v_written[b])
        waiting = []

        def with_v(kt, hh, pat, p, exp_done):
            if kt == 0:
                pe.wait(*o_bank_freed[0])
            pe.wait(exp_done)
            h = 2 * pair + hh
            used = mm(o_bank[hh * DH:(hh + 1) * DH, :], v_nat[b % 2][:, kt, h * DH:(h + 1) * DH], p[:],
                      kt == 0, kt == KT - 1, post=True)
            if kt == 0:
                first[hh] = (pat, p, exp_done, used)
            else:
                pool.wait(exp_done)
                if kt == 1:
                    if hh == 0:
                        taken.append(sum_ring.take(pool))
                    pool.wait(first[hh][2])
                total = taken[0][1]
                if kt == 1:
                    added = tt(pool, total[:, hh, :], first[hh][1][:], p[:], ALU.add)
                    prob_ring.give(first[hh][0], first[hh][3], added)
                else:
                    pool.wait(summed[hh])
                    added = tt(pool, total[:, hh, :], total[:, hh, :], p[:], ALU.add)
                summed[hh] = added
                prob_ring.give(pat, used, added)
            return used

        first, summed, taken = {}, {}, []
        for kt in range(KT):
            now = []
            for hh in range(2):
                at, out = score_banks.take(pe)
                keys = slice(kt * P, (kt + 1) * P)
                mm(out[:], ka[u][:, hh, keys], qa[u][:, hh, :], True, False)
                scored = mm(out[:], kb[u][:, hh, keys], qb[u][:, hh, :], False, True, post=True)
                pat, p = prob_ring.take(act)
                act.wait(scored)
                if kt < CT:
                    col = b * CT + kt
                    exp_done = func(p[:], out[:], ACT.Exp, bias=mask_col[:, col:col + 1])
                else:
                    exp_done = func(p[:], out[:], ACT.Exp)
                score_banks.give(at, exp_done)
                now.append((kt, hh, pat, p, exp_done))
            for item in waiting:
                with_v(*item)
            waiting = now
            between()
        for item in waiting:
            used = with_v(*item)
        unit_free[u] = (scored,)
        summed_probs[b, pair] = (summed[0], summed[1], taken[0][0])
        if pair == 1:
            v_free[b % 2] = (used,)
        act.wait(used, *o_free[0])
        a, c = 2 * pair, 2 * pair + 1
        hi_a = func(o_stack[0:DH, a, :], o_bank[0:DH, :], ACT.Copy)
        hi_c = func(o_stack[DH:P, c, :], o_bank[DH:P, :], ACT.Copy)
        dve.wait(hi_a, hi_c, *o_free[0])
        tt(dve, o_stack[DH:P, a, :], o_bank[0:DH, :], as32(o_stack[0:DH, a, :]), ALU.subtract)
        lo_c = tt(dve, o_stack[0:DH, c, :], o_bank[DH:P, :], as32(o_stack[DH:P, c, :]), ALU.subtract)
        o_bank_freed[0] = (hi_c, lo_c)
        o_written[b, pair] = (hi_c, lo_c)

    def denominators(b, pair):
        s0, s1, sat = summed_probs[b, pair]
        at, out = misc.take(pe)
        pe.wait(s0, s1)
        for hh in range(2):
            for j in range(MT):
                done = mm(out[:, hh * MT + j:hh * MT + j + 1], prob_sum[sat][:, hh, j * P:(j + 1) * P],
                          ones_col[:], True, True, post=True)
        sum_ring.give(sat, done)
        dve.wait(done, *inv_den_free[0])
        made = recip(inv_den[:, 2 * pair:2 * pair + 2, :], out[:, 0:2 * MT].rearrange("p (h j) -> p h j", h=2))
        misc.give(at, made)
        den_made[b, pair] = made
        yield

    rows_sem = semaphore("rows_stored")
    x2_sem = semaphore("x2_stored")
    chunk_sem = semaphore("chunk_stored")
    rows_free, x2_stored, logits_T_free = [()], {}, [()]
    rows_stored = [None]

    def finish(b):
        x = x_in[b % 2]
        pe.wait(*o_written[b, 0], *o_written[b, 1], wo_lo_made)
        for j in range(MT):
            at_q = slice(j * P, (j + 1) * P)
            posts = []
            for pair in range(2):
                at, out = misc.take(pe)
                for hh in range(2):
                    h = 2 * pair + hh
                    dst = out[:, hh * D:(hh + 1) * D]
                    mm(dst, o_stack[:, h, at_q], wo_hi[:, h, :], True, False)
                    done = mm(dst, o_stack[:, h, at_q], wo_lo[:, h, :], False, True, post=True)
                dve.wait(done, residual_made[b], *den_made_all(b))
                for hh in range(2):
                    h = 2 * pair + hh
                    summed = stt(x[:, j, :], out[:, hh * D:(hh + 1) * D], inv_den[:, h, j:j + 1], x[:, j, :],
                                 ALU.mult, ALU.add)
                    dve.wait(summed)
                misc.give(at, summed)
            yield
        o_free[0] = (done,)
        inv_den_free[0] = (summed,)
        sync.wait(summed)
        x2_stored[b] = load(x2_dram[b * M:(b + 1) * M, :].rearrange("(j p) d -> p j d", p=P), x[:], x2_sem)
        xn = z_nat[:]
        dve.wait(*z_free[1], *rows_free[0])
        normed = normalise(x, D, 1.0 + LN_EPS, LN_EPS * LN_EPS, xn)
        x_ring.give(b % 2, x2_stored[b], normed)
        if b + 2 < B:
            load_x(b + 2)
        pool.wait(normed)
        weighted = tt(pool, xn, xn, nw_rows[:].unsqueeze(1).broadcast_to([P, MT, D]), ALU.mult)
        yield
        pe.wait(weighted)
        halves = []
        for half in range(2):
            at, out = misc.take(pe)
            for j in range(MT):
                flipped = flip(out[:, j * P:(j + 1) * P], xn[:, j, half * P:(half + 1) * P], ident[:],
                               post=j == MT - 1)
            act.wait(flipped, *z_full_free[half])
            xn_flipped = flipped
            halves.append(func(xn_T[:, half, :], out[:], ACT.Copy))
            misc.give(at, halves[-1])
        yield
        at, out = misc.take(pe)
        pe.wait(*halves)
        mm(out[0:E, :], router_w[:, 0, :], xn_T[:, 0, :], True, False)
        routed = mm(out[0:E, :], router_w[:, 1, :], xn_T[:, 1, :], False, True, post=True)
        z_full_free[0] = z_full_free[1] = (routed,)
        act.wait(routed, *logits_T_free[0])
        biased = func(logits_T[:], out[0:E, :], ACT.Identity, bias=router_b[:, 0:1])
        misc.give(at, biased)
        sync.wait(biased)
        chunk_stored[b] = load(logits_by_chunk[b * E:(b + 1) * E, :], logits_T[:], chunk_sem)
        yield
        at, out = misc.take(pe)
        pe.wait(biased)
        for j in range(MT):
            flipped = flip(out[:, j * E:(j + 1) * E], logits_T[:, j * P:(j + 1) * P], ident[0:E, 0:E],
                           post=j == MT - 1)
        logits_T_free[0] = (chunk_stored[b], flipped)
        mine = logits[:, b * MT:(b + 1) * MT, :]
        dve.wait(flipped)
        natural = copy(dve, mine, out[:, 0:MT * E].rearrange("p (j e) -> p j e", j=MT))
        misc.give(at, natural)
        dve.wait(natural)
        dve.wait(reduce(soft_s[:, 0, :], mine, ALU.max))
        centred = tt(dve, soft[:], mine, soft_s[:, 0, :].unsqueeze(2).broadcast_to([P, MT, E]), ALU.subtract)
        yield
        act.wait(centred)
        powers = func(soft[:], soft[:], ACT.Exp)
        dve.wait(powers)
        dve.wait(reduce(soft_s[:, 0, :], soft[:], ALU.add))
        dve.wait(recip(soft_s[:, 1, :], soft_s[:, 0, :]))
        scaled = tt(dve, router_probs[:], soft[:],
                    soft_s[:, 1, :].unsqueeze(2).broadcast_to([P, MT, E]), ALU.mult)
        sync.wait(scaled, weighted)
        mine = rows_dram[b * M:(b + 1) * M, :].rearrange("(j p) d -> p j d", p=P)
        load(mine[:, :, 0:D], xn, rows_sem)
        stored = load(mine[:, :, D:ROW], router_probs[:], rows_sem)
        rows_free[0] = (stored,)
        z_free[1] = (stored, xn_flipped)
        rows_stored[0] = stored
        yield

    chunk_stored = {}

    def den_made_all(b):
        return (den_made[b, 0], den_made[b, 1])

    def run(*stages):
        for stage in stages:
            for _ in stage:
                pass

    def chain(*stages):
        for stage in stages:
            yield from stage

    load_x(1)
    run(project_latents(0), project_context(0, 0), project_context(0, 1), prepare(0, 0), find_maxima(0, 0))
    for b in range(B):
        for pair in range(2):
            todo = []
            if pair == 0:
                if b > 0:
                    todo += [denominators(b - 1, 1), finish(b - 1)]
                todo += [prepare(b, 1), find_maxima(b, 1)]
                if b + 1 < B:
                    todo += [project_latents(b + 1)]
                steps = (1 + 9 if b else 0) + 4 + 9 + (12 if b + 1 < B else 0)
            else:
                todo += [denominators(b, 0)]
                if b + 1 < B:
                    todo += [project_context(b + 1, 0), project_context(b + 1, 1),
                             prepare(b + 1, 0), find_maxima(b + 1, 0)]
                steps = 1 + (16 + 4 + 9 if b + 1 < B else 0)
            work = chain(*todo)
            state = {"kt": 0, "made": 0}

            def between():
                state["kt"] += 1
                goal = -(-steps * state["kt"] // (KT - 1))
                while state["made"] < goal:
                    state["made"] += 1
                    if next(work, "end") == "end":
                        state["made"] = goal

            attend(b, pair, between)
            run(work)
    run(denominators(B - 1, 1), finish(B - 1))
    pieces = (pe.latest(), act.latest(), dve.latest(), pool.latest())
    stores_done = (x2_stored[B - 1], rows_stored[0], chunk_stored[B - 1], acc_cleared)
    attention.close()
    choice = ExitStack()
    cb = lambda name, shape, dt: sb(name, shape, dt, choice)

    w1_raw = [sb(f"w1_raw{i}", [P, 2, F], F32) for i in range(2)]
    w2_raw = [sb(f"w2_raw{i}", [P, FT, D], F32) for i in range(2)]
    w1_hi, w1_lo = ([sb(f"w1_{n}{i}", [P, 2, F], F32R) for i in range(2)] for n in ("hi", "lo"))
    w2_hi, w2_lo = ([sb(f"w2_{n}{i}", [P, FT, D], F32R) for i in range(2)] for n in ("hi", "lo"))
    b1_cols = sb("b1_cols", [P, E, FT], F32)
    b2_rows = [sb(f"b2_rows{i}", [P, D], F32) for i in range(4)]
    gathered = [sb(f"gathered{i}", [P, 2, ROW], F32) for i in range(2)]
    xe_hi, xe_lo = ([sb(f"xe_{n}{i}", [P, 2, CAP], F32R) for i in range(2)] for n in ("hi", "lo"))
    h_full = [sb(f"h_full{i}", [P, CAP], F32) for i in range(2)]
    h_hi, h_lo = sb("h_hi", [P, FT, CAP], F32R), sb("h_lo", [P, FT, CAP], F32R)
    y_out = [sb(f"y_out{i}", [P, 2, ACC], F32) for i in range(2)]
    token_index = [sb(f"token_index{i}", [P, 2], U32) for i in range(4)]
    slot_hi, slot_lo = sb("slot_hi", [P, E, NT], F32), sb("slot_lo", [P, E, NT], F32)
    iota16, tile_ids = sb("iota16", [P, 16], F32), sb("tile_ids", [P, NT], BF16)
    token_in_tile = sb("token_in_tile", [P, 1], F32)
    expand16, pick = sb("expand16", [16, P], F32), sb("pick", [P, 2, 16], F32)
    hot_hi, hot_lo = sb("hot_hi", [P, NT, 16], BF16), sb("hot_lo", [P, NT, 16], BF16)
    hot_ids = sb("hot_ids", [P, NT, 2, 16], BF16)
    list_parts, list16 = sb("list_parts", [16, 32], F32), sb("list16", [16, 16], F32)
    picked, list_f = sb("picked", [P, 2, 16], F32), sb("list_f", [P, 2], F32)

    sync.wait(*pieces, *stores_done)
    consts_sem = semaphore("choice_consts_loaded")
    same_expert, search_bits = cb("same_expert", [P, P], F32), cb("search_bits", [P, 31], U32)
    before_f, scan_keep = cb("before_f", [P, P], F32), cb("scan_keep", [P, T // P * E], F32)
    before, all_ones = cb("before", [P, P], BF16), cb("all_ones", [P, P], BF16)
    for tile, name in ((same_expert, "same_expert"), (search_bits, "search_bits"), (before_f, "before"),
                       (scan_keep, "scan_keep"), (iota16, "iota16"), (token_in_tile, "token_in_tile"),
                       (expand16, "expand16"), (pick, "pick"), (b1_cols, "fc1_bias")):
        load(tile[:], io[name], consts_sem)
    tile_ids_f = cb("tile_ids_f", [P, NT], F32)
    consts_loaded = load(tile_ids_f[:], io["tile_ids"], consts_sem)

    w_sem = [semaphore(f"expert_weights_loaded{i}") for i in range(2)]
    raw_free, weights_here = [(), ()], {}
    b2_sem = [semaphore(f"expert_bias_loaded{i}") for i in range(4)]
    b2_free, b2_here = [()] * 4, {}

    def load_expert(e):
        i = e % 2
        sync.wait(*raw_free[i], *b2_free[e % 4])
        load(w1_raw[i][:], io["fc1"][e], w_sem[i])
        weights_here[e] = load(w2_raw[i][:], io["fc2"][e], w_sem[i])
        b2_here[e] = load(b2_rows[e % 4][:], io["fc2_bias"][e].partition_broadcast(P), b2_sem[e % 4])

    load_expert(0)
    load_expert(1)

    split_free = [(), ()]
    split_made = {}

    def split_weights(e):
        i = e % 2
        posts = []
        halves = [(w1_raw[i][:, a, :], w1_hi[i][:, a, :], w1_lo[i][:, a, :]) for a in range(2)]
        halves += [tuple(w[:, 4 * a:4 * a + 4, :] for w in (w2_raw[i], w2_hi[i], w2_lo[i])) for a in range(2)]
        for n, (raw, hi, lo) in enumerate(halves):
            act.wait(weights_here[e], *split_free[i])
            hi_made = func(hi, raw, ACT.Copy)
            lane = dve if n == 3 else pool
            lane.wait(hi_made, *split_free[i])
            lo_made = tt(lane, lo, raw, as32(hi), ALU.subtract)
            posts += [hi_made, lo_made]
            yield
        raw_free[i] = tuple(posts)
        split_made[e] = tuple(posts)
        if e + 2 < E:
            load_expert(e + 2)

    for lane in (act, pool, dve, pe):
        lane.wait(*pieces, *stores_done[:3])

    key, trial, kept = cb("key", [P, 1], U32), cb("trial", [P, 1], U32), cb("kept", [P, 1], U32)
    key_flip, trial_flips = cb("key_flip", [P, 1], U32), cb("trial_flips", [P, 31], U32)
    count, junk_cmp = cb("count", [P, 1], F32), [cb(f"junk_cmp{i}", [P, M], BF16) for i in range(2)]
    count_bank = bank[0]

    def count_at_least(threshold, n):
        return dve.do(lambda e: e.tensor_scalar(junk_cmp[n % 2][:], logits_by_chunk[:], threshold, None,
                                                ALU.is_ge, ALU.add, accum_out=count[:]))

    def keep_bit(n, bit):
        pe.wait(dve.latest())
        summed = mm(count_bank[:, 0:1], same_expert[:], count[:], True, True, post=True)
        dve.wait(summed)
        dve.wait(ts(dve, kept[:], count_bank[:, 0:1], float(CAP), float(bit), ALU.is_ge, ALU.mult))

    dve.wait(consts_loaded)
    pe.wait(consts_loaded)
    dve.wait(dve.do(lambda e: e.memset(trial[:], 0)))
    dve.wait(count_at_least(trial[:].bitcast(F32), 0))
    keep_bit(0, 1 << 31)
    copy_key = ts(dve, key[:], kept[:], 0, None, ALU.bitwise_or)
    dve.wait(ts(dve, key_flip[:].bitcast(I32), kept[:].bitcast(I32), 31, -1, ALU.arith_shift_right,
                ALU.bitwise_xor))
    dve.wait(ts(dve, key_flip[:], key_flip[:], 1 << 31, None, ALU.bitwise_or))
    dve.wait(ts(dve, trial_flips[:], search_bits[:], key_flip[:, 0:1], None, ALU.bitwise_xor))
    dve.wait(dve.do(lambda e: e.memset(kept[:], 0)))
    for n in range(31):
        dve.wait(ts(dve, trial[:], key[:], kept[:, 0:1], trial_flips[:, n:n + 1], ALU.bitwise_or, ALU.bitwise_xor))
        dve.wait(ts(dve, key[:], key[:], kept[:, 0:1], None, ALU.bitwise_or))
        dve.wait(count_at_least(trial[:].bitcast(F32), n + 1))
        keep_bit(n, 1 << (30 - n))
    dve.wait(ts(dve, trial[:], key[:], kept[:, 0:1], key_flip[:, 0:1], ALU.bitwise_or, ALU.bitwise_xor))

    wide = cb("wide", [E, P], F32)
    limit = cb("limit", [P, E], F32)
    widened = copy(dve, wide[:], trial[0:E, 0:1].bitcast(F32).broadcast_to([E, P]))
    pe.wait(widened)
    limits_flipped = flip(bank[1][:, 0:E], wide[:], ident[0:E, 0:E], post=True)
    before_made = copy(dve, before[:], before_f[:])
    ones_made = dve.do(lambda e: e.memset(all_ones[:], 1.0))
    tile_ids_made = copy(dve, tile_ids[:], tile_ids_f[:])
    dve.wait(limits_flipped)
    dve.wait(copy(dve, limit[:], bank[1][:, 0:E]))

    by_expert = [P, E, NT]
    view = logits[:].rearrange("p j e -> p e j")
    above, equal = cb("above", by_expert, BF16), cb("equal", by_expert, BF16)
    running, earlier = cb("running", [P, E * NT], BF16), cb("earlier", [P, E * NT], BF16)
    flat = lambda t: t[:].rearrange("p e j -> p (e j)")
    order = {}
    for n, (taken, op) in enumerate(((above, ALU.is_gt), (equal, ALU.is_equal))):
        dve.wait(tt(dve, taken[:], view, limit[:].unsqueeze(2).broadcast_to(by_expert), op))
        if n:
            dve.wait(order[0])
            pe_read = order[0]
        dve.wait(dve.do(lambda e, t=taken: e.tensor_tensor_scan(running[:], scan_keep[:], flat(t), 0.0,
                                                               ALU.mult, ALU.add)))
        tiles_before = tt(dve, earlier[:], running[:], flat(taken), ALU.subtract)
        pe.wait(tiles_before, before_made, ones_made)
        mm(bank[2 + n][:], before[:], flat(taken), True, False)
        order[n] = mm(bank[2 + n][:], all_ones[:], earlier[:], False, True, post=True)
        if n == 0:
            totals = running[:].rearrange("p (e j) -> p e j", j=NT)[:, :, NT - 1]
            order[0] = mm(bank[4][:, 0:E], all_ones[:], totals, True, True, post=True)
    n_above, slot, part = cb("n_above", [P, E], F32), cb("slot", by_expert, F32), cb("part", by_expert, F32)
    slot_int, slot_bits = cb("slot_int", by_expert, I32), cb("slot_bits", by_expert, I32)
    rank = lambda n: bank[n][:].rearrange("p (e j) -> p e j", j=NT)
    dve.wait(order[0])
    dve.wait(copy(dve, n_above[:], bank[4][:, 0:E]), order[1])
    dve.wait(tt(dve, part[:], rank(3), n_above[:].unsqueeze(2).broadcast_to(by_expert), ALU.add))
    dve.wait(tt(dve, part[:], part[:], equal[:], ALU.mult))
    dve.wait(tt(dve, slot[:], rank(2), above[:], ALU.mult))
    dve.wait(tt(dve, slot[:], slot[:], part[:], ALU.add))
    dve.wait(tt(dve, part[:], above[:], equal[:], ALU.add))
    dve.wait(stt(slot[:], part[:], -float(NO_SLOT), slot[:], ALU.mult, ALU.add))
    dve.wait(ts(dve, slot_int[:], slot[:], float(NO_SLOT), None, ALU.add))
    dve.wait(ts(dve, slot_bits[:], slot_int[:], 4, None, ALU.logical_shift_right))
    dve.wait(copy(dve, slot_hi[:], slot_bits[:]))
    dve.wait(ts(dve, slot_bits[:], slot_int[:], 15, None, ALU.bitwise_and))
    slots_made = copy(dve, slot_lo[:], slot_bits[:])
    dve.wait(slots_made)

    list_bank, list_bank_free = bank[0], [()]
    xe_bank, xe_bank_free = bank[1], [()]
    hidden_banks = Ring(bank[2:5])
    y_banks, y_bank_free = bank[5:7], [(), ()]
    hot_free = [()]
    index_made, gather_done, xe_made = {}, {}, {}
    index_free, gathered_free, xe_free = [()] * 4, [(), ()], [(), ()]
    gather_sem = [semaphore(f"gathered{i}") for i in range(2)]
    scatter_sem = [semaphore(f"scattered{i}") for i in range(2)]
    rows_at = (rows_stored[0],)

    def list_tokens(e):
        i = e % 2
        hot = [P, NT, 16]
        iota = iota16[:].unsqueeze(1).broadcast_to(hot)
        dve.wait(*hot_free[0])
        tt(dve, hot_hi[:], iota, slot_hi[:, e, :].unsqueeze(2).broadcast_to(hot), ALU.is_equal)
        dve.wait(tt(dve, hot_lo[:], iota, slot_lo[:, e, :].unsqueeze(2).broadcast_to(hot), ALU.is_equal))
        ts(dve, hot_ids[:, :, 0, :], hot_lo[:], token_in_tile[:, 0:1], None, ALU.mult)
        ids_made = tt(dve, hot_ids[:, :, 1, :], hot_lo[:], tile_ids[:].unsqueeze(2).broadcast_to(hot), ALU.mult)
        yield
        pe.wait(ids_made, *list_bank_free[0])
        for j in range(NT):
            listed = mm(list_bank[0:16, 0:32], hot_hi[:, j, :], hot_ids[:, j].rearrange("p a b -> p (a b)"),
                        j == 0, j == NT - 1, post=j == NT - 1)
        hot_free[0] = (listed,)
        yield
        dve.wait(listed)
        dve.wait(copy(dve, list_parts[:], list_bank[0:16, 0:32]))
        made = stt(list16[:], list_parts[:, 16:32], float(P), list_parts[:, 0:16], ALU.mult, ALU.add)
        pe.wait(made)
        spread = mm(list_bank[:, 64:80], expand16[:], list16[:], True, True, post=True)
        dve.wait(spread)
        dve.wait(tt(dve, picked[:], pick[:], list_bank[:, 64:80].unsqueeze(1).broadcast_to([P, 2, 16]), ALU.mult))
        list_bank_free[0] = (dve.latest(),)
        dve.wait(reduce(list_f[:], picked[:], ALU.add))
        dve.wait(*index_free[e % 4])
        index_made[e] = copy(dve, token_index[e % 4][:], list_f[:])
        yield

    def gather(e):
        i = e % 2
        pool.wait(index_made[e], *gathered_free[i], *rows_at)
        for c in range(2):
            gather_done[e] = pool.do(
                lambda g, c=c: g.indirect_dma_start(gathered[i][:, c, :], None, rows_dram,
                                                    bass.IndirectOffsetOnAxis(ap=token_index[e % 4][:, c:c + 1], axis=0)),
                gather_sem[i], 16)
        yield

    def transpose_tokens(e):
        i = e % 2
        pe.wait(gather_done[e], *xe_bank_free[0])
        for half in range(2):
            for c in range(2):
                flipped = flip(xe_bank[:, half * CAP + c * P:half * CAP + (c + 1) * P],
                               gathered[i][:, c, half * P:(half + 1) * P], ident[:], post=half and c)
        act.wait(flipped, *xe_free[i])
        flat_hi = xe_hi[i][:].rearrange("p a n -> p (a n)")
        hi = func(flat_hi, xe_bank[:], ACT.Copy)
        dve.wait(hi, *xe_free[i])
        lo = tt(dve, xe_lo[i][:].rearrange("p a n -> p (a n)"), xe_bank[:], as32(flat_hi), ALU.subtract)
        xe_bank_free[0] = (lo,)
        xe_made[e] = (hi, lo)
        yield

    h_free = [()] * FT
    h_ring = Ring(h_full)
    y_free = [(), ()]
    scattered = [()]

    def run_expert(e, between):
        i = e % 2
        pe.wait(*xe_made[e], *split_made[e])
        h_made = []
        for f in range(FT):
            at, out = hidden_banks.take(pe)
            cols = slice(f * P, (f + 1) * P)
            n = 0
            for half in range(2):
                for w, x in ((w1_hi, xe_hi), (w1_lo, xe_hi), (w1_hi, xe_lo)):
                    done = mm(out[:, 0:CAP], w[i][:, half, cols], x[i][:, half, :], n == 0, n == 5, post=n == 5)
                    n += 1
            hat, full = h_ring.take(act)
            act.wait(done)
            activated = func(full[:], out[:, 0:CAP], ACT.Gelu, bias=b1_cols[:, e, f:f + 1])
            hidden_banks.give(at, activated)
            dve.wait(activated, *h_free[f])
            hi = copy(dve, h_hi[:, f, :], full[:])
            dve.wait(hi)
            lo = tt(dve, h_lo[:, f, :], full[:], as32(h_hi[:, f, :]), ALU.subtract)
            h_ring.give(hat, lo)
            h_made.append(lo)
            between()
        xe_free[i] = (done,)
        for c in range(2):
            pe.wait(*y_bank_free[c])
            tokens = slice(c * P, (c + 1) * P)
            n = 0
            for f in range(FT):
                pe.wait(h_made[f])
                for h, w in ((h_hi, w2_hi), (h_lo, w2_hi), (h_hi, w2_lo)):
                    done = mm(y_banks[c][:, 0:D], h[:, f, tokens], w[i][:, f, :], n == 0, n == 3 * FT - 1,
                              post=n == 3 * FT - 1)
                    n += 1
                if f % 2:
                    between()
            dve.wait(done, b2_here[e], *y_free[i])
            biased = tt(dve, y_out[i][:, c, 0:D], y_banks[c][:, 0:D], b2_rows[e % 4][:], ALU.add)
            y_bank_free[c] = (biased,)
            dve.wait(biased)
            gate = gathered[i][:, c, D + e:D + e + 1]
            ts(dve, y_out[i][:, c, 0:D], y_out[i][:, c, 0:D], gate, None, ALU.mult)
            gated = copy(dve, y_out[i][:, c, D:ACC], gate)
        for f in range(FT):
            h_free[f] = (done,)
        split_free[i] = (done,)
        b2_free[e % 4] = (biased,)
        gathered_free[i] = (gated,)
        pool.wait(gated, acc_cleared, *scattered[0])
        for c in range(2):
            landed = pool.do(
                lambda g, c=c: g.indirect_dma_start(acc_dram,
                                                    bass.IndirectOffsetOnAxis(ap=token_index[e % 4][:, c:c + 1], axis=0),
                                                    y_out[i][:, c, :], None, compute_op=ALU.add),
                scatter_sem[i], 16)
        scattered[0] = (landed,)
        y_free[i] = index_free[e % 4] = (landed,)

    run(list_tokens(0), gather(0), split_weights(0), list_tokens(1), transpose_tokens(0))
    choice.close()
    x2_back, x2_back_sem = sb("x2_back", [P, NT, D], F32), semaphore("x2_loaded")
    for e in range(E):
        todo = []
        if e + 1 < E:
            todo += [gather(e + 1), split_weights(e + 1), transpose_tokens(e + 1)]
        if e + 2 < E:
            todo += [list_tokens(e + 2)]
        steps = 1 + 4 + 1 + 3
        work = chain(*todo)
        state = {"at": 0, "made": 0}

        def between():
            state["at"] += 1
            goal = -(-steps * state["at"] // 14)
            while state["made"] < goal:
                state["made"] += 1
                if next(work, "end") == "end":
                    state["made"] = goal

        run_expert(e, between)
        run(work)
        if e == 1:
            sync.wait(slots_made, pe.latest(), dve.latest())
            x2_loaded = load(x2_back[:], x2_dram.rearrange("(j p) d -> p j d", p=P), x2_back_sem)

    acc_in = [sb(f"acc_in{i}", [P, 4, ACC], F32) for i in range(2)]
    inv_gate = [sb(f"inv_gate{i}", [P, 2, 4], F32) for i in range(2)]
    acc_sem = [semaphore(f"acc_loaded{i}") for i in range(2)]
    out_sem = semaphore("out_stored")
    acc_free = [(), ()]
    out_view = io["out"].rearrange("b (j p) d -> p (b j) d", p=P)
    sync.wait(*scattered[0])
    for g in range(NT // 4):
        i = g % 2
        tiles = slice(4 * g, 4 * g + 4)
        sync.wait(*acc_free[i])
        here = load(acc_in[i][:], acc_view[:, tiles, :], acc_sem[i])
        dve.wait(here, x2_loaded)
        sums = acc_in[i][:, :, D]
        dve.wait(ts(dve, inv_gate[i][:, 0, :], sums, 0.0, None, ALU.is_le))
        dve.wait(tt(dve, inv_gate[i][:, 0, :], inv_gate[i][:, 0, :], sums, ALU.add))
        dve.wait(recip(inv_gate[i][:, 1, :], inv_gate[i][:, 0, :]))
        for j in range(4):
            last = stt(x2_back[:, 4 * g + j, :], acc_in[i][:, j, 0:D], inv_gate[i][:, 1, j:j + 1],
                       x2_back[:, 4 * g + j, :], ALU.mult, ALU.add)
        acc_free[i] = (last,)
        act.wait(last)
        stored = act.do(lambda e, o=out_view[:, tiles, :], a=x2_back[:, tiles, :]: e.dma_start(o, a), out_sem, 16)
    act.wait(stored)

    with nc.Block() as block:
        block.sync(lambda e: sync.write(e))
        block.gpsimd(lambda e: pool.write(e))
        block.scalar(lambda e: act.write(e))
        block.vector(lambda e: dve.write(e))
        block.tensor(lambda e: pe.write(e))


def _operands(i):
    def cols(v, width):
        return np.ascontiguousarray(v.reshape(2, width).T)

    f32 = np.float32
    part, eye = np.arange(P), np.eye(P, dtype=f32)
    ops = {
        "x": i["x"], "ctx": i["ctx_768"], "mask": i["mask_BxS2_bk0"],
        "lnl_g": cols(i["L0_xattn_ln_l_g"], DHF), "lnl_b": cols(i["L0_xattn_ln_l_b"], DHF),
        "lnx_g": cols(i["L0_xattn_ln_x_g"], CHF), "lnx_b": cols(i["L0_xattn_ln_x_b"], CHF),
        "qn_g": i["L0_xattn_qn_g"][:, None], "kn_g": i["L0_xattn_kn_g"][:, None],
        "w_lat": np.concatenate([i["L0_xattn_Wq"].T, i["L0_xattn_Wlkv"].T], axis=1),
        "w_ctx": i["L0_xattn_Wkv"].T, "wo": i["L0_xattn_Wo"].T, "bo": i["L0_xattn_bo"],
        "norm_weight": i["L0_ffn_norm_weight"],
        "router_w": i["L0_ffn_router_weight"].T.reshape(2, P, E).transpose(1, 0, 2),
        "router_b": i["L0_ffn_router_bias"][:, None],
        "fc1": i["L0_ffn_fc1_weight"].transpose(0, 2, 1).reshape(E, 2, P, F).transpose(0, 2, 1, 3),
        "fc1_bias": i["L0_ffn_fc1_bias"].reshape(E, FT, P).transpose(2, 0, 1),
        "fc2": i["L0_ffn_fc2_weight"].transpose(0, 2, 1).reshape(E, FT, P, D).transpose(0, 2, 1, 3),
        "fc2_bias": i["L0_ffn_fc2_bias"],
        "ident": eye, "neg_ident": -eye,
        "same_expert": (part[:, None] % E == part[None, :] % E).astype(f32),
        "search_bits": np.broadcast_to(np.uint32(1) << np.arange(30, -1, -1, dtype=np.uint32), (P, 31)),
        "before": (part[:, None] < part[None, :]).astype(f32),
        "scan_keep": np.broadcast_to((np.arange(E * NT) % NT != 0).astype(f32), (P, E * NT)),
        "iota16": np.broadcast_to(np.arange(16, dtype=f32), (P, 16)),
        "tile_ids": np.broadcast_to(np.arange(NT, dtype=f32), (P, NT)),
        "token_in_tile": part[:, None].astype(f32),
        "expand16": (np.arange(16)[:, None] == part[None, :] // 8).astype(f32),
        "pick": (np.arange(16)[None, None, :]
                 == 2 * (part % 8)[:, None, None] + np.arange(2)[None, :, None]).astype(f32),
    }
    return {name: np.ascontiguousarray(a) for name, a in ops.items()}


def kernel(**inputs):
    import concourse.bacc as bacc
    from concourse.bass_utils import run_bass_kernel_spmd

    nc = bacc.Bacc("TRN2", target_bir_lowering=False, num_devices=1)
    operands = _operands({name: np.asarray(a) for name, a in inputs.items()})
    io = {name: nc.dram_tensor(f"in_{name}", a.shape, mybir.dt.from_np(a.dtype), kind="ExternalInput").ap()
          for name, a in operands.items()}
    io["out"] = nc.dram_tensor("out_x", (B, M, D), F32, kind="ExternalOutput").ap()
    build(nc, io)
    result = run_bass_kernel_spmd(nc, [{f"in_{name}": a for name, a in operands.items()}], core_ids=[0])
    return result.results[0]["out_x"]
```

```python
from contextlib import ExitStack

import numpy as np

import concourse.bass as bass
from concourse import mybir

F32, F32R, BF16 = mybir.dt.float32, mybir.dt.float32r, mybir.dt.bfloat16
I32, U32, U8 = mybir.dt.int32, mybir.dt.uint32, mybir.dt.uint8
ALU, ACT, AX = mybir.AluOpType, mybir.ActivationFunctionType, mybir.AxisListType.X

P = 128
B, M, D = 8, 512, 256
NC_, DC = 1024, 192
H, DH = 4, 64
INNER = H * DH
E, F = 16, 1024
T = B * M
CAP = T // E
MT, CT = M // P, NC_ // P
KT = CT + MT
NT = T // P
KEYS = KT * P
DHF, CHF = D // 2, DC // 2
FT = F // P
ROW = D + E
ACC = D + 1
LN_EPS = 1e-5
RMS_EPS = 1e-8
SCALE = DH ** -0.5
MASKED = -1e30
RSQRT_MAGIC = 0x5F3759DF
NO_SLOT = 2 * CAP


class Signal:

    def __init__(self, sem):
        self.sem, self.value = sem, 0

    def post(self, by):
        self.value += by
        return (self, self.value)


class Lane:

    def __init__(self, done):
        self.done, self.steps, self.waited = done, [], {}

    def wait(self, *posts):
        for post in posts:
            if post is None:
                continue
            signal, value = post
            if self.waited.get(signal, 0) < value:
                self.waited[signal] = value
                self.steps.append((lambda e, s=signal.sem, v=value: e.wait_ge(s, v), None, 0))

    def do(self, instruction, signal=None, by=1):
        signal = signal or self.done
        self.steps.append((instruction, signal.sem, by))
        return signal.post(by)

    def latest(self):
        return (self.done, self.done.value)

    def quiet(self, instruction):
        self.steps.append((instruction, None, 0))

    def write(self, engine):
        for instruction, sem, by in self.steps:
            made = instruction(engine)
            if sem is not None:
                made.then_inc(sem, by)


class Ring:

    def __init__(self, buffers):
        self.buffers, self.freed, self.at = buffers, [()] * len(buffers), -1
        self.held = [False] * len(buffers)

    def take(self, *lanes):
        self.at = (self.at + 1) % len(self.buffers)
        assert not self.held[self.at], "the next buffer is still in use"
        self.held[self.at] = True
        for lane in lanes:
            lane.wait(*self.freed[self.at])
        return self.at, self.buffers[self.at]

    def give(self, at, *posts):
        self.freed[at], self.held[at] = posts, False


def build(nc, io):
    with ExitStack() as everything:
        _build(nc, io, everything)


def _build(nc, io, everything):
    def semaphore(name):
        return Signal(everything.enter_context(nc.semaphore(name)))

    def sb(name, shape, dt, where=None):
        return (where or everything).enter_context(nc.sbuf_tensor(name, shape, dt))

    pe, act, dve, pool = (Lane(semaphore(n)) for n in ("pe_done", "act_done", "dve_done", "pool_done"))
    sync = Lane(None)

    bank = [everything.enter_context(nc.psum_tensor(f"bank{i}", [P, 512], F32)) for i in range(8)]

    def mm(out, lhsT, rhs, start, stop, post=False):
        f = lambda e: e.matmul(out, lhsT, rhs, start=start, stop=stop, skip_group_check=True)
        return pe.do(f) if post else pe.quiet(f)

    def flip(out, in_, ident, post=False):
        f = lambda e: e.transpose(out, in_, ident)
        return pe.do(f) if post else pe.quiet(f)

    def tt(lane, out, a, b, op):
        return lane.do(lambda e: e.tensor_tensor(out, a, b, op))

    def ts(lane, out, a, s1, s2, op0, op1=ALU.bypass):
        return lane.do(lambda e: e.tensor_scalar(out, a, s1, s2, op0, op1))

    def stt(out, a, s, b, op0, op1):
        return dve.do(lambda e: e.scalar_tensor_tensor(out, a, s, b, op0, op1))

    def copy(lane, out, a):
        return lane.do(lambda e: e.tensor_copy(out, a))

    def func(out, a, f, bias=0.0, scale=1.0):
        return act.do(lambda e: e.activation(out, a, f, bias=bias, scale=scale))

    def reduce(out, a, op):
        return dve.do(lambda e: e.tensor_reduce(out, a, AX, op))

    def recip(out, a):
        return dve.do(lambda e: e.reciprocal(out, a))

    def load(out, in_, signal, lane=sync):
        return lane.do(lambda e: e.dma_start(out, in_), signal, 16)

    def as32(ap):
        return ap.bitcast(F32)

    rows_dram = nc.dram_tensor("rows_scratch", [T, ROW], F32, kind="Internal").ap()
    x2_dram = nc.dram_tensor("x2_scratch", [T, D], F32, kind="Internal").ap()
    acc_dram = nc.dram_tensor("acc_scratch", [T, ACC], F32, kind="Internal").ap()
    logits_dram = nc.dram_tensor("logits_scratch", [B * E, M], F32, kind="Internal").ap()

    small = semaphore("small_loaded")
    ident = sb("ident", [P, P], F32)
    neg_ident = sb("neg_ident", [P, P], F32)
    ones_col = sb("ones_col", [P, 1], F32)
    lnl_g, lnl_b = sb("lnl_g", [P, 2], F32), sb("lnl_b", [P, 2], F32)
    lnx_g, lnx_b = sb("lnx_g", [CHF, 2], F32), sb("lnx_b", [CHF, 2], F32)
    qn_col, kn_col, gqk = sb("qn_col", [P, 1], F32), sb("kn_col", [P, 1], F32), sb("gqk", [P, 1], F32)
    router_w, router_b = sb("router_w", [P, 2, E], F32), sb("router_b", [E, 1], F32)
    mask_rows = sb("mask_rows", [B * CT, P], U8)
    mask_rows_f = sb("mask_rows_f", [B * CT, P], F32)
    mask_col = sb("mask_col", [P, B * CT], F32)
    logits = sb("logits", [P, NT, E], F32)

    attention = ExitStack()
    ab = lambda name, shape, dt: sb(name, shape, dt, attention)
    bo_rows, nw_rows = ab("bo_rows", [P, D], F32), ab("nw_rows", [P, D], F32)
    WL = 3 * INNER
    w_lat_hi, w_lat_lo = ab("w_lat_hi", [P, 2, WL], F32R), ab("w_lat_lo", [P, 2, WL], F32R)
    w_ctx_hi, w_ctx_lo = ab("w_ctx_hi", [CHF, 2, 2 * INNER], F32R), ab("w_ctx_lo", [CHF, 2, 2 * INNER], F32R)
    wo_hi, wo_lo = ab("wo_hi", [P, H, D], F32R), ab("wo_lo", [P, H, D], F32R)
    x_in = [ab(f"x_in{i}", [P, MT, D], F32) for i in range(2)]
    c_in = [ab(f"c_in{i}", [P, 4, DC], F32) for i in range(2)]
    z_nat = ab("z_nat", [P, 4, D], F32)
    z_full = ab("z_full", [P, 2, 512], F32)
    z_hi, z_lo = ab("z_hi", [P, 2, 512], F32R), ab("z_lo", [P, 2, 512], F32R)
    squares = [ab(f"squares{i}", [P, 512], F32) for i in range(2)]
    qk_nat = ab("qk_nat", [P, MT, 2 * INNER], F32)
    kc_nat = ab("kc_nat", [P, CT, INNER], F32)
    v_nat = [ab(f"v_nat{i}", [P, KT, INNER], F32) for i in range(2)]
    qa = [ab(f"qa{i}", [P, 2, M], F32R) for i in range(2)]
    qb = [ab(f"qb{i}", [P, 2, M], F32R) for i in range(2)]
    ka = [ab(f"ka{i}", [P, 2, KEYS], F32R) for i in range(2)]
    kb = [ab(f"kb{i}", [P, 2, KEYS], F32R) for i in range(2)]
    maxima = ab("maxima", [P, 2, MT, 3], F32)
    row_max = ab("row_max", [P, 2, MT], F32)
    masked_scores = [ab(f"masked_scores{i}", [P, 512], BF16) for i in range(2)]
    mask_bias8 = ab("mask_bias8", [P, NC_], U8)
    mask_bias = ab("mask_bias", [P, NC_], BF16)
    probs = [ab(f"probs{i}", [P, M], F32) for i in range(6)]
    prob_sum = [ab(f"prob_sum{i}", [P, 2, M], F32) for i in range(2)]
    inv_den = ab("inv_den", [P, H, MT], F32)
    o_stack = ab("o_stack", [P, H, M], F32R)
    router_probs = ab("router_probs", [P, MT, E], F32)
    xn_T = z_full
    stats = ab("stats", [P, KT, 6], F32)
    mean_var = ab("mean_var", [P, KT, 2], F32)
    N_HEADS = (CT + 2 * MT) * H
    norm_w, norm_y, norm_t = (ab(n, [P, N_HEADS], F32) for n in ("norm_w", "norm_y", "norm_t"))
    sq_sum = ab("sq_sum", [P, N_HEADS], F32)
    soft = ab("soft", [P, MT, E], F32)
    soft_s = ab("soft_s", [P, 2, MT], F32)

    def column(name, tile):
        return load(tile[:], io[name], small)

    x_sem = [semaphore(f"x_loaded{i}") for i in range(2)]
    c_sem = [semaphore(f"c_loaded{i}") for i in range(2)]
    mask_sem = semaphore("mask_loaded")
    weight_sem = semaphore("weights_loaded")
    x_ring, c_ring = Ring(x_in), Ring(c_in)
    x_loaded, c_loaded = {}, {}

    def load_x(b):
        at, buf = x_ring.take(sync)
        x_loaded[b] = load(buf[:], io["x"][b].rearrange("(j p) d -> p j d", p=P), x_sem[at])

    def load_ctx(b, half):
        at, buf = c_ring.take(sync)
        src = io["ctx"][b].rearrange("(j p) d -> p j d", p=P)[:, 4 * half:4 * half + 4, :]
        c_loaded[b, half] = (at, load(buf[:], src, c_sem[at]))

    load_x(0)
    column("ident", ident)
    column("neg_ident", neg_ident)
    for name, tile in (("lnl_g", lnl_g), ("lnl_b", lnl_b), ("lnx_g", lnx_g), ("lnx_b", lnx_b),
                       ("router_w", router_w), ("router_b", router_b)):
        column(name, tile)
    for half in (slice(0, DH), slice(DH, P)):
        load(qn_col[half, :], io["qn_g"], small)
        load(kn_col[half, :], io["kn_g"], small)
    load(mask_rows[:], io["mask"].rearrange("b (j p) -> (b j) p", p=P), small)
    load(bo_rows[:], io["bo"].partition_broadcast(P), small)
    small_loaded = load(nw_rows[:], io["norm_weight"].partition_broadcast(P), small)
    raw = v_nat[1][:].rearrange("p j d -> p (j d)")
    raw_lat = raw[:, 0:2 * WL].rearrange("p (a b) -> p a b", a=2)
    raw_ctx = raw[0:CHF, 2 * WL:2 * WL + 4 * INNER].rearrange("p (a b) -> p a b", a=2)
    raw_wo = [probs[i][:].rearrange("p (a b) -> p a b", a=2) for i in range(2)]
    load(raw_lat, io["w_lat"].rearrange("(a p) n -> p a n", p=P), weight_sem)
    load_ctx(0, 0)
    load(raw_ctx, io["w_ctx"].rearrange("(a p) n -> p a n", p=CHF), weight_sem)
    load_ctx(0, 1)
    for half in (slice(0, DH), slice(DH, P)):
        for i in range(2):
            weights_loaded = load(raw_wo[i][half], io["wo"].rearrange("(h d) n -> d h n", d=DH)[:, 2 * i:2 * i + 2, :],
                                  weight_sem)

    pool.do(lambda e: e.memset(ones_col[:], 1.0))
    zeros = squares[1][:, 0:ACC]
    zeros_set = pool.do(lambda e: e.memset(zeros, 0.0))
    for h in range(H):
        other = slice(DH, P) if h % 2 == 0 else slice(0, DH)
        wo_lo_cleared = dve.do(lambda e, o=wo_lo[other, h, :]: e.memset(as32(o), 0.0))
    act.wait(weights_loaded)
    lat_hi_made = func(w_lat_hi[:], raw_lat, ACT.Copy)
    ctx_hi_made = func(w_ctx_hi[:], raw_ctx, ACT.Copy)
    for i in range(2):
        wo_hi_made = func(wo_hi[:, 2 * i:2 * i + 2, :], raw_wo[i], ACT.Copy)
    pool.wait(weights_loaded, lat_hi_made)
    lat_lo_made = tt(pool, w_lat_lo[:], raw_lat, as32(w_lat_hi[:]), ALU.subtract)
    pool.wait(ctx_hi_made)
    ctx_lo_made = tt(pool, w_ctx_lo[:], raw_ctx, as32(w_ctx_hi[:]), ALU.subtract)
    dve.wait(wo_hi_made, wo_lo_cleared)
    for h in range(H):
        own = slice(0, DH) if h % 2 == 0 else slice(DH, P)
        wo_lo_made = tt(dve, wo_lo[own, h, :], raw_wo[h // 2][own, h % 2, :], as32(wo_hi[own, h, :]), ALU.subtract)
    dve.wait(wo_lo_made)
    for i in range(2):
        for hh, half in enumerate((slice(DH, P), slice(0, DH))):
            kb_ones_set = dve.do(lambda e, o=kb[i][half, hh, :]: e.memset(as32(o), 1.0))
    dve.wait(small_loaded)
    mask_f_made = ts(dve, mask_rows_f[:], mask_rows[:], -1.0, -MASKED, ALU.add, ALU.mult)
    gqk_made = ts(dve, gqk[:], qn_col[:], kn_col[:, 0:1], SCALE, ALU.mult, ALU.mult)
    zero_sem = semaphore("acc_cleared")
    sync.wait(zeros_set)
    acc_view = acc_dram.rearrange("(j p) d -> p j d", p=P)
    for j in range(0, NT, 8):
        acc_cleared = load(acc_view[:, j:j + 8, :], zeros.unsqueeze(1).broadcast_to([P, 8, ACC]), zero_sem)

    score_banks = Ring(bank[0:2])
    o_bank, o_bank_freed = bank[2], [()]
    max_banks = Ring(bank[3:5])
    misc = Ring(bank[5:8])

    at, out = misc.take(pe)
    pe.wait(small_loaded, mask_f_made)
    mask_flipped = flip(out[:, 0:B * CT], mask_rows_f[:], ident[0:B * CT, 0:B * CT], post=True)
    act.wait(mask_flipped)
    mask_col_made = func(mask_col[:], out[:, 0:B * CT], ACT.Copy)
    misc.give(at, mask_col_made)

    def rsqrt(y, w, t):
        yi, wi = y.bitcast(I32), w.bitcast(I32)
        dve.wait(dve.latest())
        dve.wait(ts(dve, yi, wi, 1, None, ALU.logical_shift_right))
        dve.wait(ts(dve, yi, yi, -1.0, float(RSQRT_MAGIC), ALU.mult, ALU.add))
        for _ in range(3):
            dve.wait(tt(dve, t, y, y, ALU.mult))
            dve.wait(stt(t, t, -0.5, w, ALU.mult, ALU.mult))
            last = stt(y, t, 1.5, y, ALU.add, ALU.mult)
            dve.wait(last)
        return last

    z_free = [(), ()]
    sq_ring = Ring(squares)
    sq_ring.freed[1] = (acc_cleared,)
    nat_free = {"qk": (), "kc": ()}
    qk_normed, v_written = {}, {}
    v_free = [(), (lat_lo_made, ctx_lo_made)]

    def idle(n):
        for _ in range(n):
            yield

    def tile_stats(src, at):
        for i in range(4):
            last = dve.do(lambda e, o=stats[:, at + i, :], a=src[:, i, :]: e.bn_stats(o, a))
        dve.wait(last)
        for i in range(4):
            last = dve.do(lambda e, o=mean_var[:, at + i, :], a=stats[:, at + i, :]: e.bn_aggr(o, a))
        return last

    def centre(src, at, dst):
        for i in range(4):
            last = ts(dve, dst[:, i, :], src[:, i, :], mean_var[:, at + i, 0:1], norm_y[:, at + i:at + i + 1],
                      ALU.subtract, ALU.mult)
        return last

    def spread(start, width, src, z_made, g, b, made):
        for half in range(2):
            at, out = misc.take(pe)
            pe.wait(z_made)
            for i in range(4):
                flipped = flip(out[0:width, i * P:(i + 1) * P],
                               src[:, i, half * width:(half + 1) * width], ident[:], post=i == 3)
            dve.wait(flipped, *z_full_free[half])
            full = ts(dve, z_full[0:width, half, :], out[0:width, :], g[:, half:half + 1], b[:, half:half + 1],
                      ALU.mult, ALU.add)
            misc.give(at, full)
            act.wait(full, *z_free[0])
            hi = func(z_hi[0:width, half, :], z_full[0:width, half, :], ACT.Copy)
            pool.wait(full, hi, *z_free[0])
            lo = tt(pool, z_lo[0:width, half, :], z_full[0:width, half, :], as32(z_hi[0:width, half, :]),
                    ALU.subtract)
            z_full_free[half] = (hi, lo)
            made += [hi, lo]
            start.append(flipped)
            yield

    z_full_free = [(), ()]

    def three_passes(out, width, tile, w_hi, w_lo, cols):
        at = slice(tile * P, (tile + 1) * P)
        n = 0
        for half in range(2):
            for z, w in ((z_hi, w_hi), (z_lo, w_hi), (z_hi, w_lo)):
                last = mm(out, z[0:width, half, at], w[0:width, half, cols], n == 0, n == 5, post=n == 5)
                n += 1
        return last

    def project(b):
        x = x_in[b % 2]
        for chunk in range(2):
            dve.wait(c_loaded[b, chunk][1])
            stats_made = tile_stats(c_in[c_loaded[b, chunk][0]], 4 * chunk)
            yield
        dve.wait(x_loaded[b])
        stats_made = tile_stats(x, CT)
        yield
        dve.wait(stats_made)
        ts(dve, norm_w[:, 0:CT], mean_var[:, 0:CT, 1], 1.0, LN_EPS, ALU.mult, ALU.add)
        ts(dve, norm_w[:, CT:KT], mean_var[:, CT:KT, 1], 1.0 + LN_EPS, LN_EPS * LN_EPS, ALU.mult, ALU.add)
        dve.wait(rsqrt(norm_y[:, 0:KT], norm_w[:, 0:KT], norm_t[:, 0:KT]))
        yield
        centred = [centre(c_in[c_loaded[b, chunk][0]], 4 * chunk, c_in[c_loaded[b, chunk][0]])
                   for chunk in range(2)]
        yield
        dve.wait(*z_free[1])
        z_made = centre(x, CT, z_nat)
        pool.wait(z_made, small_loaded)
        residual_made[b] = tt(pool, x[:], x[:], bo_rows[:].unsqueeze(1).broadcast_to([P, MT, D]), ALU.add)
        pending = []

        def sum_squares():
            while pending:
                place, heads, sat, sq, sq_out = pending.pop()
                dve.wait(sq_out)
                summed = reduce(sq_sum[:, place:place + heads],
                                sq[:, 0:heads * DH].rearrange("p (h d) -> p h d", d=DH), ALU.add)
                sq_ring.give(sat, summed)

        for chunk in range(2):
            at_in = c_loaded[b, chunk][0]
            start, made = [], []
            yield from spread(start, CHF, c_in[at_in], centred[chunk], lnx_g, lnx_b, made)
            c_ring.give(at_in, start[-1])
            if b + 1 < B:
                load_ctx(b + 1, chunk)
            yield from idle(3)
            assert b == 0 or (b - 1, 1) in prepared, "q and k of the last batch are still needed"
            for i in range(4):
                tile = 4 * chunk + i
                at, out = misc.take(pe)
                pe.wait(ctx_lo_made, *made)
                kv_done = three_passes(out[:], CHF, i, w_ctx_hi, w_ctx_lo, slice(0, 2 * INNER))
                act.wait(kv_done, *nat_free["kc"], *v_free[b % 2])
                func(kc_nat[:, tile, :], out[:, 0:INNER], ACT.Copy)
                sat, sq = sq_ring.take(act)
                sq_out = func(sq[:, 0:INNER], out[:, 0:INNER], ACT.Square)
                v_out = func(v_nat[b % 2][:, tile, :], out[:, INNER:2 * INNER], ACT.Copy)
                misc.give(at, v_out)
                sum_squares()
                pending.append((tile * H, H, sat, sq, sq_out))
                yield
            z_free[0] = (kv_done,)
        start, made = [], []
        yield from spread(start, DHF, z_nat, z_made, lnl_g, lnl_b, made)
        z_free[1] = (start[-1],)
        yield from idle(3)
        for i in range(MT):
            at, out = misc.take(pe)
            pe.wait(lat_lo_made, *made)
            qk_done = three_passes(out[:], DHF, i, w_lat_hi, w_lat_lo, slice(0, 2 * INNER))
            act.wait(qk_done, *nat_free["qk"])
            func(qk_nat[:, i, :], out[:], ACT.Copy)
            sat, sq = sq_ring.take(act)
            sq_out = func(sq[:], out[:], ACT.Square)
            misc.give(at, sq_out)
            sum_squares()
            pending.append(((CT + 2 * i) * H, 2 * H, sat, sq, sq_out))
            yield
            at, out = misc.take(pe)
            v_done = three_passes(out[:, 0:INNER], DHF, i, w_lat_hi, w_lat_lo, slice(2 * INNER, WL))
            act.wait(v_done, *v_free[b % 2])
            v_out = func(v_nat[b % 2][:, CT + i, :], out[:, 0:INNER], ACT.Copy)
            misc.give(at, v_out)
            if i % 2:
                yield
        z_free[0] = (v_done,)
        v_written[b] = v_out
        sum_squares()
        dve.wait(dve.latest())
        dve.wait(ts(dve, norm_w[:], sq_sum[:], 1.0 / DH, RMS_EPS ** 2, ALU.mult, ALU.max))
        dve.wait(rsqrt(norm_y[:], norm_w[:], norm_t[:]), v_out)
        yield
        inverse = lambda first, tiles: (norm_y[:, first * H:(first + tiles) * H].unsqueeze(2)
                                        .broadcast_to([P, tiles * H, DH]))
        for i in range(0, MT, 2):
            view = qk_nat[:, i:i + 2, :].rearrange("p j (h d) -> p (j h) d", d=DH)
            normed = tt(dve, view, view, inverse(CT + 2 * i, 4), ALU.mult)
        qk_normed[b] = normed
        yield
        for i in range(0, CT, 4):
            view = kc_nat[:, i:i + 4, :].rearrange("p j (h d) -> p (j h) d", d=DH)
            normed = tt(dve, view, view, inverse(i, 4), ALU.mult)
            kc_normed[b, i // 4] = normed
            yield

    residual_made, kc_normed = {}, {}
    unit_free = [(), ()]
    prepared, shift_made = {}, {}
    mask_free = [()]

    def prepare(b, pair):
        u = (2 * b + pair) % 2
        if pair == 0:
            load_mask(b)
        both = slice(2 * pair * DH, 2 * (pair + 1) * DH)
        at, out = misc.take(pe)
        pe.wait(qk_normed[b])
        for j in range(MT):
            flipped = flip(out[:, j * P:(j + 1) * P], qk_nat[:, j, both], ident[:], post=j == MT - 1)
        q_hi, q_lo = [], []
        for hh, (hi, lo) in enumerate(ROWS):
            act.wait(flipped, gqk_made, *unit_free[u])
            q_hi.append(func(qb[u][hi, hh, :], out[hi, :], ACT.Identity, scale=gqk[hi, 0:1]))
            dve.wait(q_hi[hh], *unit_free[u])
            q_lo.append(stt(qa[u][lo, hh, :], out[hi, :], gqk[hi, 0:1], as32(qb[u][hi, hh, :]),
                            ALU.mult, ALU.subtract))
        misc.give(at, *q_lo)
        sync.wait(*q_hi, *unit_free[u])
        for hh, (hi, lo) in enumerate(ROWS):
            load(as32(qa[u][hi, hh, :]), as32(qb[u][hi, hh, :]), copied[u])
        yield
        for g in range(3):
            at, out = misc.take(pe)
            pe.wait(kc_normed[b, min(g, 1)])
            for j in range(4):
                tile = 4 * g + j
                k = (kc_nat[:, tile, both] if tile < CT else
                     qk_nat[:, tile - CT, INNER + both.start:INNER + both.stop])
                flipped = flip(out[:, j * P:(j + 1) * P], k, ident[:], post=j == 3)
            cols = slice(512 * g, 512 * (g + 1))
            k_hi, k_lo = [], []
            for hh, (hi, lo) in enumerate(ROWS):
                act.wait(flipped, kb_ones_set, *unit_free[u])
                k_hi.append(func(ka[u][hi, hh, cols], out[hi, :], ACT.Copy))
                dve.wait(k_hi[hh], *unit_free[u])
                k_lo.append(tt(dve, kb[u][hi, hh, cols], out[hi, :], as32(ka[u][hi, hh, cols]), ALU.subtract))
            misc.give(at, *k_lo)
            sync.wait(*k_hi)
            for hh, (hi, lo) in enumerate(ROWS):
                k_copied = load(as32(ka[u][lo, hh, cols]), as32(ka[u][hi, hh, cols]), copied[u])
            yield
        prepared[b, pair] = (k_copied, *q_lo, *k_lo)
        if pair == 1:
            nat_free["qk"] = nat_free["kc"] = (flipped,)

    ROWS = ((slice(0, DH), slice(DH, P)), (slice(DH, P), slice(0, DH)))
    copied = [semaphore(f"copied{i}") for i in range(2)]

    def load_mask(b):
        sync.wait(*mask_free[0])
        mask_here[b] = load(mask_bias8[:], io["mask"][b].partition_broadcast(P), mask_sem)

    def make_mask(b):
        act.wait(mask_here[b], *max_free[0])
        made = func(mask_bias[:], mask_bias8[:], ACT.Copy, bias=MASKED, scale=-MASKED)
        mask_free[0] = (made,)
        return made

    max_free = [()]
    mask_made, mask_here = {}, {}

    def find_maxima(b, pair):
        u = (2 * b + pair) % 2
        if pair == 0:
            mask_made[b] = make_mask(b)
        pe.wait(*prepared[b, pair])
        for hh in range(2):
            for j in range(MT):
                for g in range(3):
                    at, out = max_banks.take(pe)
                    done = mm(out[:], qa[u][:, hh, j * P:(j + 1) * P], ka[u][:, hh, 512 * g:512 * (g + 1)],
                              True, True, post=True)
                    if g < 2:
                        jat, junk = junk_ring.take(dve)
                        dve.wait(done, mask_made[b])
                        mx = dve.do(lambda e, o=junk[:], a=out[:], m=mask_bias[:, 512 * g:512 * (g + 1)],
                                    r=maxima[:, hh, j, g:g + 1]:
                                    e.tensor_tensor_reduce(o, a, m, 1.0, -3e38, ALU.add, ALU.max, r))
                        junk_ring.give(jat, mx)
                    else:
                        dve.wait(done)
                        mx = reduce(maxima[:, hh, j, 2:3], out[:], ALU.max)
                    max_banks.give(at, mx)
                    yield
        max_free[0] = (mx,)
        dve.wait(mx)
        dve.wait(reduce(row_max[:], maxima[:], ALU.max))
        for hh, (hi, lo) in enumerate(ROWS):
            cols = qb[u][lo, hh, :].rearrange("p (j q) -> p j q", q=P)
            for low in (0, DH):
                m = row_max[low:low + DH, hh, :].unsqueeze(2).broadcast_to([DH, MT, DH])
                i = neg_ident[low:low + DH, low:low + DH].unsqueeze(1).broadcast_to([DH, MT, DH])
                last = tt(dve, cols[:, :, low:low + DH], i, m, ALU.mult)
        shift_made[b, pair] = last
        yield

    junk_ring = Ring(masked_scores)
    prob_ring = Ring(probs)
    prob_ring.freed[0] = prob_ring.freed[1] = (wo_hi_made, wo_lo_made)
    sum_ring = Ring(prob_sum)
    summed_probs = {}
    o_written = {}
    o_free = [()]
    inv_den_free = [()]
    den_made = {}

    def attend(b, pair, between):
        u = (2 * b + pair) % 2
        pe.wait(*prepared[b, pair], shift_made[b, pair], v_written[b])
        waiting = []

        def with_v(kt, hh, pat, p, exp_done):
            if kt == 0:
                pe.wait(*o_bank_freed[0])
            pe.wait(exp_done)
            h = 2 * pair + hh
            used = mm(o_bank[hh * DH:(hh + 1) * DH, :], v_nat[b % 2][:, kt, h * DH:(h + 1) * DH], p[:],
                      kt == 0, kt == KT - 1, post=True)
            if kt == 0:
                first[hh] = (pat, p, exp_done, used)
            else:
                pool.wait(exp_done)
                if kt == 1:
                    if hh == 0:
                        taken.append(sum_ring.take(pool))
                    pool.wait(first[hh][2])
                total = taken[0][1]
                if kt == 1:
                    added = tt(pool, total[:, hh, :], first[hh][1][:], p[:], ALU.add)
                    prob_ring.give(first[hh][0], first[hh][3], added)
                else:
                    pool.wait(summed[hh])
                    added = tt(pool, total[:, hh, :], total[:, hh, :], p[:], ALU.add)
                summed[hh] = added
                prob_ring.give(pat, used, added)
            return used

        first, summed, taken = {}, {}, []
        for kt in range(KT):
            now = []
            for hh in range(2):
                at, out = score_banks.take(pe)
                keys = slice(kt * P, (kt + 1) * P)
                mm(out[:], ka[u][:, hh, keys], qa[u][:, hh, :], True, False)
                scored = mm(out[:], kb[u][:, hh, keys], qb[u][:, hh, :], False, True, post=True)
                pat, p = prob_ring.take(act)
                act.wait(scored)
                if kt < CT:
                    col = b * CT + kt
                    exp_done = func(p[:], out[:], ACT.Exp, bias=mask_col[:, col:col + 1])
                else:
                    exp_done = func(p[:], out[:], ACT.Exp)
                score_banks.give(at, exp_done)
                now.append((kt, hh, pat, p, exp_done))
                if hh == 0:
                    between()
            if kt == 0:
                last_products[0]()
            between()
            for item in waiting:
                with_v(*item)
            waiting = now
            between()
        unit_free[u] = (scored,)

        def close():
            for item in waiting:
                used = with_v(*item)
            summed_probs[b, pair] = (summed[0], summed[1], taken[0][0])
            if pair == 1:
                v_free[b % 2] = (used,)
            act.wait(used, *o_free[0])
            a, c = 2 * pair, 2 * pair + 1
            hi_a = func(o_stack[0:DH, a, :], o_bank[0:DH, :], ACT.Copy)
            hi_c = func(o_stack[DH:P, c, :], o_bank[DH:P, :], ACT.Copy)
            dve.wait(hi_a, hi_c, *o_free[0])
            tt(dve, o_stack[DH:P, a, :], o_bank[0:DH, :], as32(o_stack[0:DH, a, :]), ALU.subtract)
            lo_c = tt(dve, o_stack[0:DH, c, :], o_bank[DH:P, :], as32(o_stack[DH:P, c, :]), ALU.subtract)
            o_bank_freed[0] = (hi_c, lo_c)
            o_written[b, pair] = (hi_c, lo_c)

        last_products[0] = close

    last_products = [lambda: None]

    def denominators(b, pair):
        s0, s1, sat = summed_probs[b, pair]
        at, out = misc.take(pe)
        pe.wait(s0, s1)
        for hh in range(2):
            for j in range(MT):
                done = mm(out[:, hh * MT + j:hh * MT + j + 1], prob_sum[sat][:, hh, j * P:(j + 1) * P],
                          ones_col[:], True, True, post=True)
        sum_ring.give(sat, done)
        dve.wait(done, *inv_den_free[0])
        made = recip(inv_den[:, 2 * pair:2 * pair + 2, :], out[:, 0:2 * MT].rearrange("p (h j) -> p h j", h=2))
        misc.give(at, made)
        den_made[b, pair] = made
        yield

    rows_sem = semaphore("rows_stored")
    x2_sem = semaphore("x2_stored")
    chunk_sem = semaphore("chunk_stored")
    rows_free, x2_stored = [()], {}
    rows_stored = [None]

    def finish(b):
        x = x_in[b % 2]
        pe.wait(*o_written[b, 0], *o_written[b, 1], wo_lo_made)
        before_sum = [(), ()]
        for j0 in range(0, MT, 2):
            for pair in range(2):
                outs = []
                for j in (j0, j0 + 1):
                    at, out = misc.take(pe)
                    outs.append((at, out, j))
                    for hh in range(2):
                        h, dst = 2 * pair + hh, out[:, hh * D:(hh + 1) * D]
                        at_q = slice(j * P, (j + 1) * P)
                        mm(dst, o_stack[:, h, at_q], wo_hi[:, h, :], True, False)
                        done = mm(dst, o_stack[:, h, at_q], wo_lo[:, h, :], False, True, post=True)
                dve.wait(done, residual_made[b], *den_made_all(b))
                added = [None, None]
                for hh in range(2):
                    h = 2 * pair + hh
                    for n, (at, out, j) in enumerate(outs):
                        dve.wait(added[n], *before_sum[n])
                        added[n] = stt(x[:, j, :], out[:, hh * D:(hh + 1) * D], inv_den[:, h, j:j + 1], x[:, j, :],
                                       ALU.mult, ALU.add)
                before_sum = [(added[0],), (added[1],)]
                for n, (at, out, j) in enumerate(outs):
                    misc.give(at, added[n])
                yield
        o_free[0] = (done,)
        inv_den_free[0] = (added[1],)
        sync.wait(added[1])
        x2_stored[b] = load(x2_dram[b * M:(b + 1) * M, :].rearrange("(j p) d -> p j d", p=P), x[:], x2_sem)
        xn = z_nat[:]
        dve.wait(added[1])
        dve.wait(tile_stats(x, 0))
        dve.wait(ts(dve, norm_w[:, 0:MT], mean_var[:, 0:MT, 1], 1.0 + LN_EPS, LN_EPS * LN_EPS, ALU.mult, ALU.add))
        dve.wait(rsqrt(norm_y[:, 0:MT], norm_w[:, 0:MT], norm_t[:, 0:MT]), *z_free[1], *rows_free[0])
        normed = centre(x, 0, xn)
        x_ring.give(b % 2, x2_stored[b], normed)
        if b + 2 < B:
            load_x(b + 2)
        yield
        pool.wait(normed)
        weighted = tt(pool, xn, xn, nw_rows[:].unsqueeze(1).broadcast_to([P, MT, D]), ALU.mult)
        yield
        yield
        yield
        pe.wait(weighted)
        halves = []
        for half in range(2):
            at, out = misc.take(pe)
            for j in range(MT):
                flipped = flip(out[:, j * P:(j + 1) * P], xn[:, j, half * P:(half + 1) * P], ident[:],
                               post=j == MT - 1)
            act.wait(flipped, *z_full_free[half])
            xn_flipped = flipped
            halves.append(func(xn_T[:, half, :], out[:], ACT.Copy))
            misc.give(at, halves[-1])
        yield
        at, out = misc.take(pe)
        pe.wait(*halves)
        mm(out[0:E, :], router_w[:, 0, :], xn_T[:, 0, :], True, False)
        routed = mm(out[0:E, :], router_w[:, 1, :], xn_T[:, 1, :], False, True, post=True)
        z_full_free[0] = z_full_free[1] = (routed,)
        act.wait(routed)
        sat, sq = sq_ring.take(act)
        logits_T = sq[0:E, :]
        biased = func(logits_T, out[0:E, :], ACT.Identity, bias=router_b[:, 0:1])
        misc.give(at, biased)
        sync.wait(biased)
        chunk_stored[b] = load(logits_dram[b * E:(b + 1) * E, :], logits_T, chunk_sem)
        yield
        at, out = misc.take(pe)
        pe.wait(biased)
        for j in range(MT):
            flipped = flip(out[:, j * E:(j + 1) * E], logits_T[:, j * P:(j + 1) * P], ident[0:E, 0:E],
                           post=j == MT - 1)
        sq_ring.give(sat, chunk_stored[b], flipped)
        mine = logits[:, b * MT:(b + 1) * MT, :]
        dve.wait(flipped)
        natural = copy(dve, mine, out[:, 0:MT * E].rearrange("p (j e) -> p j e", j=MT))
        misc.give(at, natural)
        dve.wait(natural)
        dve.wait(reduce(soft_s[:, 0, :], mine, ALU.max))
        centred = tt(dve, soft[:], mine, soft_s[:, 0, :].unsqueeze(2).broadcast_to([P, MT, E]), ALU.subtract)
        yield
        act.wait(centred)
        powers = func(soft[:], soft[:], ACT.Exp)
        dve.wait(powers)
        dve.wait(reduce(soft_s[:, 0, :], soft[:], ALU.add))
        dve.wait(recip(soft_s[:, 1, :], soft_s[:, 0, :]))
        scaled = tt(dve, router_probs[:], soft[:],
                    soft_s[:, 1, :].unsqueeze(2).broadcast_to([P, MT, E]), ALU.mult)
        sync.wait(scaled, weighted)
        mine = rows_dram[b * M:(b + 1) * M, :].rearrange("(j p) d -> p j d", p=P)
        load(mine[:, :, 0:D], xn, rows_sem)
        stored = load(mine[:, :, D:ROW], router_probs[:], rows_sem)
        rows_free[0] = (stored,)
        z_free[1] = (stored, xn_flipped)
        rows_stored[0] = stored
        yield

    chunk_stored = {}

    def den_made_all(b):
        return (den_made[b, 0], den_made[b, 1])

    def run(*stages):
        for stage in stages:
            for _ in stage:
                pass

    def chain(*stages):
        for stage in stages:
            yield from stage

    def paced(work, n_steps, n_points):
        state = {"point": 0, "made": 0}

        def advance():
            state["point"] += 1
            goal = -(-n_steps * state["point"] // n_points)
            while state["made"] < goal:
                state["made"] += 1
                if next(work, "end") == "end":
                    state["made"] = n_steps * n_points
        return advance

    load_x(1)
    run(project(0), prepare(0, 0), find_maxima(0, 0))
    POINTS = 2 * 3 * KT
    Z_END = 57
    for b in range(B):
        more = b + 1 < B
        z_work = chain(*([idle(2), denominators(b - 1, 1), idle(1), finish(b - 1)] if b else []),
                       *([project(b + 1)] if more else []))
        z_step = paced(z_work, (18 if b else 0) + (39 if more else 0), Z_END)
        q_step = paced(chain(prepare(b, 1), idle(4), find_maxima(b, 1)), 4 + 4 + 25, 3 * KT - 3)
        q_work = chain(denominators(b, 0), *([prepare(b + 1, 0), idle(3), find_maxima(b + 1, 0)] if more else []))
        next_step = paced(q_work, 1 + (4 + 3 + 25 if more else 0), POINTS - Z_END - 2)
        state = {"point": 0}

        def between():
            state["point"] += 1
            if state["point"] < Z_END or b == B - 1:
                z_step()
            elif state["point"] == Z_END:
                run(z_work)
            else:
                next_step()
            if state["point"] <= 3 * KT:
                q_step()

        for pair in range(2):
            attend(b, pair, between)
        run(z_work, q_work)
    last_products[0]()
    run(denominators(B - 1, 1), finish(B - 1))
    pieces = (pe.latest(), act.latest(), dve.latest(), pool.latest())
    stores_done = (x2_stored[B - 1], rows_stored[0], chunk_stored[B - 1], acc_cleared)
    attention.close()
    choice = ExitStack()
    cb = lambda name, shape, dt: sb(name, shape, dt, choice)

    GATHERS, LISTS = 3, 5
    w1_raw = [sb(f"w1_raw{i}", [P, 2, F], F32) for i in range(2)]
    w2_raw = [sb(f"w2_raw{i}", [P, FT, D], F32) for i in range(2)]
    w1_hi, w1_lo = ([sb(f"w1_{n}{i}", [P, 2, F], F32R) for i in range(2)] for n in ("hi", "lo"))
    w2_hi, w2_lo = ([sb(f"w2_{n}{i}", [P, FT, D], F32R) for i in range(2)] for n in ("hi", "lo"))
    b1_cols = sb("b1_cols", [P, E, FT], F32)
    b2_rows = [sb(f"b2_rows{i}", [P, D], F32) for i in range(4)]
    gathered = [sb(f"gathered{i}", [P, 2, ROW], F32) for i in range(GATHERS)]
    xe_hi, xe_lo = ([sb(f"xe_{n}{i}", [P, 2, CAP], F32R) for i in range(2)] for n in ("hi", "lo"))
    h_full = [sb(f"h_full{i}", [P, CAP], F32) for i in range(2)]
    h_hi, h_lo = sb("h_hi", [P, FT, CAP], F32R), sb("h_lo", [P, FT, CAP], F32R)
    y_out = [sb(f"y_out{i}", [P, 2, ACC], F32) for i in range(2)]
    token_index = [sb(f"token_index{i}", [P, 2], U32) for i in range(LISTS)]
    slot_hi, slot_lo = sb("slot_hi", [P, E, NT], F32), sb("slot_lo", [P, E, NT], F32)
    iota16, tile_ids = sb("iota16", [P, 16], F32), sb("tile_ids", [P, NT], BF16)
    token_in_tile = sb("token_in_tile", [P, 1], F32)
    expand16, pick = sb("expand16", [16, P], F32), sb("pick", [P, 2, 16], F32)
    hot_hi, hot_lo = sb("hot_hi", [P, NT, 16], BF16), sb("hot_lo", [P, NT, 16], BF16)
    hot_ids = sb("hot_ids", [P, NT, 2, 16], BF16)
    list_parts, list16 = sb("list_parts", [16, 32], F32), sb("list16", [16, 16], F32)
    picked, list_f = sb("picked", [P, 2, 16], F32), sb("list_f", [P, 2], F32)

    sync.wait(*pieces, *stores_done)
    consts_sem = semaphore("choice_consts_loaded")
    logits_by_chunk = cb("logits_by_chunk", [P, M], F32)
    load(logits_by_chunk[:], logits_dram, consts_sem)
    same_expert, search_bits = cb("same_expert", [P, P], F32), cb("search_bits", [P, 31], U32)
    before_f, scan_keep = cb("before_f", [P, P], F32), cb("scan_keep", [P, T // P * E], F32)
    before, all_ones = cb("before", [P, P], BF16), cb("all_ones", [P, P], BF16)
    for tile, name in ((same_expert, "same_expert"), (search_bits, "search_bits"), (before_f, "before"),
                       (scan_keep, "scan_keep"), (iota16, "iota16"), (token_in_tile, "token_in_tile"),
                       (expand16, "expand16"), (pick, "pick"), (b1_cols, "fc1_bias")):
        load(tile[:], io[name], consts_sem)
    tile_ids_f = cb("tile_ids_f", [P, NT], F32)
    consts_loaded = load(tile_ids_f[:], io["tile_ids"], consts_sem)

    w_sem = [semaphore(f"expert_weights_loaded{i}") for i in range(2)]
    raw_free, weights_here = [(), ()], {}
    b2_sem = [semaphore(f"expert_bias_loaded{i}") for i in range(4)]
    b2_free, b2_here = [()] * 4, {}

    def load_expert(e):
        i = e % 2
        sync.wait(*raw_free[i], *b2_free[e % 4])
        load(w1_raw[i][:], io["fc1"][e], w_sem[i])
        weights_here[e] = load(w2_raw[i][:], io["fc2"][e], w_sem[i])
        b2_here[e] = load(b2_rows[e % 4][:], io["fc2_bias"][e].partition_broadcast(P), b2_sem[e % 4])

    load_expert(0)
    load_expert(1)

    split_free = [(), ()]
    split_made = {}

    def split_weights(e):
        i = e % 2
        posts = []
        halves = [(w1_raw[i][:, a, :], w1_hi[i][:, a, :], w1_lo[i][:, a, :]) for a in range(2)]
        halves += [tuple(w[:, 4 * a:4 * a + 4, :] for w in (w2_raw[i], w2_hi[i], w2_lo[i])) for a in range(2)]
        for n, (raw, hi, lo) in enumerate(halves):
            act.wait(weights_here[e], *split_free[i])
            hi_made = func(hi, raw, ACT.Copy)
            lane = dve if n == 3 else pool
            lane.wait(hi_made, *split_free[i])
            lo_made = tt(lane, lo, raw, as32(hi), ALU.subtract)
            posts += [hi_made, lo_made]
            yield
        raw_free[i] = tuple(posts)
        split_made[e] = tuple(posts)
        if e + 2 < E:
            load_expert(e + 2)

    for lane in (act, pool, dve, pe):
        lane.wait(*pieces, *stores_done[:3])
    run(split_weights(0))

    key, trial, kept = cb("key", [P, 1], U32), cb("trial", [P, 1], U32), cb("kept", [P, 1], U32)
    key_flip, trial_flips = cb("key_flip", [P, 1], U32), cb("trial_flips", [P, 31], U32)
    count, junk_cmp = cb("count", [P, 1], F32), [cb(f"junk_cmp{i}", [P, M], BF16) for i in range(2)]
    count_bank = bank[0]

    def count_at_least(threshold, n):
        return dve.do(lambda e: e.tensor_scalar(junk_cmp[n % 2][:], logits_by_chunk[:], threshold, None,
                                                ALU.is_ge, ALU.add, accum_out=count[:]))

    def keep_bit(n, bit, counted):
        pe.wait(counted)
        dve.wait(dve.latest())
        summed = mm(count_bank[:, 0:1], same_expert[:], count[:], True, True, post=True)
        dve.wait(summed)
        dve.wait(ts(dve, kept[:], count_bank[:, 0:1], float(CAP), float(bit), ALU.is_ge, ALU.mult))

    dve.wait(consts_loaded)
    pe.wait(consts_loaded)
    dve.wait(dve.do(lambda e: e.memset(trial[:], 0)))
    keep_bit(0, 1 << 31, count_at_least(trial[:].bitcast(F32), 0))
    copy_key = ts(dve, key[:], kept[:], 0, None, ALU.bitwise_or)
    dve.wait(ts(dve, key_flip[:].bitcast(I32), kept[:].bitcast(I32), 31, -1, ALU.arith_shift_right,
                ALU.bitwise_xor))
    dve.wait(ts(dve, key_flip[:], key_flip[:], 1 << 31, None, ALU.bitwise_or))
    dve.wait(ts(dve, trial_flips[:], search_bits[:], key_flip[:, 0:1], None, ALU.bitwise_xor))
    dve.wait(dve.do(lambda e: e.memset(kept[:], 0)))
    for n in range(31):
        dve.wait(ts(dve, trial[:], key[:], kept[:, 0:1], trial_flips[:, n:n + 1], ALU.bitwise_or, ALU.bitwise_xor))
        counted = count_at_least(trial[:].bitcast(F32), n + 1)
        ts(dve, key[:], key[:], kept[:, 0:1], None, ALU.bitwise_or)
        keep_bit(n, 1 << (30 - n), counted)
    dve.wait(ts(dve, trial[:], key[:], kept[:, 0:1], key_flip[:, 0:1], ALU.bitwise_or, ALU.bitwise_xor))

    wide = cb("wide", [E, P], F32)
    limit = cb("limit", [P, E], F32)
    widened = copy(dve, wide[:], trial[0:E, 0:1].bitcast(F32).broadcast_to([E, P]))
    pe.wait(widened)
    limits_flipped = flip(bank[1][:, 0:E], wide[:], ident[0:E, 0:E], post=True)
    before_made = copy(dve, before[:], before_f[:])
    ones_made = dve.do(lambda e: e.memset(all_ones[:], 1.0))
    tile_ids_made = copy(dve, tile_ids[:], tile_ids_f[:])
    dve.wait(limits_flipped)
    dve.wait(copy(dve, limit[:], bank[1][:, 0:E]))

    by_expert = [P, E, NT]
    view = logits[:].rearrange("p j e -> p e j")
    above, equal = cb("above", by_expert, BF16), cb("equal", by_expert, BF16)
    running, earlier = cb("running", [P, E * NT], BF16), cb("earlier", [P, E * NT], BF16)
    flat = lambda t: t[:].rearrange("p e j -> p (e j)")
    order = {}
    for n, (taken, op) in enumerate(((above, ALU.is_gt), (equal, ALU.is_equal))):
        dve.wait(tt(dve, taken[:], view, limit[:].unsqueeze(2).broadcast_to(by_expert), op))
        if n:
            dve.wait(order[0])
            pe_read = order[0]
        dve.wait(dve.do(lambda e, t=taken: e.tensor_tensor_scan(running[:], scan_keep[:], flat(t), 0.0,
                                                               ALU.mult, ALU.add)))
        tiles_before = tt(dve, earlier[:], running[:], flat(taken), ALU.subtract)
        pe.wait(tiles_before, before_made, ones_made)
        mm(bank[2 + n][:], before[:], flat(taken), True, False)
        order[n] = mm(bank[2 + n][:], all_ones[:], earlier[:], False, True, post=True)
        if n == 0:
            totals = running[:].rearrange("p (e j) -> p e j", j=NT)[:, :, NT - 1]
            order[0] = mm(bank[4][:, 0:E], all_ones[:], totals, True, True, post=True)
    n_above, slot, part = cb("n_above", [P, E], F32), cb("slot", by_expert, F32), cb("part", by_expert, F32)
    slot_int, slot_bits = cb("slot_int", by_expert, I32), cb("slot_bits", by_expert, I32)
    rank = lambda n: bank[n][:].rearrange("p (e j) -> p e j", j=NT)
    dve.wait(order[0])
    dve.wait(copy(dve, n_above[:], bank[4][:, 0:E]), order[1])
    dve.wait(tt(dve, part[:], rank(3), n_above[:].unsqueeze(2).broadcast_to(by_expert), ALU.add))
    dve.wait(tt(dve, part[:], part[:], equal[:], ALU.mult))
    dve.wait(tt(dve, slot[:], rank(2), above[:], ALU.mult))
    dve.wait(tt(dve, slot[:], slot[:], part[:], ALU.add))
    dve.wait(tt(dve, part[:], above[:], equal[:], ALU.add))
    dve.wait(stt(slot[:], part[:], -float(NO_SLOT), slot[:], ALU.mult, ALU.add))
    dve.wait(ts(dve, slot_int[:], slot[:], float(NO_SLOT), None, ALU.add))
    dve.wait(ts(dve, slot_bits[:], slot_int[:], 4, None, ALU.logical_shift_right))
    dve.wait(copy(dve, slot_hi[:], slot_bits[:]))
    dve.wait(ts(dve, slot_bits[:], slot_int[:], 15, None, ALU.bitwise_and))
    slots_made = copy(dve, slot_lo[:], slot_bits[:])
    dve.wait(slots_made)

    list_bank, list_bank_free = bank[0], [()]
    xe_bank, xe_bank_free = bank[1], [()]
    hidden_banks = Ring(bank[2:5])
    y_banks, y_bank_free = bank[5:7], [(), ()]
    hot_free = [()]
    index_made, gather_done, xe_made = {}, {}, {}
    index_free, gathered_free, xe_free = [()] * LISTS, [()] * GATHERS, [(), ()]
    gather_sem = [semaphore(f"gathered{i}") for i in range(GATHERS)]
    scatter_sem = [semaphore(f"scattered{i}") for i in range(2)]
    rows_at = (rows_stored[0],)

    def list_tokens(e):
        hot = [P, NT, 16]
        iota = iota16[:].unsqueeze(1).broadcast_to(hot)
        dve.wait(*hot_free[0])
        tt(dve, hot_hi[:], iota, slot_hi[:, e, :].unsqueeze(2).broadcast_to(hot), ALU.is_equal)
        dve.wait(tt(dve, hot_lo[:], iota, slot_lo[:, e, :].unsqueeze(2).broadcast_to(hot), ALU.is_equal))
        ts(dve, hot_ids[:, :, 0, :], hot_lo[:], token_in_tile[:, 0:1], None, ALU.mult)
        ids_made = tt(dve, hot_ids[:, :, 1, :], hot_lo[:], tile_ids[:].unsqueeze(2).broadcast_to(hot), ALU.mult)
        yield from idle(3)
        pe.wait(ids_made, *list_bank_free[0])
        for j in range(NT):
            listed = mm(list_bank[0:16, 0:32], hot_hi[:, j, :], hot_ids[:, j].rearrange("p a b -> p (a b)"),
                        j == 0, j == NT - 1, post=j == NT - 1)
        hot_free[0] = (listed,)
        yield
        dve.wait(listed)
        dve.wait(copy(dve, list_parts[:], list_bank[0:16, 0:32]))
        made = stt(list16[:], list_parts[:, 16:32], float(P), list_parts[:, 0:16], ALU.mult, ALU.add)
        yield from idle(2)
        pe.wait(made)
        spread = mm(list_bank[:, 64:80], expand16[:], list16[:], True, True, post=True)
        dve.wait(spread)
        dve.wait(tt(dve, picked[:], pick[:], list_bank[:, 64:80].unsqueeze(1).broadcast_to([P, 2, 16]), ALU.mult))
        list_bank_free[0] = (dve.latest(),)
        dve.wait(reduce(list_f[:], picked[:], ALU.add))
        dve.wait(*index_free[e % LISTS])
        index_made[e] = copy(dve, token_index[e % LISTS][:], list_f[:])
        yield

    def gather(e):
        i = e % GATHERS
        pool.wait(index_made[e], *gathered_free[i], *rows_at)
        for c in range(2):
            gather_done[e] = pool.do(
                lambda g, c=c: g.indirect_dma_start(gathered[i][:, c, :], None, rows_dram,
                                                    bass.IndirectOffsetOnAxis(ap=token_index[e % LISTS][:, c:c + 1], axis=0)),
                gather_sem[i], 16)
        yield

    def transpose_tokens(e):
        i = e % 2
        pe.wait(gather_done[e], *xe_bank_free[0])
        for half in range(2):
            for c in range(2):
                flipped = flip(xe_bank[:, half * CAP + c * P:half * CAP + (c + 1) * P],
                               gathered[e % GATHERS][:, c, half * P:(half + 1) * P], ident[:], post=half and c)
        act.wait(flipped, *xe_free[i])
        flat_hi = xe_hi[i][:].rearrange("p a n -> p (a n)")
        hi = func(flat_hi, xe_bank[:], ACT.Copy)
        dve.wait(hi, *xe_free[i])
        lo = tt(dve, xe_lo[i][:].rearrange("p a n -> p (a n)"), xe_bank[:], as32(flat_hi), ALU.subtract)
        xe_bank_free[0] = (lo,)
        xe_made[e] = (hi, lo)
        yield

    h_free = [()] * FT
    h_ring = Ring(h_full)
    y_free = [(), ()]
    scattered = [()]

    def run_expert(e, between):
        i = e % 2
        pe.wait(*xe_made[e], *split_made[e])
        h_made = []
        for f in range(FT):
            at, out = hidden_banks.take(pe)
            cols = slice(f * P, (f + 1) * P)
            n = 0
            for half in range(2):
                for w, x in ((w1_hi, xe_hi), (w1_lo, xe_hi), (w1_hi, xe_lo)):
                    done = mm(out[:, 0:CAP], w[i][:, half, cols], x[i][:, half, :], n == 0, n == 5, post=n == 5)
                    n += 1
            hat, full = h_ring.take(act)
            act.wait(done)
            activated = func(full[:], out[:, 0:CAP], ACT.Gelu, bias=b1_cols[:, e, f:f + 1])
            hidden_banks.give(at, activated)
            dve.wait(activated, *h_free[f])
            hi = copy(dve, h_hi[:, f, :], full[:])
            dve.wait(hi)
            lo = tt(dve, h_lo[:, f, :], full[:], as32(h_hi[:, f, :]), ALU.subtract)
            h_ring.give(hat, lo)
            h_made.append(lo)
            between()
        xe_free[i] = (done,)
        for c in range(2):
            pe.wait(*y_bank_free[c])
            tokens = slice(c * P, (c + 1) * P)
            n = 0
            for f in range(FT):
                pe.wait(h_made[f])
                for h, w in ((h_hi, w2_hi), (h_lo, w2_hi), (h_hi, w2_lo)):
                    done = mm(y_banks[c][:, 0:D], h[:, f, tokens], w[i][:, f, :], n == 0, n == 3 * FT - 1,
                              post=n == 3 * FT - 1)
                    n += 1
                if c:
                    between()
            dve.wait(done, b2_here[e], *y_free[i])
            biased = tt(dve, y_out[i][:, c, 0:D], y_banks[c][:, 0:D], b2_rows[e % 4][:], ALU.add)
            y_bank_free[c] = (biased,)
            dve.wait(biased)
            gate = gathered[e % GATHERS][:, c, D + e:D + e + 1]
            ts(dve, y_out[i][:, c, 0:D], y_out[i][:, c, 0:D], gate, None, ALU.mult)
            gated = copy(dve, y_out[i][:, c, D:ACC], gate)
        for f in range(FT):
            h_free[f] = (done,)
        split_free[i] = (done,)
        b2_free[e % 4] = (biased,)
        gathered_free[e % GATHERS] = (gated,)

        def scatter():
            pool.wait(gated, acc_cleared, *scattered[0])
            for c in range(2):
                landed = pool.do(
                    lambda g, c=c: g.indirect_dma_start(acc_dram,
                                                        bass.IndirectOffsetOnAxis(ap=token_index[e % LISTS][:, c:c + 1], axis=0),
                                                        y_out[i][:, c, :], None, compute_op=ALU.add),
                    scatter_sem[i], 16)
            scattered[0] = (landed,)
            y_free[i] = index_free[e % LISTS] = (landed,)

        scatter_next[0] = scatter

    scatter_next = [lambda: None]

    for e in range(3):
        run(list_tokens(e))
        if e < 2:
            run(gather(e))
    run(transpose_tokens(0))
    choice.close()
    x2_back, x2_back_sem = sb("x2_back", [P, NT, D], F32), semaphore("x2_loaded")
    POINTS = FT + FT
    for e in range(E):
        lists = paced(list_tokens(e + 3) if e + 3 < E else idle(0), 3 + 2 + 1 + 1, POINTS)
        splits = paced(split_weights(e + 1) if e + 1 < E else idle(0), 4, POINTS - 4)
        state = {"point": 0}

        def between():
            state["point"] += 1
            if state["point"] == 2:
                scatter_next[0]()
                if e + 2 < E:
                    run(gather(e + 2))
            splits()
            lists()
            if state["point"] == POINTS - 4 and e + 1 < E:
                run(transpose_tokens(e + 1))

        run_expert(e, between)
        if e == 1:
            sync.wait(slots_made, pe.latest(), dve.latest())
            x2_loaded = load(x2_back[:], x2_dram.rearrange("(j p) d -> p j d", p=P), x2_back_sem)

    scatter_next[0]()

    acc_in = [sb(f"acc_in{i}", [P, 4, ACC], F32) for i in range(2)]
    inv_gate = [sb(f"inv_gate{i}", [P, 2, 4], F32) for i in range(2)]
    acc_sem = [semaphore(f"acc_loaded{i}") for i in range(2)]
    out_sem = semaphore("out_stored")
    acc_free = [(), ()]
    out_view = io["out"].rearrange("b (j p) d -> p (b j) d", p=P)
    sync.wait(*scattered[0])
    for g in range(NT // 4):
        i = g % 2
        tiles = slice(4 * g, 4 * g + 4)
        sync.wait(*acc_free[i])
        here = load(acc_in[i][:], acc_view[:, tiles, :], acc_sem[i])
        dve.wait(here, x2_loaded)
        sums = acc_in[i][:, :, D]
        dve.wait(ts(dve, inv_gate[i][:, 0, :], sums, 0.0, None, ALU.is_le))
        dve.wait(tt(dve, inv_gate[i][:, 0, :], inv_gate[i][:, 0, :], sums, ALU.add))
        dve.wait(recip(inv_gate[i][:, 1, :], inv_gate[i][:, 0, :]))
        for j in range(4):
            last = stt(x2_back[:, 4 * g + j, :], acc_in[i][:, j, 0:D], inv_gate[i][:, 1, j:j + 1],
                       x2_back[:, 4 * g + j, :], ALU.mult, ALU.add)
        acc_free[i] = (last,)
        act.wait(last)
        stored = act.do(lambda e, o=out_view[:, tiles, :], a=x2_back[:, tiles, :]: e.dma_start(o, a), out_sem, 16)
    act.wait(stored)

    with nc.Block() as block:
        block.sync(lambda e: sync.write(e))
        block.gpsimd(lambda e: pool.write(e))
        block.scalar(lambda e: act.write(e))
        block.vector(lambda e: dve.write(e))
        block.tensor(lambda e: pe.write(e))


def _operands(i):
    def cols(v, width):
        return np.ascontiguousarray(v.reshape(2, width).T)

    f32 = np.float32
    part, eye = np.arange(P), np.eye(P, dtype=f32)
    ops = {
        "x": i["x"], "ctx": i["ctx_768"], "mask": i["mask_BxS2_bk0"],
        "lnl_g": cols(i["L0_xattn_ln_l_g"], DHF), "lnl_b": cols(i["L0_xattn_ln_l_b"], DHF),
        "lnx_g": cols(i["L0_xattn_ln_x_g"], CHF), "lnx_b": cols(i["L0_xattn_ln_x_b"], CHF),
        "qn_g": i["L0_xattn_qn_g"][:, None], "kn_g": i["L0_xattn_kn_g"][:, None],
        "w_lat": np.concatenate([i["L0_xattn_Wq"].T, i["L0_xattn_Wlkv"].T], axis=1),
        "w_ctx": i["L0_xattn_Wkv"].T, "wo": i["L0_xattn_Wo"].T, "bo": i["L0_xattn_bo"],
        "norm_weight": i["L0_ffn_norm_weight"],
        "router_w": i["L0_ffn_router_weight"].T.reshape(2, P, E).transpose(1, 0, 2),
        "router_b": i["L0_ffn_router_bias"][:, None],
        "fc1": i["L0_ffn_fc1_weight"].transpose(0, 2, 1).reshape(E, 2, P, F).transpose(0, 2, 1, 3),
        "fc1_bias": i["L0_ffn_fc1_bias"].reshape(E, FT, P).transpose(2, 0, 1),
        "fc2": i["L0_ffn_fc2_weight"].transpose(0, 2, 1).reshape(E, FT, P, D).transpose(0, 2, 1, 3),
        "fc2_bias": i["L0_ffn_fc2_bias"],
        "ident": eye, "neg_ident": -eye,
        "same_expert": (part[:, None] % E == part[None, :] % E).astype(f32),
        "search_bits": np.broadcast_to(np.uint32(1) << np.arange(30, -1, -1, dtype=np.uint32), (P, 31)),
        "before": (part[:, None] < part[None, :]).astype(f32),
        "scan_keep": np.broadcast_to((np.arange(E * NT) % NT != 0).astype(f32), (P, E * NT)),
        "iota16": np.broadcast_to(np.arange(16, dtype=f32), (P, 16)),
        "tile_ids": np.broadcast_to(np.arange(NT, dtype=f32), (P, NT)),
        "token_in_tile": part[:, None].astype(f32),
        "expand16": (np.arange(16)[:, None] == part[None, :] // 8).astype(f32),
        "pick": (np.arange(16)[None, None, :]
                 == 2 * (part % 8)[:, None, None] + np.arange(2)[None, :, None]).astype(f32),
    }
    return {name: np.ascontiguousarray(a) for name, a in ops.items()}


def kernel(**inputs):
    import concourse.bacc as bacc
    from concourse.bass_utils import run_bass_kernel_spmd

    nc = bacc.Bacc("TRN2", target_bir_lowering=False, num_devices=1)
    operands = _operands({name: np.asarray(a) for name, a in inputs.items()})
    io = {name: nc.dram_tensor(f"in_{name}", a.shape, mybir.dt.from_np(a.dtype), kind="ExternalInput").ap()
          for name, a in operands.items()}
    io["out"] = nc.dram_tensor("out_x", (B, M, D), F32, kind="ExternalOutput").ap()
    build(nc, io)
    result = run_bass_kernel_spmd(nc, [{f"in_{name}": a for name, a in operands.items()}], core_ids=[0])
    return result.results[0]["out_x"]
```

```python
from contextlib import ExitStack

import numpy as np

import concourse.bass as bass
from concourse import mybir

F32, F32R, BF16 = mybir.dt.float32, mybir.dt.float32r, mybir.dt.bfloat16
I32, U32, U8 = mybir.dt.int32, mybir.dt.uint32, mybir.dt.uint8
ALU, ACT, AX = mybir.AluOpType, mybir.ActivationFunctionType, mybir.AxisListType.X

P = 128
B, M, D = 8, 512, 256
NC_, DC = 1024, 192
H, DH = 4, 64
INNER = H * DH
E, F = 16, 1024
T = B * M
CAP = T // E
MT, CT = M // P, NC_ // P
KT = CT + MT
NT = T // P
KEYS = KT * P
DHF, CHF = D // 2, DC // 2
FT = F // P
ROW = D + E
ACC = D + 1
LN_EPS = 1e-5
RMS_EPS = 1e-8
SCALE = DH ** -0.5
REST_SUMS, REST_WEIGHTED, REST_CONTEXT, REST_LATENTS = 2, 3, 5, 3
REST_FIRST, REST_COPY, REST_COPY2, REST_LAST = 2, 4, 5, 4
REST_SQUARES, REST_ROUTE = 1, 1
Z_POINTS, Q_POINTS = 47, 35
TRIAL_BITS = [m << low for low in range(29, 0, -2) for m in (1, 2, 3)] + [1]
N_TRIALS = len(TRIAL_BITS)
MASKED = -1e30
RSQRT_MAGIC = 0x5F3759DF
NO_SLOT = 2 * CAP


class Signal:

    def __init__(self, sem):
        self.sem, self.value = sem, 0

    def post(self, by):
        self.value += by
        return (self, self.value)


class Lane:

    def __init__(self, done):
        self.done, self.steps, self.waited = done, [], {}

    def wait(self, *posts):
        for post in posts:
            if post is None:
                continue
            signal, value = post
            if self.waited.get(signal, 0) < value:
                self.waited[signal] = value
                self.steps.append((lambda e, s=signal.sem, v=value: e.wait_ge(s, v), None, 0))

    def do(self, instruction, signal=None, by=1):
        signal = signal or self.done
        self.steps.append((instruction, signal.sem, by))
        return signal.post(by)

    def latest(self):
        return (self.done, self.done.value)

    def quiet(self, instruction):
        self.steps.append((instruction, None, 0))

    def write(self, engine):
        for instruction, sem, by in self.steps:
            made = instruction(engine)
            if sem is not None:
                made.then_inc(sem, by)


class Ring:

    def __init__(self, buffers):
        self.buffers, self.freed, self.at = buffers, [()] * len(buffers), -1
        self.held = [False] * len(buffers)

    def take(self, *lanes):
        self.at = (self.at + 1) % len(self.buffers)
        assert not self.held[self.at], "the next buffer is still in use"
        self.held[self.at] = True
        for lane in lanes:
            lane.wait(*self.freed[self.at])
        return self.at, self.buffers[self.at]

    def give(self, at, *posts):
        self.freed[at], self.held[at] = posts, False


def build(nc, io):
    with ExitStack() as everything:
        _build(nc, io, everything)


def _build(nc, io, everything):
    def semaphore(name):
        return Signal(everything.enter_context(nc.semaphore(name)))

    def sb(name, shape, dt, where=None):
        return (where or everything).enter_context(nc.sbuf_tensor(name, shape, dt))

    pe, act, dve, pool = (Lane(semaphore(n)) for n in ("pe_done", "act_done", "dve_done", "pool_done"))
    sync = Lane(None)

    bank = [everything.enter_context(nc.psum_tensor(f"bank{i}", [P, 512], F32)) for i in range(8)]

    def mm(out, lhsT, rhs, start, stop, post=False):
        f = lambda e: e.matmul(out, lhsT, rhs, start=start, stop=stop, skip_group_check=True)
        return pe.do(f) if post else pe.quiet(f)

    def flip(out, in_, ident, post=False):
        f = lambda e: e.transpose(out, in_, ident)
        return pe.do(f) if post else pe.quiet(f)

    def tt(lane, out, a, b, op):
        return lane.do(lambda e: e.tensor_tensor(out, a, b, op))

    def ts(lane, out, a, s1, s2, op0, op1=ALU.bypass):
        return lane.do(lambda e: e.tensor_scalar(out, a, s1, s2, op0, op1))

    def stt(out, a, s, b, op0, op1):
        return dve.do(lambda e: e.scalar_tensor_tensor(out, a, s, b, op0, op1))

    def copy(lane, out, a):
        return lane.do(lambda e: e.tensor_copy(out, a))

    def func(out, a, f, bias=0.0, scale=1.0):
        return act.do(lambda e: e.activation(out, a, f, bias=bias, scale=scale))

    def reduce(out, a, op):
        return dve.do(lambda e: e.tensor_reduce(out, a, AX, op))

    def recip(out, a):
        return dve.do(lambda e: e.reciprocal(out, a))

    def load(out, in_, signal, lane=sync):
        return lane.do(lambda e: e.dma_start(out, in_), signal, 16)

    def as32(ap):
        return ap.bitcast(F32)

    rows_dram = nc.dram_tensor("rows_scratch", [T, ROW], F32, kind="Internal").ap()
    x2_dram = nc.dram_tensor("x2_scratch", [T, D], F32, kind="Internal").ap()
    acc_dram = nc.dram_tensor("acc_scratch", [T, ACC], F32, kind="Internal").ap()
    logits_dram = nc.dram_tensor("logits_scratch", [T, E], F32, kind="Internal").ap()
    chunks_dram = nc.dram_tensor("chunks_scratch", [B * E, M], F32, kind="Internal").ap()

    small = semaphore("small_loaded")
    ident = sb("ident", [P, P], F32)
    neg_ident = sb("neg_ident", [P, P], F32)
    ones_col = sb("ones_col", [P, 1], F32)
    lnl_g, lnl_b = sb("lnl_g", [P, 2], F32), sb("lnl_b", [P, 2], F32)
    lnx_g, lnx_b = sb("lnx_g", [CHF, 2], F32), sb("lnx_b", [CHF, 2], F32)
    qn_col, kn_col, gqk = sb("qn_col", [P, 1], F32), sb("kn_col", [P, 1], F32), sb("gqk", [P, 1], F32)
    router_w, router_b = sb("router_w", [P, 2, E], F32), sb("router_b", [E, 1], F32)
    mask_rows = sb("mask_rows", [B * CT, P], U8)
    mask_rows_f = sb("mask_rows_f", [B * CT, P], F32)
    mask_col = sb("mask_col", [P, B * CT], F32)

    attention = ExitStack()
    ab = lambda name, shape, dt: sb(name, shape, dt, attention)
    bo_rows, nw_rows = ab("bo_rows", [P, D], F32), ab("nw_rows", [P, D], F32)
    WL = 3 * INNER
    w_lat_hi, w_lat_lo = ab("w_lat_hi", [P, 2, WL], F32R), ab("w_lat_lo", [P, 2, WL], F32R)
    w_ctx_hi, w_ctx_lo = ab("w_ctx_hi", [CHF, 2, 2 * INNER], F32R), ab("w_ctx_lo", [CHF, 2, 2 * INNER], F32R)
    wo_hi, wo_lo = ab("wo_hi", [P, H, D], F32R), ab("wo_lo", [P, H, D], F32R)
    x_in = [ab(f"x_in{i}", [P, MT, D], F32) for i in range(3)]
    c_in = [ab(f"c_in{i}", [P, 4, DC], F32) for i in range(2)]
    z_nat = ab("z_nat", [P, 4, D], F32)
    z_full = ab("z_full", [P, 2, 512], F32)
    z_hi, z_lo = ab("z_hi", [P, 2, 512], F32R), ab("z_lo", [P, 2, 512], F32R)
    squares = [ab(f"squares{i}", [P, 512], F32) for i in range(2)]
    qk_nat = ab("qk_nat", [P, MT, 2 * INNER], F32)
    kc_nat = ab("kc_nat", [P, CT, INNER], F32)
    v_nat = [ab(f"v_nat{i}", [P, KT, INNER], F32) for i in range(2)]
    qa = [ab(f"qa{i}", [P, 2, M], F32R) for i in range(2)]
    qb = [ab(f"qb{i}", [P, 2, M], F32R) for i in range(2)]
    ka = [ab(f"ka{i}", [P, 2, KEYS], F32R) for i in range(2)]
    kb = [ab(f"kb{i}", [P, 2, KEYS], F32R) for i in range(2)]
    maxima = ab("maxima", [P, 2, MT, 3], F32)
    row_max = ab("row_max", [P, 2, MT], F32)
    mask_bias8 = ab("mask_bias8", [P, NC_], U8)
    mask_bias = ab("mask_bias", [P, NC_], BF16)
    probs = [ab(f"probs{i}", [P, M], F32) for i in range(6)]
    prob_sum = [ab(f"prob_sum{i}", [P, 2, M], F32) for i in range(2)]
    inv_den = ab("inv_den", [P, H, MT], F32)
    o_stack = ab("o_stack", [P, H, M], F32R)
    router_probs = ab("router_probs", [P, MT, E], F32)
    xn_T = z_full
    stats = ab("stats", [P, KT, 6], F32)
    mean_var = ab("mean_var", [P, KT, 2], F32)
    N_HEADS = (CT + 2 * MT) * H
    norm_w, norm_y, norm_t = (ab(n, [P, N_HEADS], F32) for n in ("norm_w", "norm_y", "norm_t"))
    sq_sum = ab("sq_sum", [P, N_HEADS], F32)
    soft, batch_logits = ab("soft", [P, MT, E], F32), ab("batch_logits", [P, MT, E], F32)
    soft_s = ab("soft_s", [P, 2, MT], F32)

    x_sem = [semaphore(f"x_loaded{i}") for i in range(3)]
    c_sem = [semaphore(f"c_loaded{i}") for i in range(2)]
    mask_sem = semaphore("mask_loaded")
    lat_sem, ctx_sem, wo_sem = (semaphore(f"{n}_weights_loaded") for n in ("latent", "context", "output"))
    x_ring, c_ring = Ring(x_in), Ring(c_in)
    x_loaded, c_loaded = {}, {}

    def load_x(b):
        at, buf = x_ring.take(sync)
        x_loaded[b] = load(buf[:], io["x"][b].rearrange("(j p) d -> p j d", p=P), x_sem[at])

    def load_ctx(b, half):
        at, buf = c_ring.take(sync)
        src = io["ctx"][b].rearrange("(j p) d -> p j d", p=P)[:, 4 * half:4 * half + 4, :]
        c_loaded[b, half] = (at, load(buf[:], src, c_sem[at]))

    raw = v_nat[1][:].rearrange("p j d -> p (j d)")
    raw_lat = raw[:, 0:2 * WL].rearrange("p (a b) -> p a b", a=2)
    raw_ctx = raw[0:CHF, 2 * WL:2 * WL + 4 * INNER].rearrange("p (a b) -> p a b", a=2)
    raw_wo = [probs[i][:].rearrange("p (a b) -> p a b", a=2) for i in range(2)]
    load_ctx(0, 0)
    load_ctx(0, 1)
    load_x(0)
    ctx_loaded = load(raw_ctx, io["w_ctx"].rearrange("(a p) n -> p a n", p=CHF), ctx_sem)
    lat_loaded = load(raw_lat, io["w_lat"].rearrange("(a p) n -> p a n", p=P), lat_sem)
    for name, tile in (("ident", ident), ("lnx_g", lnx_g), ("lnx_b", lnx_b), ("lnl_g", lnl_g), ("lnl_b", lnl_b),
                       ("neg_ident", neg_ident), ("router_w", router_w), ("router_b", router_b)):
        load(tile[:], io[name], small, act)
    load(mask_rows[:], io["mask"].rearrange("b (j p) -> (b j) p", p=P), small, act)
    for half in (slice(0, DH), slice(DH, P)):
        load(qn_col[half, :], io["qn_g"], small, act)
        load(kn_col[half, :], io["kn_g"], small, act)
    load(bo_rows[:], io["bo"].partition_broadcast(P), small)
    small_loaded = load(nw_rows[:], io["norm_weight"].partition_broadcast(P), small)
    for half in (slice(0, DH), slice(DH, P)):
        for i in range(2):
            wo_loaded = load(raw_wo[i][half], io["wo"].rearrange("(h d) n -> d h n", d=DH)[:, 2 * i:2 * i + 2, :],
                             wo_sem)

    pool.do(lambda e: e.memset(ones_col[:], 1.0))
    zeros = squares[1][:, 0:ACC]
    zeros_set = pool.do(lambda e: e.memset(zeros, 0.0))
    act.wait(ctx_loaded)
    ctx_hi_made = func(w_ctx_hi[:], raw_ctx, ACT.Copy)
    act.wait(lat_loaded)
    lat_hi_made = func(w_lat_hi[:], raw_lat, ACT.Copy)
    pool.wait(ctx_loaded, ctx_hi_made)
    ctx_lo_made = tt(pool, w_ctx_lo[:], raw_ctx, as32(w_ctx_hi[:]), ALU.subtract)

    def split_latent_weights():
        pool.wait(lat_loaded, lat_hi_made)
        return tt(pool, w_lat_lo[:], raw_lat, as32(w_lat_hi[:]), ALU.subtract)

    def set_constant_rows():
        for h in range(H):
            other = slice(DH, P) if h % 2 == 0 else slice(0, DH)
            cleared = dve.do(lambda e, o=wo_lo[other, h, :]: e.memset(as32(o), 0.0))
        for i in range(2):
            for hh, half in enumerate((slice(DH, P), slice(0, DH))):
                ones_set = dve.do(lambda e, o=kb[i][half, hh, :]: e.memset(as32(o), 1.0))
        return cleared, ones_set

    def split_output_weights():
        act.wait(wo_loaded)
        for i in range(2):
            wo_hi_made = func(wo_hi[:, 2 * i:2 * i + 2, :], raw_wo[i], ACT.Copy)
        dve.wait(wo_hi_made, wo_lo_cleared)
        for h in range(H):
            own = slice(0, DH) if h % 2 == 0 else slice(DH, P)
            wo_lo_made = tt(dve, wo_lo[own, h, :], raw_wo[h // 2][own, h % 2, :], as32(wo_hi[own, h, :]),
                            ALU.subtract)
        prob_ring.freed[0] = prob_ring.freed[1] = (wo_hi_made, wo_lo_made)
        return wo_lo_made

    def set_up_columns():
        dve.wait(small_loaded)
        mask_f_made = ts(dve, mask_rows_f[:], mask_rows[:], -1.0, -MASKED, ALU.add, ALU.mult)
        gqk_made = ts(dve, gqk[:], qn_col[:], kn_col[:, 0:1], SCALE, ALU.mult, ALU.mult)
        at, out = misc.take(pe)
        pe.wait(small_loaded, mask_f_made)
        mask_flipped = flip(out[:, 0:B * CT], mask_rows_f[:], ident[0:B * CT, 0:B * CT], post=True)
        act.wait(mask_flipped)
        mask_col_made = func(mask_col[:], out[:, 0:B * CT], ACT.Copy)
        misc.give(at, mask_col_made)
        return gqk_made

    zero_sem = semaphore("acc_cleared")
    sync.wait(zeros_set)
    acc_view = acc_dram.rearrange("(j p) d -> p j d", p=P)
    for j in range(0, NT, 8):
        acc_cleared = load(acc_view[:, j:j + 8, :], zeros.unsqueeze(1).broadcast_to([P, 8, ACC]), zero_sem)

    score_banks = Ring(bank[0:2])
    o_bank, o_bank_freed = bank[2], [()]
    max_banks = Ring(bank[3:5])
    misc = Ring(bank[5:8])

    def rsqrt(y, w, t):
        yi, wi = y.bitcast(I32), w.bitcast(I32)
        dve.wait(dve.latest())
        dve.wait(ts(dve, yi, wi, 1, None, ALU.logical_shift_right))
        dve.wait(ts(dve, yi, yi, -1.0, float(RSQRT_MAGIC), ALU.mult, ALU.add))
        for _ in range(3):
            dve.wait(tt(dve, t, y, y, ALU.mult))
            dve.wait(stt(t, t, -0.5, w, ALU.mult, ALU.mult))
            last = stt(y, t, 1.5, y, ALU.add, ALU.mult)
            yield
            dve.wait(last)
        return last

    z_free = [(), ()]
    sq_ring = Ring(squares)
    sq_ring.freed[1] = (acc_cleared,)
    nat_free = {"qk": (), "kc": ()}
    qk_normed, v_written = {}, {}
    v_free = [(), ()]

    def idle(n):
        for _ in range(n):
            yield

    def tile_stats(src, at):
        for i in range(4):
            last = dve.do(lambda e, o=stats[:, at + i, :], a=src[:, i, :]: e.bn_stats(o, a))
        dve.wait(last)
        for i in range(4):
            last = dve.do(lambda e, o=mean_var[:, at + i, :], a=stats[:, at + i, :]: e.bn_aggr(o, a))
        return last

    def centre(src, at, dst):
        for i in range(4):
            last = ts(dve, dst[:, i, :], src[:, i, :], mean_var[:, at + i, 0:1], norm_y[:, at + i:at + i + 1],
                      ALU.subtract, ALU.mult)
        return last

    def spread(start, width, src, z_made, g, b, made):
        for half in range(2):
            at, out = misc.take(pe)
            pe.wait(z_made)
            pe.wait(small_loaded)
            for i in range(4):
                flipped = flip(out[0:width, i * P:(i + 1) * P],
                               src[:, i, half * width:(half + 1) * width], ident[:], post=i == 3)
            act.wait(flipped, small_loaded, *z_full_free[half])
            full = func(z_full[0:width, half, :], out[0:width, :], ACT.Identity,
                        bias=b[0:width, half:half + 1], scale=g[0:width, half:half + 1])
            misc.give(at, full)
            act.wait(full, *z_free[0])
            hi = func(z_hi[0:width, half, :], z_full[0:width, half, :], ACT.Copy)
            pool.wait(full, hi, *z_free[0])
            lo = tt(pool, z_lo[0:width, half, :], z_full[0:width, half, :], as32(z_hi[0:width, half, :]),
                    ALU.subtract)
            z_full_free[half] = (hi, lo)
            made += [hi, lo]
            start.append(flipped)
            yield

    z_full_free = [(), ()]

    def three_passes(out, width, tile, w_hi, w_lo, cols):
        at = slice(tile * P, (tile + 1) * P)
        n = 0
        for half in range(2):
            for z, w in ((z_hi, w_hi), (z_lo, w_hi), (z_hi, w_lo)):
                last = mm(out, z[0:width, half, at], w[0:width, half, cols], n == 0, n == 5, post=n == 5)
                n += 1
        return last

    def project(b):
        x = x_in[b % 3]
        for chunk in range(2):
            dve.wait(c_loaded[b, chunk][1])
            stats_made = tile_stats(c_in[c_loaded[b, chunk][0]], 4 * chunk)
            yield
        dve.wait(x_loaded[b])
        stats_made = tile_stats(x, CT)
        yield
        dve.wait(stats_made)
        ts(dve, norm_w[:, 0:CT], mean_var[:, 0:CT, 1], 1.0, LN_EPS, ALU.mult, ALU.add)
        ts(dve, norm_w[:, CT:KT], mean_var[:, CT:KT, 1], 1.0 + LN_EPS, LN_EPS * LN_EPS, ALU.mult, ALU.add)
        dve.wait((yield from rsqrt(norm_y[:, 0:KT], norm_w[:, 0:KT], norm_t[:, 0:KT])))
        centred = [centre(c_in[c_loaded[b, chunk][0]], 4 * chunk, c_in[c_loaded[b, chunk][0]])
                   for chunk in range(2)]
        yield
        dve.wait(*z_free[1])
        z_made = centre(x, CT, z_nat)
        pending = []

        def sum_squares(left):
            while len(pending) > left:
                place, heads, sat, sq, sq_out = pending.pop(0)
                dve.wait(sq_out)
                summed = reduce(sq_sum[:, place:place + heads],
                                sq[:, 0:heads * DH].rearrange("p (h d) -> p h d", d=DH), ALU.add)
                sq_ring.give(sat, summed)

        yield
        for chunk in range(2):
            at_in = c_loaded[b, chunk][0]
            start, made = [], []
            yield from spread(start, CHF, c_in[at_in], centred[chunk], lnx_g, lnx_b, made)
            c_ring.give(at_in, start[-1])
            if b + 1 < B:
                load_ctx(b + 1, chunk)
            if chunk == 0:
                pool.wait(z_made, small_loaded)
                residual_made[b] = tt(pool, x[:], x[:], bo_rows[:].unsqueeze(1).broadcast_to([P, MT, D]), ALU.add)
            yield from idle(REST_CONTEXT)
            assert b == 0 or (b - 1, 1) in prepared, "q and k of the last batch are still needed"
            for i in range(4):
                tile = 4 * chunk + i
                at, out = misc.take(pe)
                pe.wait(ctx_lo_made, *made)
                kv_done = three_passes(out[:], CHF, i, w_ctx_hi, w_ctx_lo, slice(0, 2 * INNER))
                act.wait(kv_done, *nat_free["kc"], *v_free[b % 2])
                func(kc_nat[:, tile, :], out[:, 0:INNER], ACT.Copy)
                sat, sq = sq_ring.take(act)
                sq_out = func(sq[:, 0:INNER], out[:, 0:INNER], ACT.Square)
                v_out = func(v_nat[b % 2][:, tile, :], out[:, INNER:2 * INNER], ACT.Copy)
                misc.give(at, v_out)
                sum_squares(0)
                pending.append((tile * H, H, sat, sq, sq_out))
                yield
            z_free[0] = (kv_done,)
        start, made = [], []
        yield from spread(start, DHF, z_nat, z_made, lnl_g, lnl_b, made)
        z_free[1] = (start[-1],)
        yield from idle(REST_LATENTS)
        for i in range(MT):
            at, out = misc.take(pe)
            pe.wait(lat_lo_made, *made)
            qk_done = three_passes(out[:], DHF, i, w_lat_hi, w_lat_lo, slice(0, 2 * INNER))
            act.wait(qk_done, *nat_free["qk"])
            func(qk_nat[:, i, :], out[:], ACT.Copy)
            sat, sq = sq_ring.take(act)
            sq_out = func(sq[:], out[:], ACT.Square)
            misc.give(at, sq_out)
            sum_squares(0)
            pending.append(((CT + 2 * i) * H, 2 * H, sat, sq, sq_out))
            yield
            at, out = misc.take(pe)
            v_done = three_passes(out[:, 0:INNER], DHF, i, w_lat_hi, w_lat_lo, slice(2 * INNER, WL))
            act.wait(v_done, *v_free[b % 2])
            v_out = func(v_nat[b % 2][:, CT + i, :], out[:, 0:INNER], ACT.Copy)
            misc.give(at, v_out)
            if i % 2:
                yield
        z_free[0] = (v_done,)
        v_written[b] = v_out
        yield from idle(REST_SQUARES)
        sum_squares(0)
        dve.wait(dve.latest())
        dve.wait(ts(dve, norm_w[:], sq_sum[:], 1.0 / DH, RMS_EPS ** 2, ALU.mult, ALU.max))
        dve.wait((yield from rsqrt(norm_y[:], norm_w[:], norm_t[:])), v_out)
        inverse = lambda first, tiles: (norm_y[:, first * H:(first + tiles) * H].unsqueeze(2)
                                        .broadcast_to([P, tiles * H, DH]))
        for i in range(0, MT, 2):
            view = qk_nat[:, i:i + 2, :].rearrange("p j (h d) -> p (j h) d", d=DH)
            normed = tt(dve, view, view, inverse(CT + 2 * i, 4), ALU.mult)
        qk_normed[b] = normed
        yield
        for i in range(0, CT, 4):
            view = kc_nat[:, i:i + 4, :].rearrange("p j (h d) -> p (j h) d", d=DH)
            normed = tt(dve, view, view, inverse(i, 4), ALU.mult)
            kc_normed[b, i // 4] = normed
            yield

    residual_made, kc_normed = {}, {}
    unit_free = [(), ()]
    prepared, shift_made = {}, {}
    mask_free = [()]

    def prepare(b, pair):
        u = (2 * b + pair) % 2
        if pair == 0:
            load_mask(b)
        both = slice(2 * pair * DH, 2 * (pair + 1) * DH)
        at, out = misc.take(pe)
        pe.wait(qk_normed[b])
        for j in range(MT):
            flipped = flip(out[:, j * P:(j + 1) * P], qk_nat[:, j, both], ident[:], post=j == MT - 1)
        q_hi, q_lo = [], []
        for hh, (hi, lo) in enumerate(ROWS):
            act.wait(flipped, gqk_made, *unit_free[u])
            q_hi.append(func(qb[u][hi, hh, :], out[hi, :], ACT.Identity, scale=gqk[hi, 0:1]))
            dve.wait(q_hi[hh], *unit_free[u])
            q_lo.append(stt(qa[u][lo, hh, :], out[hi, :], gqk[hi, 0:1], as32(qb[u][hi, hh, :]),
                            ALU.mult, ALU.subtract))
        misc.give(at, *q_lo)
        sync.wait(*q_hi, *unit_free[u])
        for hh, (hi, lo) in enumerate(ROWS):
            load(as32(qa[u][hi, hh, :]), as32(qb[u][hi, hh, :]), copied[u])
        yield
        for g in range(3):
            at, out = misc.take(pe)
            pe.wait(kc_normed[b, min(g, 1)])
            for j in range(4):
                tile = 4 * g + j
                k = (kc_nat[:, tile, both] if tile < CT else
                     qk_nat[:, tile - CT, INNER + both.start:INNER + both.stop])
                flipped = flip(out[:, j * P:(j + 1) * P], k, ident[:], post=j == 3)
            cols = slice(512 * g, 512 * (g + 1))
            k_hi, k_lo = [], []
            for hh, (hi, lo) in enumerate(ROWS):
                act.wait(flipped, kb_ones_set, *unit_free[u])
                k_hi.append(func(ka[u][hi, hh, cols], out[hi, :], ACT.Copy))
                dve.wait(k_hi[hh], *unit_free[u])
                k_lo.append(tt(dve, kb[u][hi, hh, cols], out[hi, :], as32(ka[u][hi, hh, cols]), ALU.subtract))
            misc.give(at, *k_lo)
            sync.wait(*k_hi)
            for hh, (hi, lo) in enumerate(ROWS):
                k_copied = load(as32(ka[u][lo, hh, cols]), as32(ka[u][hi, hh, cols]), copied[u])
            yield
        prepared[b, pair] = (k_copied, *q_lo, *k_lo)
        if pair == 1:
            nat_free["qk"] = nat_free["kc"] = (flipped,)

    ROWS = ((slice(0, DH), slice(DH, P)), (slice(DH, P), slice(0, DH)))
    copied = [semaphore(f"copied{i}") for i in range(2)]

    def load_mask(b):
        sync.wait(*mask_free[0])
        mask_here[b] = load(mask_bias8[:], io["mask"][b].partition_broadcast(P), mask_sem)

    def make_mask(b):
        act.wait(mask_here[b], *max_free[0])
        made = func(mask_bias[:], mask_bias8[:], ACT.Copy, bias=MASKED, scale=-MASKED)
        mask_free[0] = (made,)
        return made

    max_free = [()]
    mask_made, mask_here = {}, {}

    def find_maxima(b, pair):
        u = (2 * b + pair) % 2
        if pair == 0:
            mask_made[b] = make_mask(b)
        pe.wait(*prepared[b, pair])
        rings, n_taken = (max_banks, misc) if pair == 0 else (max_banks,), 0
        for hh in range(2):
            for j in range(MT):
                for g in range(3):
                    ring = rings[n_taken % len(rings)]
                    n_taken += 1
                    at, out = ring.take(pe)
                    done = mm(out[:], qa[u][:, hh, j * P:(j + 1) * P], ka[u][:, hh, 512 * g:512 * (g + 1)],
                              True, True, post=True)
                    if g < 2:
                        dve.wait(done, mask_made[b])
                        mx = dve.do(lambda e, a=out[:], m=mask_bias[:, 512 * g:512 * (g + 1)],
                                    r=maxima[:, hh, j, g:g + 1]:
                                    e.tensor_tensor_reduce(a, a, m, 1.0, -3e38, ALU.add, ALU.max, r))
                    else:
                        dve.wait(done)
                        mx = reduce(maxima[:, hh, j, 2:3], out[:], ALU.max)
                    ring.give(at, mx)
                    yield
        max_free[0] = (mx,)
        dve.wait(mx)
        dve.wait(reduce(row_max[:], maxima[:], ALU.max))
        for hh, (hi, lo) in enumerate(ROWS):
            cols = qb[u][lo, hh, :].rearrange("p (j q) -> p j q", q=P)
            for low in (0, DH):
                m = row_max[low:low + DH, hh, :].unsqueeze(2).broadcast_to([DH, MT, DH])
                i = neg_ident[low:low + DH, low:low + DH].unsqueeze(1).broadcast_to([DH, MT, DH])
                last = tt(dve, cols[:, :, low:low + DH], i, m, ALU.mult)
        shift_made[b, pair] = last
        yield

    prob_ring = Ring(probs)
    sum_ring = Ring(prob_sum)
    summed_probs = {}
    o_written = {}
    o_free = [()]
    inv_den_free = [()]
    den_made = {}

    def attend(b, pair, between):
        u = (2 * b + pair) % 2
        pe.wait(*prepared[b, pair], shift_made[b, pair], v_written[b])
        waiting = []

        def with_v(kt, hh, pat, p, exp_done):
            if kt == 0:
                pe.wait(*o_bank_freed[0])
            pe.wait(exp_done)
            h = 2 * pair + hh
            used = mm(o_bank[hh * DH:(hh + 1) * DH, :], v_nat[b % 2][:, kt, h * DH:(h + 1) * DH], p[:],
                      kt == 0, kt == KT - 1, post=True)
            if kt == 0:
                first[hh] = (pat, p, exp_done, used)
            else:
                pool.wait(exp_done)
                if kt == 1:
                    if hh == 0:
                        taken.append(sum_ring.take(pool))
                    pool.wait(first[hh][2])
                total = taken[0][1]
                if kt == 1:
                    added = tt(pool, total[:, hh, :], first[hh][1][:], p[:], ALU.add)
                    prob_ring.give(first[hh][0], first[hh][3], added)
                else:
                    pool.wait(summed[hh])
                    added = tt(pool, total[:, hh, :], total[:, hh, :], p[:], ALU.add)
                summed[hh] = added
                prob_ring.give(pat, used, added)
            return used

        first, summed, taken = {}, {}, []
        for kt in range(KT):
            now = []
            for hh in range(2):
                at, out = score_banks.take(pe)
                keys = slice(kt * P, (kt + 1) * P)
                mm(out[:], ka[u][:, hh, keys], qa[u][:, hh, :], True, False)
                scored = mm(out[:], kb[u][:, hh, keys], qb[u][:, hh, :], False, True, post=True)
                pat, p = prob_ring.take(act)
                act.wait(scored)
                if kt < CT:
                    col = b * CT + kt
                    exp_done = func(p[:], out[:], ACT.Exp, bias=mask_col[:, col:col + 1])
                else:
                    exp_done = func(p[:], out[:], ACT.Exp)
                score_banks.give(at, exp_done)
                now.append((kt, hh, pat, p, exp_done))
                if hh == 0:
                    between()
            if kt == 0:
                last_products[0]()
            between()
            for item in waiting:
                with_v(*item)
            waiting = now
            if kt == 0:
                rest_of_o[0]()
            between()
        unit_free[u] = (scored,)

        def close():
            for item in waiting:
                used = with_v(*item)
            summed_probs[b, pair] = (summed[0], summed[1], taken[0][0])
            if pair == 1:
                v_free[b % 2] = (used,)
            act.wait(used, *o_free[0])
            a, c = 2 * pair, 2 * pair + 1
            hi_a = func(o_stack[0:DH, a, :], o_bank[0:DH, :], ACT.Copy)
            hi_c = func(o_stack[DH:P, c, :], o_bank[DH:P, :], ACT.Copy)
            rest_of_o[0] = lambda: split_rest_of_o(a, c, hi_a, hi_c)

        def split_rest_of_o(a, c, hi_a, hi_c):
            dve.wait(hi_a, hi_c, *o_free[0])
            tt(dve, o_stack[DH:P, a, :], o_bank[0:DH, :], as32(o_stack[0:DH, a, :]), ALU.subtract)
            lo_c = tt(dve, o_stack[0:DH, c, :], o_bank[DH:P, :], as32(o_stack[DH:P, c, :]), ALU.subtract)
            o_bank_freed[0] = (hi_c, lo_c)
            o_written[b, pair] = (hi_c, lo_c)

        last_products[0] = close

    last_products, rest_of_o = [lambda: None], [lambda: None]

    def denominators(b, pair):
        s0, s1, sat = summed_probs[b, pair]
        at, out = misc.take(pe)
        pe.wait(s0, s1)
        for hh in range(2):
            for j in range(MT):
                done = mm(out[:, hh * MT + j:hh * MT + j + 1], prob_sum[sat][:, hh, j * P:(j + 1) * P],
                          ones_col[:], True, True, post=True)
        sum_ring.give(sat, done)
        dve.wait(done, *inv_den_free[0])
        made = recip(inv_den[:, 2 * pair:2 * pair + 2, :], out[:, 0:2 * MT].rearrange("p (h j) -> p h j", h=2))
        misc.give(at, made)
        den_made[b, pair] = made
        yield

    rows_sem = semaphore("rows_stored")
    x2_sem = semaphore("x2_stored")
    chunk_sem = semaphore("chunk_stored")
    rows_free, x2_stored = [()], {}
    rows_stored = [None]
    logits_sem, logits_free, logits_done = semaphore("logits_stored"), [()], [()]

    def project_out(b):
        x = x_in[b % 3]
        pe.wait(*o_written[b, 0], *o_written[b, 1], wo_lo_made)
        before_sum = [(), ()]
        for j0 in range(0, MT, 2):
            for pair in range(2):
                outs = []
                for j in (j0, j0 + 1):
                    at, out = misc.take(pe)
                    outs.append((at, out, j))
                    for hh in range(2):
                        h, dst = 2 * pair + hh, out[:, hh * D:(hh + 1) * D]
                        at_q = slice(j * P, (j + 1) * P)
                        mm(dst, o_stack[:, h, at_q], wo_hi[:, h, :], True, False)
                        done = mm(dst, o_stack[:, h, at_q], wo_lo[:, h, :], False, True, post=True)
                dve.wait(done, residual_made[b], *den_made_all(b))
                added = [None, None]
                for hh in range(2):
                    h = 2 * pair + hh
                    for n, (at, out, j) in enumerate(outs):
                        dve.wait(added[n], *before_sum[n])
                        added[n] = stt(x[:, j, :], out[:, hh * D:(hh + 1) * D], inv_den[:, h, j:j + 1], x[:, j, :],
                                       ALU.mult, ALU.add)
                before_sum = [(added[0],), (added[1],)]
                for n, (at, out, j) in enumerate(outs):
                    misc.give(at, added[n])
                yield
        o_free[0] = (done,)
        inv_den_free[0] = (added[1],)
        sync.wait(added[1])
        x2_stored[b] = load(x2_dram[b * M:(b + 1) * M, :].rearrange("(j p) d -> p j d", p=P), x[:], x2_sem)
        x2_made[b] = added[1]

    x2_made = {}

    def route(b):
        x = x_in[b % 3]
        xn = z_nat[:]
        dve.wait(x2_made[b])
        stats_made = tile_stats(x, 0)
        yield
        dve.wait(stats_made)
        dve.wait(ts(dve, norm_w[:, 0:MT], mean_var[:, 0:MT, 1], 1.0 + LN_EPS, LN_EPS * LN_EPS, ALU.mult, ALU.add))
        inverse_made = yield from rsqrt(norm_y[:, 0:MT], norm_w[:, 0:MT], norm_t[:, 0:MT])
        dve.wait(inverse_made, *z_free[1], *rows_free[0])
        normed = centre(x, 0, xn)
        x_ring.give(b % 3, x2_stored[b], normed)
        if b + 3 < B:
            load_x(b + 3)
        yield
        lane = pool if b < B - 1 else dve
        lane.wait(normed)
        weighted = tt(lane, xn, xn, nw_rows[:].unsqueeze(1).broadcast_to([P, MT, D]), ALU.mult)
        yield from idle(REST_WEIGHTED)
        pe.wait(weighted)
        halves = []
        for half in range(2):
            at, out = misc.take(pe)
            for j in range(MT):
                flipped = flip(out[:, j * P:(j + 1) * P], xn[:, j, half * P:(half + 1) * P], ident[:],
                               post=j == MT - 1)
            act.wait(flipped, *z_full_free[half])
            xn_flipped = flipped
            halves.append(func(xn_T[:, half, :], out[:], ACT.Copy))
            misc.give(at, halves[-1])
        yield
        at, out = misc.take(pe)
        pe.wait(*halves)
        mm(out[0:E, :], router_w[:, 0, :], xn_T[:, 0, :], True, False)
        routed = mm(out[0:E, :], router_w[:, 1, :], xn_T[:, 1, :], False, True, post=True)
        z_full_free[0] = z_full_free[1] = (routed,)
        act.wait(routed)
        sat, sq = sq_ring.take(act)
        logits_T = sq[0:E, :]
        biased = func(logits_T, out[0:E, :], ACT.Identity, bias=router_b[:, 0:1])
        misc.give(at, biased)
        sync.wait(biased)
        chunk_stored[b] = load(chunks_dram[b * E:(b + 1) * E, :], logits_T, chunk_sem)
        yield
        at, out = misc.take(pe)
        pe.wait(biased)
        for j in range(MT):
            flipped = flip(out[:, j * E:(j + 1) * E], logits_T[:, j * P:(j + 1) * P], ident[0:E, 0:E],
                           post=j == MT - 1)
        sq_ring.give(sat, chunk_stored[b], flipped)
        mine = batch_logits[:]
        dve.wait(flipped, *logits_free[0])
        natural = copy(dve, mine, out[:, 0:MT * E].rearrange("p (j e) -> p j e", j=MT))
        misc.give(at, natural)
        sync.wait(natural)
        logits_stored = load(logits_dram[b * M:(b + 1) * M, :].rearrange("(j p) e -> p j e", p=P), mine, logits_sem)
        logits_free[0] = logits_done[0] = (logits_stored,)
        dve.wait(natural)
        dve.wait(reduce(soft_s[:, 0, :], mine, ALU.max))
        centred = tt(dve, soft[:], mine, soft_s[:, 0, :].unsqueeze(2).broadcast_to([P, MT, E]), ALU.subtract)
        yield
        act.wait(centred)
        powers = func(soft[:], soft[:], ACT.Exp)
        dve.wait(powers)
        dve.wait(reduce(soft_s[:, 0, :], soft[:], ALU.add))
        dve.wait(recip(soft_s[:, 1, :], soft_s[:, 0, :]))
        scaled = tt(dve, router_probs[:], soft[:],
                    soft_s[:, 1, :].unsqueeze(2).broadcast_to([P, MT, E]), ALU.mult)
        sync.wait(scaled, weighted)
        mine = rows_dram[b * M:(b + 1) * M, :].rearrange("(j p) d -> p j d", p=P)
        load(mine[:, :, 0:D], xn, rows_sem)
        stored = load(mine[:, :, D:ROW], router_probs[:], rows_sem)
        rows_free[0] = (stored,)
        z_free[1] = (stored, xn_flipped)
        rows_stored[0] = stored
        yield

    chunk_stored = {}

    def den_made_all(b):
        return (den_made[b, 0], den_made[b, 1])

    def run(*stages):
        for stage in stages:
            for _ in stage:
                pass

    def chain(*stages):
        for stage in stages:
            yield from stage

    def first_steps(work, n):
        for _ in range(n):
            next(work)
            yield

    def paced(work, n_steps, n_points):
        state = {"point": 0, "made": 0}

        def advance():
            state["point"] += 1
            goal = -(-n_steps * state["point"] // n_points)
            while state["made"] < goal:
                state["made"] += 1
                if next(work, "end") == "end":
                    state["made"] = n_steps * n_points
        return advance

    load_x(1)
    load_x(2)
    lat_lo_made = None
    first = project(0)
    run(first_steps(first, 10))
    lat_lo_made = split_latent_weights()
    v_free[1] = (lat_lo_made, ctx_lo_made)
    wo_lo_cleared, kb_ones_set = set_constant_rows()
    gqk_made = set_up_columns()
    run(first, prepare(0, 0))
    wo_lo_made = split_output_weights()
    run(find_maxima(0, 0))
    POINTS = 2 * 3 * KT
    MAXIMA = 2 * MT * 3 + 1
    for b in range(B):
        more = b + 1 < B
        z_work = chain(*([idle(REST_SUMS), denominators(b - 1, 1), idle(1), project_out(b - 1)] if b else []),
                       *([project(b + 1)] if more else []))
        z_step = paced(z_work, (6 + REST_SUMS if b else 0)
                       + (37 + 2 * REST_CONTEXT + REST_LATENTS + REST_SQUARES if more else 0),
                       Z_POINTS if more else 12)
        q_step = paced(chain(idle(REST_FIRST), prepare(b, 1), idle(REST_COPY), find_maxima(b, 1)),
                       REST_FIRST + 4 + REST_COPY + MAXIMA, Q_POINTS)
        q_work = chain(denominators(b, 0), *([prepare(b + 1, 0), idle(REST_COPY2), find_maxima(b + 1, 0)] if more else []))
        next_step = paced(q_work, 1 + (4 + REST_COPY2 + MAXIMA if more else 0), POINTS - Z_POINTS - REST_LAST)
        r_work = chain(idle(REST_ROUTE), *([route(b - 1)] if b else []))
        r_step = paced(r_work, REST_ROUTE + 11 + REST_WEIGHTED, POINTS - Z_POINTS - 1)
        z_end = Z_POINTS if more else 12
        state = {"point": 0}

        def between():
            state["point"] += 1
            if state["point"] < z_end:
                z_step()
            elif state["point"] == z_end:
                run(z_work)
            else:
                if more or state["point"] > 3 * KT + 2:
                    next_step()
                r_step()
            if state["point"] <= 3 * KT:
                q_step()

        for pair in range(2):
            attend(b, pair, between)
        run(z_work, q_work, r_work)
    last_products[0]()
    rest_of_o[0]()
    run(denominators(B - 1, 1), project_out(B - 1), route(B - 1))
    pieces = (pe.latest(), act.latest(), dve.latest(), pool.latest())
    stores_done = (*logits_done[0], x2_stored[B - 1], rows_stored[0], chunk_stored[B - 1], acc_cleared)
    attention.close()
    choice = ExitStack()
    cb = lambda name, shape, dt: sb(name, shape, dt, choice)

    GATHERS, LISTS = 3, 5
    w1_raw = [sb(f"w1_raw{i}", [P, 2, F], F32) for i in range(2)]
    w2_raw = [sb(f"w2_raw{i}", [P, FT, D], F32) for i in range(2)]
    w1_hi, w1_lo = ([sb(f"w1_{n}{i}", [P, 2, F], F32R) for i in range(2)] for n in ("hi", "lo"))
    w2_hi, w2_lo = ([sb(f"w2_{n}{i}", [P, FT, D], F32R) for i in range(2)] for n in ("hi", "lo"))
    b1_cols = sb("b1_cols", [P, E, FT], F32)
    b2_rows = [sb(f"b2_rows{i}", [P, D], F32) for i in range(4)]
    gathered = [sb(f"gathered{i}", [P, 2, ROW], F32) for i in range(GATHERS)]
    xe_hi, xe_lo = ([sb(f"xe_{n}{i}", [P, 2, CAP], F32R) for i in range(2)] for n in ("hi", "lo"))
    h_full = [sb(f"h_full{i}", [P, CAP], F32) for i in range(4)]
    h_hi, h_lo = sb("h_hi", [P, FT, CAP], F32R), sb("h_lo", [P, FT, CAP], F32R)
    y_out = [sb(f"y_out{i}", [P, 2, ACC], F32) for i in range(2)]
    token_index = [sb(f"token_index{i}", [P, 2], U32) for i in range(LISTS)]
    slot_hi, slot_lo = sb("slot_hi", [P, E, NT], F32), sb("slot_lo", [P, E, NT], F32)
    iota16, tile_ids = sb("iota16", [P, 16], F32), sb("tile_ids", [P, NT], BF16)
    token_in_tile = sb("token_in_tile", [P, 1], F32)
    expand16, pick = sb("expand16", [16, P], F32), sb("pick", [P, 2, 16], F32)
    hot_hi, hot_lo = sb("hot_hi", [P, NT, 16], BF16), sb("hot_lo", [P, NT, 16], BF16)
    hot_ids = sb("hot_ids", [P, NT, 2, 16], BF16)
    list_parts, list16 = sb("list_parts", [16, 32], F32), sb("list16", [16, 16], F32)
    picked, list_f = sb("picked", [P, 2, 16], F32), sb("list_f", [P, 2], F32)

    for lane in (sync, act):
        lane.wait(*pieces, *stores_done)
    search_sem, consts_sem = semaphore("search_operands_loaded"), semaphore("choice_consts_loaded")
    logits_by_chunk = cb("logits_by_chunk", [P, M], F32)
    logits = cb("logits", [P, NT, E], F32)
    load(logits_by_chunk[:], chunks_dram, search_sem)
    same_expert, search_bits = cb("same_expert", [P, P], F32), cb("search_bits", [P, N_TRIALS], U32)
    before_f, scan_keep = cb("before_f", [P, P], F32), cb("scan_keep", [P, T // P * E], F32)
    before, all_ones = cb("before", [P, P], BF16), cb("all_ones", [P, P], BF16)
    load(same_expert[:], io["same_expert"], search_sem)
    search_loaded = load(search_bits[:], io["search_bits"], search_sem)
    for tile, name in ((before_f, "before"),
                       (scan_keep, "scan_keep"), (iota16, "iota16"), (token_in_tile, "token_in_tile"),
                       (expand16, "expand16"), (pick, "pick"), (b1_cols, "fc1_bias")):
        load(tile[:], io[name], consts_sem, act)
    tile_ids_f = cb("tile_ids_f", [P, NT], F32)
    load(logits[:], logits_dram.rearrange("(j p) e -> p j e", p=P), consts_sem, act)
    consts_loaded = load(tile_ids_f[:], io["tile_ids"], consts_sem, act)

    w_sem = [semaphore(f"expert_weights_loaded{i}") for i in range(2)]
    raw_free, weights_here = [(), ()], {}
    b2_sem = [semaphore(f"expert_bias_loaded{i}") for i in range(4)]
    b2_free, b2_here = [()] * 4, {}

    def load_expert(e):
        i = e % 2
        sync.wait(*raw_free[i], *b2_free[e % 4])
        load(w1_raw[i][:], io["fc1"][e], w_sem[i])
        weights_here[e] = load(w2_raw[i][:], io["fc2"][e], w_sem[i])
        b2_here[e] = load(b2_rows[e % 4][:], io["fc2_bias"][e].partition_broadcast(P), b2_sem[e % 4])

    load_expert(0)
    load_expert(1)

    split_free = [(), ()]
    split_made = {}

    def split_weights(e):
        i = e % 2
        posts = []
        halves = [(w1_raw[i][:, a, :], w1_hi[i][:, a, :], w1_lo[i][:, a, :]) for a in range(2)]
        halves += [tuple(w[:, 4 * a:4 * a + 4, :] for w in (w2_raw[i], w2_hi[i], w2_lo[i])) for a in range(2)]
        for n, (raw, hi, lo) in enumerate(halves):
            act.wait(weights_here[e], *split_free[i])
            hi_made = func(hi, raw, ACT.Copy)
            lane = dve if n == 3 and e else pool
            lane.wait(hi_made, *split_free[i])
            lo_made = tt(lane, lo, raw, as32(hi), ALU.subtract)
            posts += [hi_made, lo_made]
            yield
        raw_free[i] = tuple(posts)
        split_made[e] = (posts[:4], posts[4:])
        if e + 2 < E:
            load_expert(e + 2)

    for lane in (act, pool, dve, pe):
        lane.wait(*pieces, *stores_done)
    run(split_weights(0))

    key, kept, key_flip = cb("key", [P, 1], U32), cb("kept", [P, 1], U32), cb("key_flip", [P, 1], U32)
    trial, trial_flips = cb("trial", [P, 3], U32), cb("trial_flips", [P, N_TRIALS], U32)
    count, n_enough = cb("count", [P, 3], F32), cb("n_enough", [P, 1], F32)
    enough = cb("enough", [P, 3], F32)
    above_trial = [cb(f"above_trial{i}", [P, M], BF16) for i in range(3)]
    count_bank = bank[0]

    def count_at_least(i):
        return dve.do(lambda e: e.tensor_scalar(above_trial[i][:], logits_by_chunk[:], trial[:, i:i + 1].bitcast(F32),
                                                None, ALU.is_ge, ALU.add, accum_out=count[:, i:i + 1]))

    def keep(n, unit, counted):
        pe.wait(counted)
        summed = mm(count_bank[:, 0:n], same_expert[:], count[:, 0:n], True, True, post=True)
        dve.wait(summed)
        dve.wait(dve.do(lambda e: e.tensor_scalar(enough[:, 0:n], count_bank[:, 0:n], float(CAP), None,
                                                  ALU.is_ge, ALU.add, accum_out=n_enough[:])))
        dve.wait(ts(dve, kept[:], n_enough[:], float(unit), None, ALU.mult))

    dve.wait(search_loaded)
    pe.wait(search_loaded)
    dve.wait(dve.do(lambda e: e.memset(trial[:], 0)))
    keep(1, 1 << 31, count_at_least(0))
    ts(dve, key[:], kept[:], 0, None, ALU.bitwise_or)
    dve.wait(ts(dve, key_flip[:].bitcast(I32), kept[:].bitcast(I32), 31, -1, ALU.arith_shift_right,
                ALU.bitwise_xor))
    dve.wait(ts(dve, key_flip[:], key_flip[:], 1 << 31, None, ALU.bitwise_or))
    dve.wait(ts(dve, trial_flips[:], search_bits[:], key_flip[:, 0:1], None, ALU.bitwise_xor))
    dve.wait(dve.do(lambda e: e.memset(kept[:], 0)))
    for first in range(0, N_TRIALS, 3):
        n = min(3, N_TRIALS - first)
        dve.wait(ts(dve, trial[:, 0:n], trial_flips[:, first:first + n], key[:, 0:1], kept[:, 0:1],
                    ALU.bitwise_xor, ALU.bitwise_xor))
        for i in range(n):
            counted = count_at_least(i)
        dve.wait(ts(dve, key[:], key[:], kept[:, 0:1], None, ALU.bitwise_or))
        keep(n, TRIAL_BITS[first], counted)
    dve.wait(ts(dve, trial[:, 0:1], key[:], kept[:, 0:1], key_flip[:, 0:1], ALU.bitwise_or, ALU.bitwise_xor))

    for lane in (dve, pe, act):
        lane.wait(consts_loaded)
    wide = cb("wide", [E, P], F32)
    limit = cb("limit", [P, E], F32)
    widened = copy(dve, wide[:], trial[0:E, 0:1].bitcast(F32).broadcast_to([E, P]))
    pe.wait(widened)
    limits_flipped = flip(bank[1][:, 0:E], wide[:], ident[0:E, 0:E], post=True)
    before_made = copy(dve, before[:], before_f[:])
    ones_made = dve.do(lambda e: e.memset(all_ones[:], 1.0))
    tile_ids_made = copy(dve, tile_ids[:], tile_ids_f[:])
    dve.wait(limits_flipped)
    dve.wait(copy(dve, limit[:], bank[1][:, 0:E]))

    by_expert = [P, E, NT]
    view = logits[:].rearrange("p j e -> p e j")
    above, equal = cb("above", by_expert, BF16), cb("equal", by_expert, BF16)
    running, earlier = cb("running", [P, E * NT], BF16), cb("earlier", [P, E * NT], BF16)
    flat = lambda t: t[:].rearrange("p e j -> p (e j)")
    order = {}
    for n, (taken, op) in enumerate(((above, ALU.is_gt), (equal, ALU.is_equal))):
        dve.wait(tt(dve, taken[:], view, limit[:].unsqueeze(2).broadcast_to(by_expert), op))
        if n:
            dve.wait(order[0])
            pe_read = order[0]
        dve.wait(dve.do(lambda e, t=taken: e.tensor_tensor_scan(running[:], scan_keep[:], flat(t), 0.0,
                                                               ALU.mult, ALU.add)))
        tiles_before = tt(dve, earlier[:], running[:], flat(taken), ALU.subtract)
        pe.wait(tiles_before, before_made, ones_made)
        mm(bank[2 + n][:], before[:], flat(taken), True, False)
        order[n] = mm(bank[2 + n][:], all_ones[:], earlier[:], False, True, post=True)
        if n == 0:
            totals = running[:].rearrange("p (e j) -> p e j", j=NT)[:, :, NT - 1]
            order[0] = mm(bank[4][:, 0:E], all_ones[:], totals, True, True, post=True)
    n_above, slot, part = cb("n_above", [P, E], F32), cb("slot", by_expert, F32), cb("part", by_expert, F32)
    slot_int, slot_bits = cb("slot_int", by_expert, I32), cb("slot_bits", by_expert, I32)
    rank = lambda n: bank[n][:].rearrange("p (e j) -> p e j", j=NT)
    dve.wait(order[0])
    dve.wait(copy(dve, n_above[:], bank[4][:, 0:E]), order[1])
    dve.wait(tt(dve, part[:], rank(3), n_above[:].unsqueeze(2).broadcast_to(by_expert), ALU.add))
    dve.wait(tt(dve, part[:], part[:], equal[:], ALU.mult))
    dve.wait(tt(dve, slot[:], rank(2), above[:], ALU.mult))
    dve.wait(tt(dve, slot[:], slot[:], part[:], ALU.add))
    dve.wait(tt(dve, part[:], above[:], equal[:], ALU.add))
    dve.wait(stt(slot[:], part[:], -float(NO_SLOT), slot[:], ALU.mult, ALU.add))
    dve.wait(ts(dve, slot_int[:], slot[:], float(NO_SLOT), None, ALU.add))
    dve.wait(ts(dve, slot_bits[:], slot_int[:], 4, None, ALU.logical_shift_right))
    dve.wait(copy(dve, slot_hi[:], slot_bits[:]))
    dve.wait(ts(dve, slot_bits[:], slot_int[:], 15, None, ALU.bitwise_and))
    slots_made = copy(dve, slot_lo[:], slot_bits[:])
    dve.wait(slots_made)

    list_bank, list_bank_free = bank[0], [()]
    xe_bank, xe_bank_free = bank[1], [()]
    hidden_banks = Ring(bank[2:5] + bank[7:8])
    y_banks, y_bank_free = bank[5:7], [(), ()]
    hot_free = [()]
    index_made, gather_done, xe_made = {}, {}, {}
    index_free, gathered_free, xe_free = [()] * LISTS, [()] * GATHERS, [(), ()]
    gather_sem = [semaphore(f"gathered{i}") for i in range(GATHERS)]
    scatter_sem = [semaphore(f"scattered{i}") for i in range(2)]
    rows_at = (rows_stored[0],)

    def list_tokens(e):
        hot = [P, NT, 16]
        iota = iota16[:].unsqueeze(1).broadcast_to(hot)
        dve.wait(*hot_free[0])
        tt(dve, hot_hi[:], iota, slot_hi[:, e, :].unsqueeze(2).broadcast_to(hot), ALU.is_equal)
        dve.wait(tt(dve, hot_lo[:], iota, slot_lo[:, e, :].unsqueeze(2).broadcast_to(hot), ALU.is_equal))
        ts(dve, hot_ids[:, :, 0, :], hot_lo[:], token_in_tile[:, 0:1], None, ALU.mult)
        ids_made = tt(dve, hot_ids[:, :, 1, :], hot_lo[:], tile_ids[:].unsqueeze(2).broadcast_to(hot), ALU.mult)
        yield from idle(3)
        pe.wait(ids_made, *list_bank_free[0])
        for j in range(NT):
            listed = mm(list_bank[0:16, 0:32], hot_hi[:, j, :], hot_ids[:, j].rearrange("p a b -> p (a b)"),
                        j == 0, j == NT - 1, post=j == NT - 1)
        hot_free[0] = (listed,)
        yield
        dve.wait(listed)
        dve.wait(copy(dve, list_parts[:], list_bank[0:16, 0:32]))
        made = stt(list16[:], list_parts[:, 16:32], float(P), list_parts[:, 0:16], ALU.mult, ALU.add)
        yield from idle(2)
        pe.wait(made)
        spread = mm(list_bank[:, 64:80], expand16[:], list16[:], True, True, post=True)
        dve.wait(spread)
        dve.wait(tt(dve, picked[:], pick[:], list_bank[:, 64:80].unsqueeze(1).broadcast_to([P, 2, 16]), ALU.mult))
        list_bank_free[0] = (dve.latest(),)
        dve.wait(reduce(list_f[:], picked[:], ALU.add))
        dve.wait(*index_free[e % LISTS])
        index_made[e] = copy(dve, token_index[e % LISTS][:], list_f[:])
        yield

    def gather(e):
        i = e % GATHERS
        pool.wait(index_made[e], *gathered_free[i], *rows_at)
        for c in range(2):
            gather_done[e] = pool.do(
                lambda g, c=c: g.indirect_dma_start(gathered[i][:, c, :], None, rows_dram,
                                                    bass.IndirectOffsetOnAxis(ap=token_index[e % LISTS][:, c:c + 1], axis=0)),
                gather_sem[i], 16)
        yield

    def transpose_tokens(e):
        i = e % 2
        pe.wait(gather_done[e], *xe_bank_free[0])
        for half in range(2):
            for c in range(2):
                flipped = flip(xe_bank[:, half * CAP + c * P:half * CAP + (c + 1) * P],
                               gathered[e % GATHERS][:, c, half * P:(half + 1) * P], ident[:], post=half and c)
        act.wait(flipped, *xe_free[i])
        flat_hi = xe_hi[i][:].rearrange("p a n -> p (a n)")
        hi = func(flat_hi, xe_bank[:], ACT.Copy)
        dve.wait(hi, *xe_free[i])
        lo = tt(dve, xe_lo[i][:].rearrange("p a n -> p (a n)"), xe_bank[:], as32(flat_hi), ALU.subtract)
        xe_bank_free[0] = (lo,)
        xe_made[e] = (hi, lo)
        yield

    h_free = [()] * FT
    h_ring = Ring(h_full)
    y_free = [(), ()]
    scattered = [()]

    def run_expert(e, between):
        i = e % 2
        pe.wait(*xe_made[e], *split_made[e][0])
        h_made, pending = [], []

        def split_rest():
            while pending:
                f, hat, full, hi = pending.pop()
                dve.wait(hi)
                h_made.append(tt(dve, h_lo[:, f, :], full[:], as32(h_hi[:, f, :]), ALU.subtract))
                h_ring.give(hat, h_made[f])

        for f in range(FT):
            at, out = hidden_banks.take(pe)
            cols = slice(f * P, (f + 1) * P)
            n = 0
            for half in range(2):
                for w, x in ((w1_hi, xe_hi), (w1_lo, xe_hi), (w1_hi, xe_lo)):
                    done = mm(out[:, 0:CAP], w[i][:, half, cols], x[i][:, half, :], n == 0, n == 5, post=n == 5)
                    n += 1
            hat, full = h_ring.take(act)
            act.wait(done)
            activated = func(full[:], out[:, 0:CAP], ACT.Gelu, bias=b1_cols[:, e, f:f + 1])
            hidden_banks.give(at, activated)
            dve.wait(activated, *h_free[f])
            hi = copy(dve, h_hi[:, f, :], full[:])
            split_rest()
            pending.append((f, hat, full, hi))
            between()
        split_rest()
        xe_free[i] = (done,)
        pe.wait(*split_made[e][1])
        for c in range(2):
            pe.wait(*y_bank_free[c])
            tokens = slice(c * P, (c + 1) * P)
            n = 0
            for f in range(FT):
                pe.wait(h_made[f])
                for h, w in ((h_hi, w2_hi), (h_lo, w2_hi), (h_hi, w2_lo)):
                    done = mm(y_banks[c][:, 0:D], h[:, f, tokens], w[i][:, f, :], n == 0, n == 3 * FT - 1,
                              post=n == 3 * FT - 1)
                    n += 1
                if c:
                    between()
            dve.wait(done, b2_here[e], *y_free[i])
            biased = tt(dve, y_out[i][:, c, 0:D], y_banks[c][:, 0:D], b2_rows[e % 4][:], ALU.add)
            y_bank_free[c] = (biased,)
            dve.wait(biased)
            gate = gathered[e % GATHERS][:, c, D + e:D + e + 1]
            ts(dve, y_out[i][:, c, 0:D], y_out[i][:, c, 0:D], gate, None, ALU.mult)
            gated = copy(dve, y_out[i][:, c, D:ACC], gate)
        for f in range(FT):
            h_free[f] = (done,)
        split_free[i] = (done,)
        b2_free[e % 4] = (biased,)
        gathered_free[e % GATHERS] = (gated,)

        def scatter():
            pool.wait(gated, acc_cleared, *scattered[0])
            for c in range(2):
                landed = pool.do(
                    lambda g, c=c: g.indirect_dma_start(acc_dram,
                                                        bass.IndirectOffsetOnAxis(ap=token_index[e % LISTS][:, c:c + 1], axis=0),
                                                        y_out[i][:, c, :], None, compute_op=ALU.add),
                    scatter_sem[i], 16)
            scattered[0] = (landed,)
            y_free[i] = index_free[e % LISTS] = (landed,)

        scatter_next[0] = scatter

    scatter_next = [lambda: None]

    for e in range(2):
        run(list_tokens(e), gather(e))
    run(transpose_tokens(0))
    choice.close()
    x2_back, x2_back_sem = sb("x2_back", [P, NT, D], F32), semaphore("x2_loaded")
    LIST_STEPS = 7
    POINTS = FT + FT
    for e in range(E):
        lists = paced(chain(*(list_tokens(n) for n in ((e + 3,) if e else (2, 3)) if n < E)),
                      LIST_STEPS * (1 if e else 2), POINTS)
        splits = paced(split_weights(e + 1) if e + 1 < E else idle(0), 4, POINTS - 1)
        state = {"point": 0}

        def between():
            state["point"] += 1
            if state["point"] == 4:
                scatter_next[0]()
            if state["point"] == (2 if e else POINTS // 2 + 2) and e + 2 < E:
                run(gather(e + 2))
            splits()
            lists()
            if state["point"] == POINTS - 4 and e + 1 < E:
                run(transpose_tokens(e + 1))

        run_expert(e, between)
        if e == 1:
            sync.wait(slots_made, pe.latest(), dve.latest())
            x2_loaded = load(x2_back[:], x2_dram.rearrange("(j p) d -> p j d", p=P), x2_back_sem)

    scatter_next[0]()

    GROUP = 4
    N_GROUPS = NT // GROUP
    spare = [t[:].rearrange("p a b -> p (a b)")[:, 0:GROUP * ACC].rearrange("p (j d) -> p j d", d=ACC)
             for t in (*w1_raw, *w2_raw)]
    acc_in = [sb(f"acc_in{i}", [P, GROUP, ACC], F32)[:] for i in range(2)] + spare
    inv_gate = [sb(f"inv_gate{i}", [P, 2, GROUP], F32) for i in range(len(acc_in))]
    acc_sem = [semaphore(f"acc_loaded{i}") for i in range(len(acc_in))]
    out_sem = semaphore("out_stored")
    acc_ring = Ring(acc_in)
    out_view = io["out"].rearrange("b (j p) d -> p (b j) d", p=P)
    acc_here, last_store = {}, None
    sync.wait(*scattered[0], *raw_free[0], *raw_free[1])

    def load_acc(g):
        at, buf = acc_ring.take(sync)
        acc_here[g] = (at, buf, load(buf, acc_view[:, GROUP * g:GROUP * (g + 1), :], acc_sem[at]))

    for g in range(len(acc_in)):
        load_acc(g)
    for lane in (dve, act, pool):
        lane.wait(x2_loaded)
    for g in range(N_GROUPS):
        at, acc, here = acc_here[g]
        tiles = slice(GROUP * g, GROUP * (g + 1))
        safe, inverse_sum = inv_gate[at][:, 0, :], inv_gate[at][:, 1, :]
        sums = acc[:, :, D]
        dve.wait(here)
        dve.wait(ts(dve, safe, sums, 0.0, None, ALU.is_le))
        dve.wait(tt(dve, safe, safe, sums, ALU.add))
        inverse_made = recip(inverse_sum, safe)
        if g % 3 == 0:
            act.wait(inverse_made, here)
            for j in range(GROUP):
                scaled = func(acc[:, j, 0:D], acc[:, j, 0:D], ACT.Copy, scale=inverse_sum[:, j:j + 1])
            pool.wait(scaled)
            last = tt(pool, x2_back[:, tiles, :], x2_back[:, tiles, :], acc[:, :, 0:D], ALU.add)
        else:
            dve.wait(inverse_made)
            for j in range(GROUP):
                last = stt(x2_back[:, GROUP * g + j, :], acc[:, j, 0:D], inverse_sum[:, j:j + 1],
                           x2_back[:, GROUP * g + j, :], ALU.mult, ALU.add)
        acc_ring.give(at, last)
        if g + len(acc_in) < N_GROUPS:
            load_acc(g + len(acc_in))
        sync.wait(last)
        last_store = load(out_view[:, tiles, :], x2_back[:, tiles, :], out_sem)
    sync.wait(last_store)

    with nc.Block() as block:
        block.sync(lambda e: sync.write(e))
        block.gpsimd(lambda e: pool.write(e))
        block.scalar(lambda e: act.write(e))
        block.vector(lambda e: dve.write(e))
        block.tensor(lambda e: pe.write(e))


def _operands(i):
    def cols(v, width):
        return np.ascontiguousarray(v.reshape(2, width).T)

    f32 = np.float32
    part, eye = np.arange(P), np.eye(P, dtype=f32)
    ops = {
        "x": i["x"], "ctx": i["ctx_768"], "mask": i["mask_BxS2_bk0"],
        "lnl_g": cols(i["L0_xattn_ln_l_g"], DHF), "lnl_b": cols(i["L0_xattn_ln_l_b"], DHF),
        "lnx_g": cols(i["L0_xattn_ln_x_g"], CHF), "lnx_b": cols(i["L0_xattn_ln_x_b"], CHF),
        "qn_g": i["L0_xattn_qn_g"][:, None], "kn_g": i["L0_xattn_kn_g"][:, None],
        "w_lat": np.concatenate([i["L0_xattn_Wq"].T, i["L0_xattn_Wlkv"].T], axis=1),
        "w_ctx": i["L0_xattn_Wkv"].T, "wo": i["L0_xattn_Wo"].T, "bo": i["L0_xattn_bo"],
        "norm_weight": i["L0_ffn_norm_weight"],
        "router_w": i["L0_ffn_router_weight"].T.reshape(2, P, E).transpose(1, 0, 2),
        "router_b": i["L0_ffn_router_bias"][:, None],
        "fc1": i["L0_ffn_fc1_weight"].transpose(0, 2, 1).reshape(E, 2, P, F).transpose(0, 2, 1, 3),
        "fc1_bias": i["L0_ffn_fc1_bias"].reshape(E, FT, P).transpose(2, 0, 1),
        "fc2": i["L0_ffn_fc2_weight"].transpose(0, 2, 1).reshape(E, FT, P, D).transpose(0, 2, 1, 3),
        "fc2_bias": i["L0_ffn_fc2_bias"],
        "ident": eye, "neg_ident": -eye,
        "same_expert": (part[:, None] % E == part[None, :] % E).astype(f32),
        "search_bits": np.broadcast_to(np.array(TRIAL_BITS, np.uint32), (P, N_TRIALS)),
        "before": (part[:, None] < part[None, :]).astype(f32),
        "scan_keep": np.broadcast_to((np.arange(E * NT) % NT != 0).astype(f32), (P, E * NT)),
        "iota16": np.broadcast_to(np.arange(16, dtype=f32), (P, 16)),
        "tile_ids": np.broadcast_to(np.arange(NT, dtype=f32), (P, NT)),
        "token_in_tile": part[:, None].astype(f32),
        "expand16": (np.arange(16)[:, None] == part[None, :] // 8).astype(f32),
        "pick": (np.arange(16)[None, None, :]
                 == 2 * (part % 8)[:, None, None] + np.arange(2)[None, :, None]).astype(f32),
    }
    return {name: np.ascontiguousarray(a) for name, a in ops.items()}


def kernel(**inputs):
    import concourse.bacc as bacc
    from concourse.bass_utils import run_bass_kernel_spmd

    nc = bacc.Bacc("TRN2", target_bir_lowering=False, num_devices=1)
    operands = _operands({name: np.asarray(a) for name, a in inputs.items()})
    io = {name: nc.dram_tensor(f"in_{name}", a.shape, mybir.dt.from_np(a.dtype), kind="ExternalInput").ap()
          for name, a in operands.items()}
    io["out"] = nc.dram_tensor("out_x", (B, M, D), F32, kind="ExternalOutput").ap()
    build(nc, io)
    result = run_bass_kernel_spmd(nc, [{f"in_{name}": a for name, a in operands.items()}], core_ids=[0])
    return result.results[0]["out_x"]
```
